# Optimizing a Trainium2 kernel written in Bass

```python
import numpy as np
import jax
import jax.numpy as jnp

def _softmax(x, axis=-1):
    return jax.nn.softmax(x, axis=axis)

def _gelu(x):
    return jax.nn.gelu(x, approximate=True)

def _silu(x):
    return jax.nn.silu(x)

def _sigmoid(x):
    return jax.nn.sigmoid(x)

def _layernorm(x, axis=-1, eps=1e-05):
    m = jnp.mean(x, axis=axis, keepdims=True)
    v = jnp.var(x, axis=axis, keepdims=True)
    return (x - m) / jnp.sqrt(v + eps)

def _scatter_add(tgt, idx, src, axis=0):
    return tgt.at[idx].add(src)

def _segment_sum(src, seg, n):
    return jax.ops.segment_sum(src, seg, n)
kernel_name = 'mk_perceiver_d4_seqx_r4_8f645d'

def setup_inputs(seed: int=0):
    np.random.seed(seed)
    _w = jnp.asarray

    def _rec_inputs():
        import jax
        import jax.numpy as jnp
        _rk = jax.random.key(seed)
        x = 7.22e-05 + 1 * jax.random.normal(jax.random.fold_in(_rk, 1), (16, 64, 256), jnp.float32)
        _lenS = 64 - jax.random.randint(jax.random.fold_in(_rk, 7), (16,), 0, max(1, 64 // 4) + 1, jnp.int32)
        _lenS2 = 1601 - jax.random.randint(jax.random.fold_in(_rk, 8), (16,), 0, max(1, 1601 // 4) + 1, jnp.int32)
        _ctx_1024P = jax.random.normal(jax.random.fold_in(_rk, 11), (16, 16, 256), jnp.float32)
        _ctx_1024c = jax.random.dirichlet(jax.random.fold_in(_rk, 511), 0.3 * jnp.ones((16,), jnp.float32), (16, 1601))
        _ctx_1024t = jnp.einsum('bsk,bkd->bsd', _ctx_1024c, _ctx_1024P)
        _ctx_1024t = _ctx_1024t * jax.lax.rsqrt(jnp.mean(jnp.square(_ctx_1024t)) + 1e-12) * 0.953939
        ctx_1024 = -1.39393e-06 + 0.999914 * (_ctx_1024t + 0.3 * jax.random.normal(jax.random.fold_in(_rk, 611), (16, 1601, 256), jnp.float32))
        _validS = jnp.arange(64)[None, :] < _lenS[:, None]
        _validS2 = jnp.arange(1601)[None, :] < _lenS2[:, None]
        _causal = jnp.tril(jnp.ones((64, 64), dtype=bool))
        mask_Bx1xS2_ik0 = jnp.where(jnp.broadcast_to(_validS2[:, None, :], (16, 1, 1601)), 0, 1).astype(jnp.int32)
        mask_Bx1x1xS2_ik0 = jnp.where(jnp.broadcast_to(_validS2[:, None, None, :], (16, 1, 1, 1601)), 0, 1).astype(jnp.int32)
        return (x, ctx_1024, mask_Bx1xS2_ik0, mask_Bx1x1xS2_ik0)
    x, ctx_1024, mask_Bx1xS2_ik0, mask_Bx1x1xS2_ik0 = _rec_inputs()

    def _L0_xattn_setup():
        import jax, jax.numpy as jnp
        import numpy as np
        DIM = 256
        CTX_DIM = 256
        HEADS = 16
        DIM_HEAD = 64
        INNER = HEADS * DIM_HEAD
        FF_INNER = 4 * DIM
        EPS = 1e-05

        def layer_norm(x, g, b):
            mu = jnp.mean(x, axis=-1, keepdims=True)
            var = jnp.var(x, axis=-1, keepdims=True)
            return (x - mu) * jax.lax.rsqrt(var + EPS) * g + b
        key = jax.random.key(seed)
        ks = jax.random.split(key, 9)
        b, n, j = (4, 512, 256)
        inp = {'x': jax.random.normal(ks[0], (b, n, DIM), dtype=jnp.float32), 'context': jax.random.normal(ks[1], (b, j, CTX_DIM), dtype=jnp.float32), 'ln_g': jnp.ones((DIM,), jnp.float32), 'ln_b': jnp.zeros((DIM,), jnp.float32), 'cln_g': jnp.ones((CTX_DIM,), jnp.float32), 'cln_b': jnp.zeros((CTX_DIM,), jnp.float32), 'Wq': jax.random.normal(ks[2], (DIM, INNER), dtype=jnp.float32) * DIM ** (-0.5), 'Wkv': jax.random.normal(ks[3], (CTX_DIM, 2 * DIM_HEAD), dtype=jnp.float32) * CTX_DIM ** (-0.5), 'Wo': jax.random.normal(ks[4], (INNER, DIM), dtype=jnp.float32) * INNER ** (-0.5), 'Wff1': jax.random.normal(ks[5], (DIM, 2 * FF_INNER), dtype=jnp.float32) * DIM ** (-0.5), 'Wff2': jax.random.normal(ks[6], (FF_INNER, DIM), dtype=jnp.float32) * FF_INNER ** (-0.5)}
        return inp
    _L0_xattn_all = _L0_xattn_setup()
    _L0_xattn_in = {k: v for k, v in _L0_xattn_all.items() if k in ('ln_g', 'ln_b', 'cln_g', 'cln_b', 'Wq', 'Wkv', 'Wo', 'Wff1', 'Wff2')}
    del _L0_xattn_all

    def _L0_attn_setup():
        import jax, jax.numpy as jnp
        import numpy as np
        B, S, E, H = (2, 512, 256, 16)
        D = E // H
        key = jax.random.key(seed)
        k1, k2, k3 = jax.random.split(key, 3)
        x = jax.random.normal(k1, (B, S, E), dtype=jnp.float32)
        lim_qkv = np.sqrt(6.0 / (E + 3 * E)).astype(np.float32)
        lim_out = np.sqrt(6.0 / (E + E)).astype(np.float32)
        w_qkv = jax.random.uniform(k2, (E, 3 * E), jnp.float32, -lim_qkv, lim_qkv)
        w_out = jax.random.uniform(k3, (E, E), jnp.float32, -lim_out, lim_out)
        return {'x': x, 'w_qkv': w_qkv, 'w_out': w_out}
    _L0_attn_all = _L0_attn_setup()
    _L0_attn_in = {k: v for k, v in _L0_attn_all.items() if k in ('w_qkv', 'w_out')}
    del _L0_attn_all

    def _L0_ffn_setup():
        import jax, jax.numpy as jnp
        import numpy as np
        FP8_E4M3_MAX = 448.0

        def fake_quant_fp8(t):
            amax = jnp.max(jnp.abs(t))
            scale = FP8_E4M3_MAX / jnp.maximum(amax, 1e-12)
            q = (t * scale).astype(jnp.float8_e4m3fn).astype(jnp.float32)
            return q / scale
        key = jax.random.key(seed)
        k1, k2, k3 = jax.random.split(key, 3)
        d_in, d_out = (256, 256)
        x = jax.random.normal(k1, (4, 2048, d_in), dtype=jnp.float32)
        weight = jax.random.normal(k2, (d_out, d_in), dtype=jnp.float32) * (1.0 / np.sqrt(d_in))
        bias = jax.random.normal(k3, (d_out,), dtype=jnp.float32) * 0.01
        return {'x': x, 'weight': weight, 'bias': bias}
    _L0_ffn_all = _L0_ffn_setup()
    _L0_ffn_in = {k: v for k, v in _L0_ffn_all.items() if k in ('weight', 'bias')}
    del _L0_ffn_all

    def _L1_xattn_setup():
        import jax, jax.numpy as jnp
        import numpy as np
        H = 16
        D_MODEL = 256
        D_K = D_MODEL // H
        NEG_INF = -1000000000.0

        def _split_heads(x):
            B, S, _ = x.shape
            return x.reshape(B, S, H, D_K).transpose(0, 2, 1, 3)
        key = jax.random.key(seed)
        ks = jax.random.split(key, 13)
        B, S = (4, 512)
        scale = 1.0 / np.sqrt(D_MODEL)
        inp = {'query': jax.random.normal(ks[0], (B, S, D_MODEL), jnp.float32), 'key': jax.random.normal(ks[1], (B, S, D_MODEL), jnp.float32), 'value': jax.random.normal(ks[2], (B, S, D_MODEL), jnp.float32), 'mask': jax.random.randint(ks[3], (B, 1, S), 0, 2, jnp.int32), 'Wq': jax.random.normal(ks[4], (D_MODEL, D_MODEL), jnp.float32) * scale, 'bq': jnp.zeros((D_MODEL,), jnp.float32), 'Wk': jax.random.normal(ks[5], (D_MODEL, D_MODEL), jnp.float32) * scale, 'bk': jnp.zeros((D_MODEL,), jnp.float32), 'Wv': jax.random.normal(ks[6], (D_MODEL, D_MODEL), jnp.float32) * scale, 'bv': jnp.zeros((D_MODEL,), jnp.float32), 'Wo': jax.random.normal(ks[7], (D_MODEL, D_MODEL), jnp.float32) * scale, 'bo': jnp.zeros((D_MODEL,), jnp.float32)}
        return inp
    _L1_xattn_all = _L1_xattn_setup()
    _L1_xattn_in = {k: v for k, v in _L1_xattn_all.items() if k in ('Wq', 'bq', 'Wk', 'bk', 'Wv', 'bv', 'Wo', 'bo')}
    del _L1_xattn_all

    def _L1_attn_setup():
        import jax, jax.numpy as jnp
        import numpy as np
        B, T, E, H = (2, 512, 256, 16)
        D = E // H
        key = jax.random.key(seed)
        k = jax.random.split(key, 6)
        return {'x': jax.random.normal(k[0], (B, T, E), dtype=jnp.float32), 'w_att_val': jax.random.normal(k[1], (H, D, D), dtype=jnp.float32) * (6.0 / D) ** 0.5, 'wv_w': jax.random.normal(k[2], (E, E), dtype=jnp.float32) * E ** (-0.5), 'wv_b': jnp.zeros((E,), dtype=jnp.float32), 'out_w': jax.random.normal(k[3], (E, E), dtype=jnp.float32) * E ** (-0.5), 'out_b': jnp.zeros((E,), dtype=jnp.float32)}
    _L1_attn_all = _L1_attn_setup()
    _L1_attn_in = {k: v for k, v in _L1_attn_all.items() if k in ('w_att_val', 'wv_w', 'wv_b', 'out_w', 'out_b')}
    del _L1_attn_all

    def _L1_ffn_setup():
        import jax, jax.numpy as jnp
        import numpy as np
        H, F, E_SHARED, E_ROUTED, K = (256, 1024, 1, 8, 2)

        def _expert(x, w_up, w_down):
            h = jax.nn.gelu(jnp.einsum('bsh,hf->bsf', x, w_up), approximate=False)
            return jnp.einsum('bsf,fh->bsh', h, w_down)
        key = jax.random.key(seed)
        ks = jax.random.split(key, 6)
        x = jax.random.normal(ks[0], (4, 512, H), dtype=jnp.float32)
        s = 0.02
        shared_up = jax.random.normal(ks[1], (E_SHARED, H, F), dtype=jnp.float32) * s
        shared_down = jax.random.normal(ks[2], (E_SHARED, F, H), dtype=jnp.float32) * s
        routed_up = jax.random.normal(ks[3], (E_ROUTED, H, F), dtype=jnp.float32) * s
        routed_down = jax.random.normal(ks[4], (E_ROUTED, F, H), dtype=jnp.float32) * s
        router_w = jax.random.normal(ks[5], (H, E_ROUTED), dtype=jnp.float32) * s
        return {'x': x, 'shared_up': shared_up, 'shared_down': shared_down, 'routed_up': routed_up, 'routed_down': routed_down, 'router_w': router_w}
    _L1_ffn_all = _L1_ffn_setup()
    _L1_ffn_in = {k: v for k, v in _L1_ffn_all.items() if k in ('shared_up', 'shared_down', 'routed_up', 'routed_down', 'router_w')}
    del _L1_ffn_all

    def _L2_xattn_setup():
        import jax, jax.numpy as jnp
        import numpy as np
        DIM = 256
        HEADS = 16
        HEAD_DIM = DIM // HEADS
        B, N, M = (2, 512, 512)

        def _split_heads(x):
            b, s, c = x.shape
            return x.reshape(b, s, HEADS, HEAD_DIM).transpose(0, 2, 1, 3)
        key0 = jax.random.key(seed)
        ks = jax.random.split(key0, 12)
        s = 0.02
        return {'query': jax.random.normal(ks[0], (B, N, DIM), jnp.float32), 'key': jax.random.normal(ks[1], (B, M, DIM), jnp.float32), 'value': jax.random.normal(ks[2], (B, M, DIM), jnp.float32), 'Wq': jax.random.normal(ks[3], (DIM, DIM), jnp.float32) * s, 'bq': jnp.zeros((DIM,), jnp.float32), 'Wk': jax.random.normal(ks[4], (DIM, DIM), jnp.float32) * s, 'bk': jnp.zeros((DIM,), jnp.float32), 'Wv': jax.random.normal(ks[5], (DIM, DIM), jnp.float32) * s, 'bv': jnp.zeros((DIM,), jnp.float32), 'Wp': jax.random.normal(ks[6], (DIM, DIM), jnp.float32) * s, 'bp': jnp.zeros((DIM,), jnp.float32), 'scale': jnp.full((1,), HEAD_DIM ** (-0.5), jnp.float32)}
    _L2_xattn_all = _L2_xattn_setup()
    _L2_xattn_in = {k: v for k, v in _L2_xattn_all.items() if k in ('Wq', 'bq', 'Wk', 'bk', 'Wv', 'bv', 'Wp', 'bp', 'scale')}
    del _L2_xattn_all

    def _L2_attn_setup():
        import jax, jax.numpy as jnp
        import numpy as np
        D_MODEL = 256

        def dw_causal_conv(x, w, b):
            K = w.shape[1]
            out = jax.lax.conv_general_dilated(x, w[:, None, :], window_strides=(1,), padding=[(K - 1, 0)], feature_group_count=x.shape[1], dimension_numbers=('NCH', 'OIH', 'NCH'))
            return out + b[None, :, None]
        key = jax.random.key(seed)
        ks = jax.random.split(key, 9)
        B, L, D = (2, 2048, D_MODEL)
        s = 0.02
        return {'u': jax.random.normal(ks[0], (B, L, D), jnp.float32), 'W_in': jax.random.normal(ks[1], (D, 3 * D), jnp.float32) * s, 'b_in': jax.random.normal(ks[2], (3 * D,), jnp.float32) * s, 'short_w': jax.random.normal(ks[3], (3 * D, 3), jnp.float32) * s, 'short_b': jax.random.normal(ks[4], (3 * D,), jnp.float32) * s, 'inner_w': jax.random.normal(ks[5], (D, 4), jnp.float32) * s, 'inner_b': jax.random.normal(ks[6], (D,), jnp.float32) * s, 'W_out': jax.random.normal(ks[7], (D, D), jnp.float32) * s, 'b_out': jax.random.normal(ks[8], (D,), jnp.float32) * s}
    _L2_attn_all = _L2_attn_setup()
    _L2_attn_in = {k: v for k, v in _L2_attn_all.items() if k in ('W_in', 'b_in', 'short_w', 'short_b', 'inner_w', 'inner_b', 'W_out', 'b_out')}
    del _L2_attn_all

    def _L2_ffn_setup():
        import jax, jax.numpy as jnp
        import numpy as np
        EPS = 1e-06
        TOP_K = 2

        def rms_norm(x, scale, eps=EPS):
            xf = x.astype(jnp.float32)
            mean_sq = jnp.mean(xf * xf, axis=-1, keepdims=True)
            return (xf * (scale.astype(jnp.float32) * jax.lax.rsqrt(mean_sq + eps))).astype(x.dtype)
        key = jax.random.key(seed)
        k0, k1, k2, k3 = jax.random.split(key, 4)
        B, S, D, H, E = (2, 512, 256, 704, 8)
        x = jax.random.normal(k0, (B, S, D), dtype=jnp.float32)
        norm_scale = jnp.ones((D,), dtype=jnp.float32)
        w_router = jax.random.normal(k1, (E, D), dtype=jnp.float32) * 0.02
        w_up = jax.random.normal(k2, (E, 2 * H, D), dtype=jnp.float32) * 0.02
        w_down = jax.random.normal(k3, (E, D, H), dtype=jnp.float32) * 0.02
        return {'x': x, 'norm_scale': norm_scale, 'w_router': w_router, 'w_up': w_up, 'w_down': w_down}
    _L2_ffn_all = _L2_ffn_setup()
    _L2_ffn_in = {k: v for k, v in _L2_ffn_all.items() if k in ('norm_scale', 'w_router', 'w_up', 'w_down')}
    del _L2_ffn_all

    def _L3_xattn_setup():
        import jax, jax.numpy as jnp
        import numpy as np
        D_MODEL = 256
        NUM_HEADS = 16
        D_K = D_MODEL // NUM_HEADS
        B, S = (2, 512)
        NEG = -1000000000.0

        def _split_heads(x):
            b, s, _ = x.shape
            return x.reshape(b, s, NUM_HEADS, D_K).transpose(0, 2, 1, 3)
        key = jax.random.key(seed)
        ks = jax.random.split(key, 13)
        std = 0.02
        inp = {'q': jax.random.normal(ks[0], (B, S, D_MODEL), dtype=jnp.float32), 'k': jax.random.normal(ks[1], (B, S, D_MODEL), dtype=jnp.float32), 'v': jax.random.normal(ks[2], (B, S, D_MODEL), dtype=jnp.float32), 'mask': jax.random.randint(ks[3], (B, 1, 1, S), 0, 2, dtype=jnp.int32), 'Wq': jax.random.normal(ks[4], (D_MODEL, D_MODEL), dtype=jnp.float32) * std, 'bq': jnp.zeros((D_MODEL,), dtype=jnp.float32), 'Wk': jax.random.normal(ks[5], (D_MODEL, D_MODEL), dtype=jnp.float32) * std, 'bk': jnp.zeros((D_MODEL,), dtype=jnp.float32), 'Wv': jax.random.normal(ks[6], (D_MODEL, D_MODEL), dtype=jnp.float32) * std, 'bv': jnp.zeros((D_MODEL,), dtype=jnp.float32), 'Wo': jax.random.normal(ks[7], (D_MODEL, D_MODEL), dtype=jnp.float32) * std, 'bo': jnp.zeros((D_MODEL,), dtype=jnp.float32)}
        return inp
    _L3_xattn_all = _L3_xattn_setup()
    _L3_xattn_in = {k: v for k, v in _L3_xattn_all.items() if k in ('Wq', 'bq', 'Wk', 'bk', 'Wv', 'bv', 'Wo', 'bo')}
    del _L3_xattn_all

    def _L3_attn_setup():
        import jax, jax.numpy as jnp
        import numpy as np
        D_MODEL = 256
        NUM_HEADS = 16
        HEAD_DIM = D_MODEL // NUM_HEADS
        THETA = 10000.0
        B, T = (4, 512)

        def _cos_sin(seq_len, head_dim, theta):
            freqs = 1.0 / theta ** (jnp.arange(0, head_dim, 2, dtype=jnp.float32) / head_dim)
            t = jnp.arange(seq_len, dtype=jnp.float32)
            angles = jnp.outer(t, freqs)
            return jnp.concatenate([jnp.cos(angles), jnp.sin(angles)], axis=-1)

        def _apply_rope(x, cos_sin):
            x1 = x[..., 0::2]
            x2 = x[..., 1::2]
            half = x.shape[-1] // 2
            cos = cos_sin[:, :half]
            sin = cos_sin[:, half:]
            out = jnp.stack([x1 * cos - x2 * sin, x1 * sin + x2 * cos], axis=-1)
            return out.reshape(x.shape)
        key = jax.random.key(seed)
        k1, k2, k3 = jax.random.split(key, 3)
        x = jax.random.normal(k1, (B, T, D_MODEL), dtype=jnp.float32)
        W_qkv = jax.random.normal(k2, (3 * D_MODEL, D_MODEL), dtype=jnp.float32) * D_MODEL ** (-0.5)
        W_out = jax.random.normal(k3, (D_MODEL, D_MODEL), dtype=jnp.float32) * D_MODEL ** (-0.5)
        return {'x': x, 'W_qkv': W_qkv, 'W_out': W_out}
    _L3_attn_all = _L3_attn_setup()
    _L3_attn_in = {k: v for k, v in _L3_attn_all.items() if k in ('W_qkv', 'W_out')}
    del _L3_attn_all

    def _L3_ffn_setup():
        import jax, jax.numpy as jnp
        import numpy as np
        D_MODEL = 256
        D_HIDDEN = 1024
        NUM_EXPERTS = 8
        B, T = (2, 512)
        key = jax.random.key(seed)
        ks = jax.random.split(key, 8)
        s = 0.02
        x = jax.random.normal(ks[0], (B, T, D_MODEL), dtype=jnp.float32)
        Wg = jax.random.normal(ks[1], (D_MODEL, NUM_EXPERTS), dtype=jnp.float32) * s
        bg = jnp.zeros((NUM_EXPERTS,), dtype=jnp.float32)
        W1 = jax.random.normal(ks[2], (NUM_EXPERTS, D_MODEL, D_HIDDEN), dtype=jnp.float32) * s
        b1 = jnp.zeros((NUM_EXPERTS, D_HIDDEN), dtype=jnp.float32)
        W2 = jax.random.normal(ks[3], (NUM_EXPERTS, D_HIDDEN, D_MODEL), dtype=jnp.float32) * s
        b2 = jnp.zeros((NUM_EXPERTS, D_MODEL), dtype=jnp.float32)
        return {'x': x, 'Wg': Wg, 'bg': bg, 'W1': W1, 'b1': b1, 'W2': W2, 'b2': b2}
    _L3_ffn_all = _L3_ffn_setup()
    _L3_ffn_in = {k: v for k, v in _L3_ffn_all.items() if k in ('Wg', 'bg', 'W1', 'b1', 'W2', 'b2')}
    del _L3_ffn_all
    return {'x': x, 'ctx_1024': ctx_1024, 'mask_Bx1xS2_ik0': mask_Bx1xS2_ik0, 'mask_Bx1x1xS2_ik0': mask_Bx1x1xS2_ik0, 'L0_xattn_ln_g': _L0_xattn_in['ln_g'], 'L0_xattn_ln_b': _L0_xattn_in['ln_b'], 'L0_xattn_cln_g': _L0_xattn_in['cln_g'], 'L0_xattn_cln_b': _L0_xattn_in['cln_b'], 'L0_xattn_Wq': _L0_xattn_in['Wq'], 'L0_xattn_Wkv': _L0_xattn_in['Wkv'], 'L0_xattn_Wo': _L0_xattn_in['Wo'], 'L0_xattn_Wff1': _L0_xattn_in['Wff1'], 'L0_xattn_Wff2': _L0_xattn_in['Wff2'], 'L0_attn_w_qkv': _L0_attn_in['w_qkv'], 'L0_attn_w_out': _L0_attn_in['w_out'], 'L0_ffn_weight': _L0_ffn_in['weight'], 'L0_ffn_bias': _L0_ffn_in['bias'], 'L1_xattn_Wq': _L1_xattn_in['Wq'], 'L1_xattn_bq': _L1_xattn_in['bq'], 'L1_xattn_Wk': _L1_xattn_in['Wk'], 'L1_xattn_bk': _L1_xattn_in['bk'], 'L1_xattn_Wv': _L1_xattn_in['Wv'], 'L1_xattn_bv': _L1_xattn_in['bv'], 'L1_xattn_Wo': _L1_xattn_in['Wo'], 'L1_xattn_bo': _L1_xattn_in['bo'], 'L1_attn_w_att_val': _L1_attn_in['w_att_val'], 'L1_attn_wv_w': _L1_attn_in['wv_w'], 'L1_attn_wv_b': _L1_attn_in['wv_b'], 'L1_attn_out_w': _L1_attn_in['out_w'], 'L1_attn_out_b': _L1_attn_in['out_b'], 'L1_ffn_shared_up': _L1_ffn_in['shared_up'], 'L1_ffn_shared_down': _L1_ffn_in['shared_down'], 'L1_ffn_routed_up': _L1_ffn_in['routed_up'], 'L1_ffn_routed_down': _L1_ffn_in['routed_down'], 'L1_ffn_router_w': _L1_ffn_in['router_w'], 'L2_xattn_Wq': _L2_xattn_in['Wq'], 'L2_xattn_bq': _L2_xattn_in['bq'], 'L2_xattn_Wk': _L2_xattn_in['Wk'], 'L2_xattn_bk': _L2_xattn_in['bk'], 'L2_xattn_Wv': _L2_xattn_in['Wv'], 'L2_xattn_bv': _L2_xattn_in['bv'], 'L2_xattn_Wp': _L2_xattn_in['Wp'], 'L2_xattn_bp': _L2_xattn_in['bp'], 'L2_xattn_scale': _L2_xattn_in['scale'], 'L2_attn_W_in': _L2_attn_in['W_in'], 'L2_attn_b_in': _L2_attn_in['b_in'], 'L2_attn_short_w': _L2_attn_in['short_w'], 'L2_attn_short_b': _L2_attn_in['short_b'], 'L2_attn_inner_w': _L2_attn_in['inner_w'], 'L2_attn_inner_b': _L2_attn_in['inner_b'], 'L2_attn_W_out': _L2_attn_in['W_out'], 'L2_attn_b_out': _L2_attn_in['b_out'], 'L2_ffn_norm_scale': _L2_ffn_in['norm_scale'], 'L2_ffn_w_router': _L2_ffn_in['w_router'], 'L2_ffn_w_up': _L2_ffn_in['w_up'], 'L2_ffn_w_down': _L2_ffn_in['w_down'], 'L3_xattn_Wq': _L3_xattn_in['Wq'], 'L3_xattn_bq': _L3_xattn_in['bq'], 'L3_xattn_Wk': _L3_xattn_in['Wk'], 'L3_xattn_bk': _L3_xattn_in['bk'], 'L3_xattn_Wv': _L3_xattn_in['Wv'], 'L3_xattn_bv': _L3_xattn_in['bv'], 'L3_xattn_Wo': _L3_xattn_in['Wo'], 'L3_xattn_bo': _L3_xattn_in['bo'], 'L3_attn_W_qkv': _L3_attn_in['W_qkv'], 'L3_attn_W_out': _L3_attn_in['W_out'], 'L3_ffn_Wg': _L3_ffn_in['Wg'], 'L3_ffn_bg': _L3_ffn_in['bg'], 'L3_ffn_W1': _L3_ffn_in['W1'], 'L3_ffn_b1': _L3_ffn_in['b1'], 'L3_ffn_W2': _L3_ffn_in['W2'], 'L3_ffn_b2': _L3_ffn_in['b2']}

def reference(x, ctx_1024, mask_Bx1xS2_ik0, mask_Bx1x1xS2_ik0, L0_xattn_ln_g, L0_xattn_ln_b, L0_xattn_cln_g, L0_xattn_cln_b, L0_xattn_Wq, L0_xattn_Wkv, L0_xattn_Wo, L0_xattn_Wff1, L0_xattn_Wff2, L0_attn_w_qkv, L0_attn_w_out, L0_ffn_weight, L0_ffn_bias, L1_xattn_Wq, L1_xattn_bq, L1_xattn_Wk, L1_xattn_bk, L1_xattn_Wv, L1_xattn_bv, L1_xattn_Wo, L1_xattn_bo, L1_attn_w_att_val, L1_attn_wv_w, L1_attn_wv_b, L1_attn_out_w, L1_attn_out_b, L1_ffn_shared_up, L1_ffn_shared_down, L1_ffn_routed_up, L1_ffn_routed_down, L1_ffn_router_w, L2_xattn_Wq, L2_xattn_bq, L2_xattn_Wk, L2_xattn_bk, L2_xattn_Wv, L2_xattn_bv, L2_xattn_Wp, L2_xattn_bp, L2_xattn_scale, L2_attn_W_in, L2_attn_b_in, L2_attn_short_w, L2_attn_short_b, L2_attn_inner_w, L2_attn_inner_b, L2_attn_W_out, L2_attn_b_out, L2_ffn_norm_scale, L2_ffn_w_router, L2_ffn_w_up, L2_ffn_w_down, L3_xattn_Wq, L3_xattn_bq, L3_xattn_Wk, L3_xattn_bk, L3_xattn_Wv, L3_xattn_bv, L3_xattn_Wo, L3_xattn_bo, L3_attn_W_qkv, L3_attn_W_out, L3_ffn_Wg, L3_ffn_bg, L3_ffn_W1, L3_ffn_b1, L3_ffn_W2, L3_ffn_b2):
    import jax
    import jax.numpy as jnp

    def _L0_xattn_ref(x, context, ln_g, ln_b, cln_g, cln_b, Wq, Wkv, Wo, Wff1, Wff2):
        import jax, jax.numpy as jnp
        import numpy as np
        DIM = 256
        CTX_DIM = 256
        HEADS = 16
        DIM_HEAD = 64
        INNER = HEADS * DIM_HEAD
        FF_INNER = 4 * DIM
        EPS = 1e-05

        def layer_norm(x, g, b):
            mu = jnp.mean(x, axis=-1, keepdims=True)
            var = jnp.var(x, axis=-1, keepdims=True)
            return (x - mu) * jax.lax.rsqrt(var + EPS) * g + b
        scale = DIM_HEAD ** (-0.5)
        xn = layer_norm(x, ln_g, ln_b)
        cn = layer_norm(context, cln_g, cln_b)
        b, n, _ = xn.shape
        q = (xn @ Wq).reshape(b, n, HEADS, DIM_HEAD).transpose(0, 2, 1, 3) * scale
        kv = cn @ Wkv
        k, v = (kv[..., :DIM_HEAD], kv[..., DIM_HEAD:])
        sim = jnp.einsum('bhid,bjd->bhij', q, k)
        attn = jax.nn.softmax(sim, axis=-1)
        out = jnp.einsum('bhij,bjd->bhid', attn, v)
        out = out.transpose(0, 2, 1, 3).reshape(b, n, INNER) @ Wo
        ff = xn @ Wff1
        h, gate = (ff[..., :FF_INNER], ff[..., FF_INNER:])
        out = out + jax.nn.silu(gate) * h @ Wff2
        return out

    def _L0_attn_ref(x, w_qkv, w_out):
        import jax, jax.numpy as jnp
        import numpy as np
        B, S, E, H = (2, 512, 256, 16)
        D = E // H
        b, s, e = x.shape
        qkv = jnp.einsum('bse,ef->bsf', x, w_qkv)
        qkv = qkv.reshape(b, s, 3, H, D).transpose(2, 0, 3, 1, 4)
        q, k, v = (qkv[0], qkv[1], qkv[2])
        scale = 1.0 / np.sqrt(D).astype(np.float32)
        scores = jnp.einsum('bhsd,bhtd->bhst', q, k) * scale
        attn = jax.nn.softmax(scores, axis=-1)
        out = jnp.einsum('bhst,bhtd->bhsd', attn, v)
        out = out.transpose(0, 2, 1, 3).reshape(b, s, e)
        return jnp.einsum('bse,ef->bsf', out, w_out)

    def _L0_ffn_ref(x, weight, bias):
        import jax, jax.numpy as jnp
        import numpy as np
        FP8_E4M3_MAX = 448.0

        def fake_quant_fp8(t):
            amax = jnp.max(jnp.abs(t))
            scale = FP8_E4M3_MAX / jnp.maximum(amax, 1e-12)
            q = (t * scale).astype(jnp.float8_e4m3fn).astype(jnp.float32)
            return q / scale
        xq = fake_quant_fp8(x)
        wq = fake_quant_fp8(weight)
        return jnp.einsum('bsd,od->bso', xq, wq) + bias

    def _L1_xattn_ref(query, key, value, mask, Wq, bq, Wk, bk, Wv, bv, Wo, bo):
        import jax, jax.numpy as jnp
        import numpy as np
        H = 16
        D_MODEL = 256
        D_K = D_MODEL // H
        NEG_INF = -1000000000.0

        def _split_heads(x):
            B, S, _ = x.shape
            return x.reshape(B, S, H, D_K).transpose(0, 2, 1, 3)
        B, S, _ = query.shape
        q = _split_heads(query @ Wq.T + bq)
        k = _split_heads(key @ Wk.T + bk)
        v = _split_heads(value @ Wv.T + bv)
        scores = jnp.einsum('bhqd,bhkd->bhqk', q, k) / jnp.sqrt(jnp.float32(D_K))
        m = mask[:, None, :, :] != 0
        scores = jnp.where(m, scores, NEG_INF)
        p_attn = jax.nn.softmax(scores, axis=-1)
        p_attn = jnp.where(m, p_attn, 0.0)
        x = jnp.einsum('bhqk,bhkd->bhqd', p_attn, v)
        x = x.transpose(0, 2, 1, 3).reshape(B, S, D_MODEL)
        return x @ Wo.T + bo

    def _L1_attn_ref(x, w_att_val, wv_w, wv_b, out_w, out_b):
        import jax, jax.numpy as jnp
        import numpy as np
        B, T, E, H = (2, 512, 256, 16)
        D = E // H
        b, t, e = x.shape
        h, d, _ = w_att_val.shape
        x_h = x.reshape(b, t, h, d).transpose(0, 2, 1, 3)
        xw = jnp.einsum('bhtd,hde->bhte', x_h, w_att_val)
        att = jnp.einsum('bhte,bhse->bhts', xw, x_h) / jnp.sqrt(jnp.asarray(d, x.dtype))
        att = jax.nn.softmax(att, axis=-1)
        vx = x @ wv_w.T + wv_b
        vx = vx.reshape(b, t, h, d).transpose(0, 2, 1, 3)
        o = jnp.einsum('bhts,bhsd->bhtd', att, vx)
        o = o.transpose(0, 2, 1, 3).reshape(b, t, e)
        return o @ out_w.T + out_b

    def _L1_ffn_ref(x, shared_up, shared_down, routed_up, routed_down, router_w):
        import jax, jax.numpy as jnp
        import numpy as np
        H, F, E_SHARED, E_ROUTED, K = (256, 1024, 1, 8, 2)

        def _expert(x, w_up, w_down):
            h = jax.nn.gelu(jnp.einsum('bsh,hf->bsf', x, w_up), approximate=False)
            return jnp.einsum('bsf,fh->bsh', h, w_down)
        shared_out = jnp.zeros_like(x)
        for i in range(E_SHARED):
            shared_out = shared_out + _expert(x, shared_up[i], shared_down[i])
        probs = jax.nn.softmax(jnp.einsum('bsh,he->bse', x, router_w), axis=-1)
        top_k_prob, top_k_idx = jax.lax.top_k(probs, K)
        onehot = jax.nn.one_hot(top_k_idx, E_ROUTED, dtype=x.dtype)
        gates = jnp.einsum('bsk,bske->bse', top_k_prob, onehot)
        routed_out = jnp.zeros_like(x)
        for e in range(E_ROUTED):
            y = _expert(x, routed_up[e], routed_down[e])
            routed_out = routed_out + gates[..., e:e + 1] * y
        return shared_out + routed_out + x

    def _L2_xattn_ref(query, key, value, Wq, bq, Wk, bk, Wv, bv, Wp, bp, scale):
        import jax, jax.numpy as jnp
        import numpy as np
        DIM = 256
        HEADS = 16
        HEAD_DIM = DIM // HEADS
        B, N, M = (2, 512, 512)

        def _split_heads(x):
            b, s, c = x.shape
            return x.reshape(b, s, HEADS, HEAD_DIM).transpose(0, 2, 1, 3)
        q = _split_heads(query @ Wq.T + bq)
        k = _split_heads(key @ Wk.T + bk)
        v = _split_heads(value @ Wv.T + bv)
        attn = jnp.einsum('bhnd,bhmd->bhnm', q, k) * scale[0]
        attn = jax.nn.softmax(attn, axis=-1)
        x = jnp.einsum('bhnm,bhmd->bhnd', attn, v)
        x = x.transpose(0, 2, 1, 3).reshape(query.shape)
        return x @ Wp.T + bp

    def _L2_attn_ref(u, W_in, b_in, short_w, short_b, inner_w, inner_b, W_out, b_out):
        import jax, jax.numpy as jnp
        import numpy as np
        D_MODEL = 256

        def dw_causal_conv(x, w, b):
            K = w.shape[1]
            out = jax.lax.conv_general_dilated(x, w[:, None, :], window_strides=(1,), padding=[(K - 1, 0)], feature_group_count=x.shape[1], dimension_numbers=('NCH', 'OIH', 'NCH'))
            return out + b[None, :, None]
        D = D_MODEL
        x = jnp.einsum('bld,de->ble', u, W_in) + b_in
        x = jnp.swapaxes(x, 1, 2)
        uc = dw_causal_conv(x, short_w, short_b)
        q, k, v = (uc[:, :D], uc[:, D:2 * D], uc[:, 2 * D:])
        v = k * v
        v = dw_causal_conv(v, inner_w, inner_b)
        y = q * v
        y = jnp.swapaxes(y, 1, 2)
        return jnp.einsum('bld,de->ble', y, W_out) + b_out

    def _L2_ffn_ref(x, norm_scale, w_router, w_up, w_down):
        import jax, jax.numpy as jnp
        import numpy as np
        EPS = 1e-06
        TOP_K = 2

        def rms_norm(x, scale, eps=EPS):
            xf = x.astype(jnp.float32)
            mean_sq = jnp.mean(xf * xf, axis=-1, keepdims=True)
            return (xf * (scale.astype(jnp.float32) * jax.lax.rsqrt(mean_sq + eps))).astype(x.dtype)
        skip = x
        xn = rms_norm(x, norm_scale)
        scores = jnp.einsum('bsd,ed->bse', xn, w_router)
        _, ids = jax.lax.top_k(scores, TOP_K)
        probs = jax.nn.softmax(scores, axis=-1)
        c = jnp.take_along_axis(probs, ids, axis=-1)
        h = jnp.einsum('bsd,ehd->bseh', xn, w_up)
        val, gate = jnp.split(h, 2, axis=-1)
        h = val * jax.nn.silu(gate)
        y = jnp.einsum('bseh,edh->bsed', h, w_down)
        yk = jnp.take_along_axis(y, ids[..., None], axis=2)
        out = jnp.sum(yk * c[..., None], axis=2)
        return out + skip

    def _L3_xattn_ref(q, k, v, mask, Wq, bq, Wk, bk, Wv, bv, Wo, bo):
        import jax, jax.numpy as jnp
        import numpy as np
        D_MODEL = 256
        NUM_HEADS = 16
        D_K = D_MODEL // NUM_HEADS
        B, S = (2, 512)
        NEG = -1000000000.0

        def _split_heads(x):
            b, s, _ = x.shape
            return x.reshape(b, s, NUM_HEADS, D_K).transpose(0, 2, 1, 3)
        qh = _split_heads(q @ Wq.T + bq)
        kh = _split_heads(k @ Wk.T + bk)
        vh = _split_heads(v @ Wv.T + bv)
        scale = 1.0 / jnp.sqrt(jnp.float32(D_K))
        scores = jnp.einsum('bhqd,bhkd->bhqk', qh, kh) * scale
        scores = jnp.where(mask == 0, jnp.float32(NEG), scores)
        probs = jax.nn.softmax(scores, axis=-1)
        attn = jnp.einsum('bhqk,bhkd->bhqd', probs, vh)
        out = attn.transpose(0, 2, 1, 3).reshape(q.shape[0], q.shape[1], D_MODEL)
        return out @ Wo.T + bo

    def _L3_attn_ref(x, W_qkv, W_out):
        import jax, jax.numpy as jnp
        import numpy as np
        D_MODEL = 256
        NUM_HEADS = 16
        HEAD_DIM = D_MODEL // NUM_HEADS
        THETA = 10000.0
        B, T = (4, 512)

        def _cos_sin(seq_len, head_dim, theta):
            freqs = 1.0 / theta ** (jnp.arange(0, head_dim, 2, dtype=jnp.float32) / head_dim)
            t = jnp.arange(seq_len, dtype=jnp.float32)
            angles = jnp.outer(t, freqs)
            return jnp.concatenate([jnp.cos(angles), jnp.sin(angles)], axis=-1)

        def _apply_rope(x, cos_sin):
            x1 = x[..., 0::2]
            x2 = x[..., 1::2]
            half = x.shape[-1] // 2
            cos = cos_sin[:, :half]
            sin = cos_sin[:, half:]
            out = jnp.stack([x1 * cos - x2 * sin, x1 * sin + x2 * cos], axis=-1)
            return out.reshape(x.shape)
        Bsz, Tlen, _ = x.shape
        qkv = jnp.einsum('bti,oi->bto', x, W_qkv)
        qkv = qkv.reshape(Bsz, Tlen, 3 * NUM_HEADS, HEAD_DIM).transpose(0, 2, 1, 3)
        q, k, v = jnp.split(qkv, 3, axis=1)
        cos_sin = _cos_sin(Tlen, HEAD_DIM, THETA)
        q = _apply_rope(q, cos_sin)
        k = _apply_rope(k, cos_sin)
        scores = jnp.einsum('bhqd,bhkd->bhqk', q, k) / np.sqrt(HEAD_DIM).astype(np.float32)
        causal = jnp.tril(jnp.ones((Tlen, Tlen), dtype=bool))
        scores = jnp.where(causal[None, None], scores, -jnp.inf)
        attn = jax.nn.softmax(scores, axis=-1)
        o = jnp.einsum('bhqk,bhkd->bhqd', attn, v)
        o = o.transpose(0, 2, 1, 3).reshape(Bsz, Tlen, D_MODEL)
        return jnp.einsum('bti,oi->bto', o, W_out)

    def _L3_ffn_ref(x, Wg, bg, W1, b1, W2, b2):
        import jax, jax.numpy as jnp
        import numpy as np
        D_MODEL = 256
        D_HIDDEN = 1024
        NUM_EXPERTS = 8
        B, T = (2, 512)
        gate_logits = jnp.einsum('btd,de->bte', x, Wg) + bg
        gate_scores = jax.nn.softmax(gate_logits, axis=-1)
        top1_idx = jnp.argmax(gate_scores, axis=-1)
        top1_mask = jax.nn.one_hot(top1_idx, NUM_EXPERTS, dtype=x.dtype)
        top1_weight = jnp.sum(gate_scores * top1_mask, axis=-1, keepdims=True)
        h = jax.nn.silu(jnp.einsum('btd,edh->bteh', x, W1) + b1)
        o = jnp.einsum('bteh,ehd->bted', h, W2) + b2
        y = jnp.sum(o * top1_mask[..., None], axis=2) * top1_weight
        return y
    x = x + _L0_xattn_ref(_layernorm(x, axis=-1), ctx_1024, L0_xattn_ln_g, L0_xattn_ln_b, L0_xattn_cln_g, L0_xattn_cln_b, L0_xattn_Wq, L0_xattn_Wkv, L0_xattn_Wo, L0_xattn_Wff1, L0_xattn_Wff2)
    x = x + _L0_attn_ref(_layernorm(x, axis=-1), L0_attn_w_qkv, L0_attn_w_out)
    x = x + _L0_ffn_ref(_layernorm(x, axis=-1), L0_ffn_weight, L0_ffn_bias)
    x = x + _L1_xattn_ref(_layernorm(x, axis=-1), ctx_1024, ctx_1024, mask_Bx1xS2_ik0, L1_xattn_Wq, L1_xattn_bq, L1_xattn_Wk, L1_xattn_bk, L1_xattn_Wv, L1_xattn_bv, L1_xattn_Wo, L1_xattn_bo)
    x = x + _L1_attn_ref(_layernorm(x, axis=-1), L1_attn_w_att_val, L1_attn_wv_w, L1_attn_wv_b, L1_attn_out_w, L1_attn_out_b)
    x = x + _L1_ffn_ref(_layernorm(x, axis=-1), L1_ffn_shared_up, L1_ffn_shared_down, L1_ffn_routed_up, L1_ffn_routed_down, L1_ffn_router_w)
    x = x + _L2_xattn_ref(_layernorm(x, axis=-1), ctx_1024, ctx_1024, L2_xattn_Wq, L2_xattn_bq, L2_xattn_Wk, L2_xattn_bk, L2_xattn_Wv, L2_xattn_bv, L2_xattn_Wp, L2_xattn_bp, L2_xattn_scale)
    x = x + _L2_attn_ref(_layernorm(x, axis=-1), L2_attn_W_in, L2_attn_b_in, L2_attn_short_w, L2_attn_short_b, L2_attn_inner_w, L2_attn_inner_b, L2_attn_W_out, L2_attn_b_out)
    x = x + _L2_ffn_ref(_layernorm(x, axis=-1), L2_ffn_norm_scale, L2_ffn_w_router, L2_ffn_w_up, L2_ffn_w_down)
    x = x + _L3_xattn_ref(_layernorm(x, axis=-1), ctx_1024, ctx_1024, mask_Bx1x1xS2_ik0, L3_xattn_Wq, L3_xattn_bq, L3_xattn_Wk, L3_xattn_bk, L3_xattn_Wv, L3_xattn_bv, L3_xattn_Wo, L3_xattn_bo)
    x = x + _L3_attn_ref(_layernorm(x, axis=-1), L3_attn_W_qkv, L3_attn_W_out)
    x = x + _L3_ffn_ref(_layernorm(x, axis=-1), L3_ffn_Wg, L3_ffn_bg, L3_ffn_W1, L3_ffn_b1, L3_ffn_W2, L3_ffn_b2)
    return x

_drawn_inputs = setup_inputs


def setup_inputs(seed=0):
    import zlib

    import numpy as np

    out = dict(_drawn_inputs(seed))
    spreads = {'L0_xattn_ln_g': (1.0, 0.2),
     'L0_xattn_ln_b': (0.0, 0.1),
     'L0_xattn_cln_g': (1.0, 0.2),
     'L0_xattn_cln_b': (0.0, 0.1),
     'L1_xattn_bq': (0.0, 0.57),
     'L1_xattn_bk': (0.0, 2.0),
     'L1_xattn_bv': (0.0, 0.1),
     'L1_xattn_bo': (0.0, 0.1),
     'L1_attn_wv_b': (0.0, 0.1),
     'L1_attn_out_b': (0.0, 0.1),
     'L2_xattn_bq': (0.0, 0.8),
     'L2_xattn_bk': (0.0, 2.0),
     'L2_xattn_bv': (0.0, 0.764),
     'L2_xattn_bp': (0.0, 0.1),
     'L2_ffn_norm_scale': (1.0, 0.6),
     'L3_xattn_bq': (0.0, 2.0),
     'L3_xattn_bk': (0.0, 2.0),
     'L3_xattn_bv': (0.0, 2.0),
     'L3_xattn_bo': (0.0, 2.0),
     'L3_ffn_bg': (0.0, 0.8),
     'L3_ffn_b1': (0.0, 0.8),
     'L3_ffn_b2': (0.0, 2.0)}
    factors = {'L0_ffn_bias': 8.0,
     'L1_ffn_routed_up': 6.237,
     'L1_ffn_routed_down': 6.079,
     'L1_ffn_router_w': 6.868,
     'L2_xattn_Wq': 8.0,
     'L2_xattn_Wk': 8.0,
     'L2_xattn_Wv': 3.196,
     'L2_xattn_Wp': 2.726,
     'L2_attn_W_in': 8.0,
     'L2_attn_b_in': 8.0,
     'L2_attn_short_w': 8.0,
     'L2_attn_short_b': 8.0,
     'L2_attn_inner_w': 8.0,
     'L2_attn_inner_b': 8.0,
     'L2_attn_W_out': 8.0,
     'L2_attn_b_out': 8.0,
     'L2_ffn_w_router': 8.0,
     'L2_ffn_w_up': 8.0,
     'L2_ffn_w_down': 8.0,
     'L3_xattn_Wq': 8.0,
     'L3_xattn_Wk': 8.0,
     'L3_xattn_Wv': 4.226,
     'L3_xattn_Wo': 3.731,
     'L3_ffn_Wg': 8.0,
     'L3_ffn_W1': 8.0,
     'L3_ffn_W2': 8.0,
     'L3_attn_W_qkv': 3.707,
     'L3_attn_W_out': 3.834}
    for name, (base, spread) in spreads.items():
        noise = np.random.default_rng([zlib.crc32(name.encode()), seed]).standard_normal(out[name].shape)
        drawn = base * np.exp(spread * noise) if base else spread * noise
        out[name] = jnp.asarray(drawn.astype(out[name].dtype))
    for name, factor in factors.items():
        out[name] = (out[name] * factor).astype(out[name].dtype)
    return out
```

```python
from contextlib import ExitStack

import numpy as np

import concourse.bass as bass
from concourse import mybir

F32 = mybir.dt.float32
I32 = mybir.dt.int32
ALU = mybir.AluOpType
ACT = mybir.ActivationFunctionType
AX = mybir.AxisListType

P = 128
B, S, D, H = 16, 64, 256, 16
T = B * S
NT = T // P
DC = D // P
DH = D // H
KEYS = 1601
KT = -(-KEYS // P)
TAIL = KEYS - (KT - 1) * P
BANK = 512
UNITS = H // 2
EPS = 1e-5
MASKED = -float(2**30)


def cols(n, step):
    return [(a, min(step, n - a)) for a in range(0, n, step)]


def keys_in(t):
    return TAIL if t == KT - 1 else P


class Core:

    def __init__(self, nc, dram, ctx):
        self.nc, self.dram = nc, dram
        self.stage = 0

        def sb(name, shape, dt=F32):
            return ctx.enter_context(nc.sbuf_tensor(name, shape, dt))

        self.x = sb("x_res", [P, NT, D])
        self.xn = sb("x_norm", [P, NT, D])
        self.xnt = sb("x_norm_t", [P, DC, T])
        self.gates = sb("gates", [P, NT, 16])
        self.ident = sb("ident", [P, P])
        self.ones = sb("ones", [P, P])
        self.head_of_pair = sb("head_of_pair", [P, 2])


class Stage:

    def __init__(self, core, name):
        core.stage += 1
        self.nc, self.ctx, self.name = core.nc, ExitStack(), f"{name}{core.stage}"
        self.sems = []

    def sb(self, name, shape, dt=F32):
        return self.ctx.enter_context(self.nc.sbuf_tensor(f"{self.name}_{name}", shape, dt))

    def banks(self, name, n, dt=F32):
        return [self.ctx.enter_context(self.nc.psum_tensor(f"{self.name}_{name}{i}", [P, BANK], dt)) for i in range(n)]

    def sem(self, name):
        self.sems.append(self.nc.alloc_semaphore(name=f"{self.name}_{name}"))
        return self.sems[-1]

    def __enter__(self):
        self.ctx.__enter__()
        return self

    def __exit__(self, *e):
        if e[0] is None:
            self.nc.clear_and_free_semaphores(self.sems)
            self.nc.all_engine_barrier()
        return self.ctx.__exit__(*e)


def load_residual(core):
    nc, d = core.nc, core.dram
    with Stage(core, "load") as s:
        loaded = s.sem("loaded")
        ones_set = s.sem("ones_set")
        with nc.Block() as block:

            @block.sync
            def _(sp):
                sp.dma_start(core.x[:, :, :], d["x"].rearrange("(t p) d -> p t d", p=P)).then_inc(loaded, 16)
                sp.dma_start(core.ident[:, :], d["c_ident"]).then_inc(loaded, 16)
                sp.dma_start(core.head_of_pair[:, :], d["c_head_of_pair"]).then_inc(loaded, 16)
                sp.wait_ge(loaded, 48)

            @block.vector
            def _(dve):
                dve.memset(core.ones[:, :], 1.0).then_inc(ones_set, 1)
                dve.wait_ge(ones_set, 1)


def store_residual(core):
    nc, d = core.nc, core.dram
    with Stage(core, "store") as s:
        stored = s.sem("stored")
        with nc.Block() as block:

            @block.sync
            def _(sp):
                sp.dma_start(d["out"].rearrange("(t p) d -> p t d", p=P), core.x[:, :, :]).then_inc(stored, 16)
                sp.wait_ge(stored, 16)


def normalise(core, src, rms=False, gamma=None, beta=None, eps=EPS):
    nc, d = core.nc, core.dram
    dst = core.xn
    with Stage(core, "norm") as s:
        stats = s.sb("stats", [P, NT, 6])
        mean_var = s.sb("mean_var", [P, NT, 2])
        square = s.sb("square", [P, NT])
        spread = s.sb("spread", [P, NT])
        deviation = s.sb("deviation", [P, NT])
        rstd = s.sb("rstd", [P, NT])
        scaled = s.sb("scaled", [P, NT, D]) if rms else dst
        affine = s.sb("affine", [P, 2, DC])
        turned = s.banks("turned", 4)
        loaded, stats_done, aggregated, square_done, spread_done = map(
            s.sem, ("loaded", "stats_done", "aggregated", "square_done", "spread_done"))
        deviation_done, rstd_done, scaled_done, turned_done, copied = map(
            s.sem, ("deviation_done", "rstd_done", "scaled_done", "turned_done", "copied"))
        with nc.Block() as block:

            @block.sync
            def _(sp):
                if gamma:
                    sp.dma_start(affine[:, 0, :], d[gamma].rearrange("(c p) -> p c", p=P),
                                 allow_slow_non_contiguous=True).then_inc(loaded, 16)
                    sp.wait_ge(loaded, 16)
                if beta:
                    sp.dma_start(affine[:, 1, :], d[beta].rearrange("(c p) -> p c", p=P),
                                 allow_slow_non_contiguous=True).then_inc(loaded, 16)
                    sp.wait_ge(loaded, 32)

            @block.vector
            def _(dve):
                for t in range(NT):
                    dve.bn_stats(stats[:, t, :], src[:, t, :]).then_inc(stats_done, 1)
                for t in range(NT):
                    dve.wait_ge(stats_done, t + 1)
                    dve.bn_aggr(mean_var[:, t, :], stats[:, t, :]).then_inc(aggregated, 1)
                dve.wait_ge(aggregated, NT)
                if rms:
                    dve.tensor_tensor(square[:, :], mean_var[:, :, 0], mean_var[:, :, 0], ALU.mult).then_inc(square_done, 1)
                    dve.wait_ge(square_done, 1)
                    dve.scalar_tensor_tensor(out=spread[:, :], in0=mean_var[:, :, 1], scalar=eps, in1=square[:, :],
                                             op0=ALU.add, op1=ALU.add).then_inc(spread_done, 1)
                else:
                    dve.tensor_scalar(spread[:, :], mean_var[:, :, 1], eps, None, ALU.add).then_inc(spread_done, 1)
                dve.wait_ge(deviation_done, 1)
                dve.reciprocal(rstd[:, :], deviation[:, :]).then_inc(rstd_done, 1)
                dve.wait_ge(rstd_done, 1)
                for t in range(NT):
                    if rms:
                        dve.tensor_scalar(scaled[:, t, :], src[:, t, :], rstd[:, t:t + 1], None,
                                          ALU.mult).then_inc(scaled_done, 1)
                    else:
                        dve.tensor_scalar(scaled[:, t, :], src[:, t, :], mean_var[:, t, 0:1], rstd[:, t:t + 1],
                                          ALU.subtract, ALU.mult).then_inc(scaled_done, 1)

            @block.tensor
            def _(pe):
                for g in range(NT // 4):
                    for c in range(DC):
                        pe.wait_ge(scaled_done, 4 * g + 4)
                        for k in range(4):
                            t = 4 * g + k
                            mm = pe.transpose(turned[g * DC + c][:, k * P:(k + 1) * P],
                                              scaled[:, t, c * P:(c + 1) * P], core.ident[:, :])
                        mm.then_inc(turned_done, 1)

            @block.scalar
            def _(act):
                act.wait_ge(spread_done, 1)
                act.activation(deviation[:, :], spread[:, :], ACT.Sqrt).then_inc(deviation_done, 1)
                if gamma:
                    act.wait_ge(loaded, 32 if beta else 16)
                for g in range(NT // 4):
                    for c in range(DC):
                        act.wait_ge(turned_done, g * DC + c + 1)
                        out = core.xnt[:, c, g * 4 * P:(g + 1) * 4 * P]
                        if gamma and beta:
                            act.activation(out, turned[g * DC + c][:, :], ACT.Identity, scale=affine[:, 0, c:c + 1],
                                           bias=affine[:, 1, c:c + 1]).then_inc(copied, 1)
                        elif gamma:
                            act.activation(out, turned[g * DC + c][:, :], ACT.Identity,
                                           scale=affine[:, 0, c:c + 1]).then_inc(copied, 1)
                        else:
                            act.activation(out, turned[g * DC + c][:, :], ACT.Copy).then_inc(copied, 1)
                act.wait_ge(copied, DC * NT // 4)


def project_and_add(core, heads, chunks, weight, bias=None):
    nc, d = core.nc, core.dram
    with Stage(core, "proj") as s:
        w = s.sb("w", [P, chunks, D])
        bias_rows = s.sb("bias_rows", [P, D])
        acc = s.banks("acc", 4)
        loaded, projected, biased, added = map(s.sem, ("loaded", "projected", "biased", "added"))
        n_loads = 2 if bias else 1
        with nc.Block() as block:

            @block.sync
            def _(sp):
                sp.dma_start(w[:, :, :], d[weight].rearrange("(c p) f -> p c f", p=P)).then_inc(loaded, 16)
                if bias:
                    sp.dma_start(bias_rows[:, :], d[bias].partition_broadcast(P)).then_inc(loaded, 16)
                sp.wait_ge(loaded, 16 * n_loads)

            @block.tensor
            def _(pe):
                pe.wait_ge(loaded, 16 * n_loads)
                for t in range(NT):
                    if t >= 4:
                        pe.wait_ge(added, t - 3)
                    for c in range(chunks):
                        mm = pe.matmul(acc[t % 4][:, 0:D], heads[:, c, t * P:(t + 1) * P], w[:, c, :],
                                       start=(c == 0), stop=(c == chunks - 1))
                    mm.then_inc(projected, 1)

            @block.vector
            def _(dve):
                if bias:
                    dve.wait_ge(loaded, 16 * n_loads)
                    dve.tensor_tensor(core.x[:, :, :], core.x[:, :, :],
                                      bias_rows[:, :].unsqueeze(1).broadcast_to([P, NT, D]), ALU.add).then_inc(biased, 1)
                    dve.wait_ge(biased, 1)
                for t in range(NT):
                    dve.wait_ge(projected, t + 1)
                    dve.tensor_tensor(core.x[:, t, :], core.x[:, t, :], acc[t % 4][:, 0:D], ALU.add).then_inc(added, 1)
                dve.wait_ge(added, NT)


def self_attention(core, heads, wq, wk, wv, bv=None, rope=False, causal=False):
    nc, d = core.nc, core.dram
    halves = 2 if rope else 1
    with Stage(core, "self") as s:
        w_q = s.sb("w_q", [P, DC, halves * D])
        w_k = s.sb("w_k", [P, DC, halves * D]) if wk else None
        w_v = s.sb("w_v", [P, DC, D])
        v_bias = s.sb("v_bias", [P, D])
        wave = s.sb("wave", [P, 2, S])
        later = s.sb("later", [P, S])
        quarter = s.sb("quarter", [P, 2])
        tile_t = s.sb("tile_t", [P, DC, P])
        qk = s.sb("qk", [P, 2, DC, P])
        qk_cos = s.sb("qk_cos", [P, 2 * DC, 2, S])
        qk_sin = s.sb("qk_sin", [P, 2 * DC, 2, S])
        q_pair = s.sb("q_pair", [32, UNITS, 2, 2, S])
        k_pair = s.sb("k_pair", [32, UNITS, P])
        v = s.sb("v", [S, 2, D])
        shifted = s.sb("shifted", [P, 2, UNITS, S])
        probs = s.sb("probs", [P, 2, UNITS + 1, S])
        top = s.sb("top", [P, 2, UNITS])
        total = s.sb("total", [P, 2, UNITS])
        share = s.sb("share", [P, 2, UNITS])
        probs_t = s.sb("probs_t", [S, 2, UNITS, P])
        mixed = s.sb("mixed", [P, 2, UNITS, DH])
        qk_ps, swap_ps, v_ps, mixed_ps = s.banks("qk_ps", 4)
        score_ps = s.banks("score_ps", 2)
        turn_ps = s.banks("turn_ps", 2)
        (loaded, quarter_set, tile_copied, q_projected, v_projected, qk_copied, waved, split, v_copied, scored,
         masked, top_found, shift_done, exp_done, sum_done, share_done, turned, turn_copied, weighed, mixed_done,
         mixed_turned, heads_out) = map(s.sem, (
             "loaded", "quarter_set", "tile_copied", "q_projected", "v_projected", "qk_copied", "waved", "split",
             "v_copied", "scored", "masked", "top_found", "shift_done", "exp_done", "sum_done", "share_done",
             "turned", "turn_copied", "weighed", "mixed_done", "mixed_turned", "heads_out"))
        n_loads = 2 + bool(wk) + bool(bv) + bool(rope) + bool(causal)
        with nc.Block() as block:

            @block.sync
            def _(sp):
                sp.dma_start(w_q[:, :, :], d[wq].rearrange("(c p) f -> p c f", p=P)).then_inc(loaded, 16)
                sp.dma_start(w_v[:, :, :], d[wv].rearrange("(c p) f -> p c f", p=P)).then_inc(loaded, 16)
                if wk:
                    sp.dma_start(w_k[:, :, :], d[wk].rearrange("(c p) f -> p c f", p=P)).then_inc(loaded, 16)
                if bv:
                    sp.dma_start(v_bias[:, :], d[bv].partition_broadcast(P)).then_inc(loaded, 16)
                if rope:
                    sp.dma_start(wave[:, :, :], d["c_wave"]).then_inc(loaded, 16)
                if causal:
                    sp.dma_start(later[:, :], d["c_later"]).then_inc(loaded, 16)
                sp.wait_ge(loaded, 16 * n_loads)

            @block.tensor
            def _(pe):
                pe.wait_ge(loaded, 16 * n_loads)
                with pe.Fori(0, NT) as i:
                    pe.wait_ge(quarter_set, 2)
                    pe.wait_ge(tile_copied, i + 1)
                    for c2 in range(DC):
                        for c in range(DC):
                            mm = pe.matmul(qk_ps[:, c2 * P:(c2 + 1) * P], w_q[:, c, c2 * P:(c2 + 1) * P],
                                           tile_t[:, c, :], start=(c == 0), stop=(c == DC - 1))
                        if wk:
                            for c in range(DC):
                                mm = pe.matmul(qk_ps[:, (DC + c2) * P:(DC + c2 + 1) * P],
                                               w_k[:, c, c2 * P:(c2 + 1) * P],
                                               tile_t[:, c, :], start=(c == 0), stop=(c == DC - 1))
                        if rope:
                            for n, w in enumerate((w_q, w_k)):
                                for c in range(DC):
                                    mm = pe.matmul(swap_ps[:, (n * DC + c2) * P:(n * DC + c2 + 1) * P],
                                                   w[:, c, D + c2 * P:D + (c2 + 1) * P],
                                                   tile_t[:, c, :], start=(c == 0), stop=(c == DC - 1))
                    mm.then_inc(q_projected, 1)
                    for j in range(2):
                        for c in range(DC):
                            mm = pe.matmul(v_ps[0:S, j * D:(j + 1) * D], tile_t[:, c, j * S:(j + 1) * S],
                                           w_v[:, c, :], start=(c == 0), stop=(c == DC - 1))
                    mm.then_inc(v_projected, 1)
                    pe.wait_ge(split, i + 1)
                    for j in range(2):
                        for u in range(UNITS):
                            mm = pe.matmul(score_ps[j][:, u * S:(u + 1) * S], q_pair[:, u, j, :, :],
                                           k_pair[:, u, j * S:(j + 1) * S], start=True, stop=True)
                        mm.then_inc(scored, 1)
                    for j in range(2):
                        pe.wait_ge(exp_done, 2 * i + j + 1)
                        if j:
                            pe.wait_ge(turn_copied, 2 * i + 1)
                        for u in range(UNITS):
                            mm = pe.transpose(turn_ps[u // 4][:, (u % 4) * P:(u % 4 + 1) * P],
                                              probs[:, j, u:u + 2, :], core.ident[:, :])
                        mm.then_inc(turned, 1)
                    for j in range(2):
                        pe.wait_ge(turn_copied, 2 * i + j + 1)
                        pe.wait_ge(v_copied, i + 1)
                        for u in range(UNITS):
                            mm = pe.matmul(mixed_ps[:, j * D + u * 32:j * D + (u + 1) * 32], probs_t[:, j, u, :],
                                           v[:, j, u * 32:(u + 1) * 32], start=True, stop=True)
                        mm.then_inc(weighed, 1)
                    for j in range(2):
                        pe.wait_ge(mixed_done, 4 * i + 2 * j + 2)
                        mm = pe.transpose(qk_ps[:, j * P:(j + 1) * P], mixed[:, j, :, :], core.ident[:, :])
                    mm.then_inc(mixed_turned, 1)

            @block.scalar
            def _(act):
                with act.Fori(0, NT) as i:
                    if True:
                        act.wait_ge(heads_out, i)
                    act.activation(tile_t[:, :, :], core.xnt[:, :, bass.ds(i * P, P)], ACT.Copy).then_inc(tile_copied, 1)
                    act.wait_ge(q_projected, i + 1)
                    act.activation(qk[:, 0, :, :], qk_ps[:, 0:DC * P], ACT.Copy).then_inc(qk_copied, 1)
                    act.wait_ge(tile_copied, i + 1)
                    act.activation(qk[:, 1, :, :], qk_ps[:, DC * P:2 * DC * P] if wk else tile_t[:, :, :],
                                   ACT.Copy).then_inc(qk_copied, 1)
                    act.wait_ge(v_projected, i + 1)
                    if not bv:
                        act.activation(v[:, :, :], v_ps[0:S, :], ACT.Copy).then_inc(v_copied, 1)
                    for j in range(2):
                        act.wait_ge(shift_done, 2 * i + j + 1)
                        act.activation(probs[:, j, 0:UNITS, :], shifted[:, j, :, :], ACT.Exp).then_inc(exp_done, 1)
                    for j in range(2):
                        act.wait_ge(turned, 2 * i + j + 1)
                        act.activation(probs_t[:, j, 0:4, :], turn_ps[0][0:S, :], ACT.Copy)
                        act.activation(probs_t[:, j, 4:8, :], turn_ps[1][0:S, :], ACT.Copy).then_inc(turn_copied, 1)

            @block.vector
            def _(dve):
                dve.tensor_scalar(quarter[:, :], core.head_of_pair[:, :], DH ** -0.5, None, ALU.mult).then_inc(quarter_set, 1)
                dve.memset(probs[:, :, UNITS, :], 0.0).then_inc(quarter_set, 1)
                dve.wait_ge(quarter_set, 2)
                dve.wait_ge(loaded, 16 * n_loads)
                with dve.Fori(0, NT) as i:
                    dve.wait_ge(qk_copied, 2 * i + 2)
                    source = qk[:, :, :, :].rearrange("p n c (j s) -> p (n c) j s", j=2)
                    if rope:
                        swap = swap_ps[:, :].rearrange("p (n j s) -> p n j s", n=2 * DC, j=2)
                        for n in range(2 * DC):
                            dve.tensor_tensor(qk_cos[:, n], source[:, n],
                                              wave[:, 0:1, :].broadcast_to([P, 2, S]), ALU.mult)
                            rot = dve.tensor_tensor(qk_sin[:, n], swap[:, n],
                                                    wave[:, 1:2, :].broadcast_to([P, 2, S]), ALU.mult)
                        rot.then_inc(waved, 1)
                        dve.wait_ge(waved, 2 * i + 1)
                        dve.tensor_tensor(qk_cos[:, :, :, :], qk_cos[:, :, :, :], qk_sin[:, :, :, :], ALU.add).then_inc(waved, 1)
                        dve.wait_ge(waved, 2 * i + 2)
                        source = qk_cos[:, :, :, :]
                    for a in range(4):
                        rows = slice(32 * a, 32 * a + 32)
                        for c in range(DC):
                            u = 4 * c + a
                            for h2 in range(2):
                                dve.tensor_scalar(q_pair[:, u, :, h2, :], source[rows, c, :, :],
                                                  quarter[rows, h2:h2 + 1], None, ALU.mult)
                            cut = dve.tensor_copy(k_pair[:, u, :].rearrange("p (j s) -> p j s", j=2),
                                                  source[rows, DC + c, :, :])
                    cut.then_inc(split, 1)
                    if bv:
                        dve.wait_ge(v_projected, i + 1)
                        dve.tensor_tensor(v[:, :, :], v_ps[0:S, :].rearrange("p (j f) -> p j f", j=2),
                                          v_bias[0:S, :].unsqueeze(1).broadcast_to([S, 2, D]), ALU.add).then_inc(v_copied, 1)
                    for j in range(2):
                        dve.wait_ge(scored, 2 * i + j + 1)
                        score = score_ps[j][:, :].rearrange("p (u s) -> p u s", u=UNITS)
                        if causal:
                            dve.tensor_tensor(shifted[:, j], score,
                                              later[:, :].unsqueeze(1).broadcast_to([P, UNITS, S]), ALU.add).then_inc(masked, 1)
                            dve.wait_ge(masked, 2 * i + j + 1)
                            score = shifted[:, j]
                        dve.tensor_reduce(top[:, j, :], score, AX.X, ALU.max).then_inc(top_found, 1)
                        dve.wait_ge(top_found, 2 * i + j + 1)
                        dve.tensor_tensor(shifted[:, j], score, top[:, j, :].unsqueeze(2).broadcast_to([P, UNITS, S]),
                                          ALU.subtract).then_inc(shift_done, 1)
                    for j in range(2):
                        dve.wait_ge(exp_done, 2 * i + j + 1)
                        dve.tensor_reduce(total[:, j, :], probs[:, j, 0:UNITS, :], AX.X, ALU.add).then_inc(sum_done, 1)
                        dve.wait_ge(sum_done, 2 * i + j + 1)
                        dve.reciprocal(share[:, j, :], total[:, j, :]).then_inc(share_done, 1)
                    for j in range(2):
                        dve.wait_ge(weighed, 2 * i + 2)
                        dve.wait_ge(share_done, 2 * i + j + 1)
                        out = mixed_ps[:, j * D:(j + 1) * D].rearrange("p (u h f) -> p u h f", u=UNITS, h=2)
                        for h2 in range(2):
                            rows = slice(S * h2, S * h2 + S)
                            dve.tensor_tensor(mixed[rows, j, :, :], out[rows, :, h2, :],
                                              share[rows, j, :].unsqueeze(2).broadcast_to([S, UNITS, DH]),
                                              ALU.mult).then_inc(mixed_done, 1)
                    dve.wait_ge(mixed_turned, i + 1)
                    dve.tensor_copy(heads[:, 0:2, bass.ds(i * P, P)].rearrange("p h (j s) -> p h j s", j=2),
                                    qk_ps[:, 0:2 * P].rearrange("p (j h s) -> p h j s", j=2, h=2)).then_inc(heads_out, 1)
                dve.wait_ge(heads_out, NT)


def cross_attention(core, heads, wq, wk, wv, bq=None, bk=None, bv=None, mask=None, mask_cols=None, mask_values=False,
                    scale=None, context_gamma=None, context_beta=None):
    nc, d = core.nc, core.dram
    shared = context_gamma is not None
    kd = 64 if shared else 32
    extra = 2 if mask else 1
    dv = 64 if shared else 32
    nk = 1 if shared else UNITS
    n_q = 1024 if shared else D
    out_chunks = UNITS * (dv if shared else DH) // P
    with Stage(core, "cross") as s:
        w_q = s.sb("w_q", [P, DC, n_q])
        w_k = s.sb("w_k", [P, DC, kd if shared else D])
        w_v = s.sb("w_v", [P, DC, dv if shared else D])
        bias_cols = s.sb("bias_cols", [P, 2, DC])
        v_bias = s.sb("v_bias", [P, D])
        scale_col = s.sb("scale_col", [P, 1])
        q_scale = s.sb("q_scale", [P, 2])
        ctx_t = s.sb("ctx_t", [P, DC, KEYS])
        k_t = s.sb("k_t", [P, DC, KEYS]) if not shared else None
        k_rows = s.sb("k_rows", [kd + extra, nk, KEYS])
        q_rows = s.sb("q_rows", [kd + extra, UNITS, 2, S])
        v = s.sb("v", [P, KT, nk, dv + 1])
        probs = s.sb("probs", [P, KT, P])
        top_parts = s.sb("top_parts", [P, 2, 4])
        top_cols = s.sb("top_cols", [P, 2])
        share = s.sb("share", [P, UNITS])
        mixed = s.sb("mixed", [P, UNITS, dv if shared else DH])
        if mask:
            mask_int = s.sb("mask_int", [P, KEYS], I32)
            keep = s.sb("keep", [P, KEYS])
            mask_row = s.sb("mask_row", [1, KEYS])
            keep_int = s.sb("keep_int", [P, KT], I32)
            keep_cols = s.sb("keep_cols", [P, KT])
        if shared:
            ctx_raw = s.sb("ctx_raw", [P, KT, D])
            stats = s.sb("stats", [P, KT, 6])
            mean_var = s.sb("mean_var", [P, KT, 2])
            spread = s.sb("spread", [P, KT])
            deviation = s.sb("deviation", [P, KT])
            rstd = s.sb("rstd", [P, KT])
            affine = s.sb("affine", [P, 2, DC])
        score_ps = s.banks("score_ps", 2)
        weight_ps = s.banks("weight_ps", 3)
        mixed_ps = s.banks("mixed_ps", 1)[0]
        proj_ps = s.banks("proj_ps", 2)
        key_cols = cols(KEYS, BANK)
        NKC = len(key_cols)
        (loaded, raw_in, rows_set, mask_in, kept, row_ready, q_scaled, q_projected, q_split, k_projected, k_copied,
         k_placed, v_projected, v_copied, v_masked, scored, part_found, top_found, top_turned, top_placed, weighed,
         exp_done, mixed_done, share_done, mixed_out, mixed_turned, heads_out) = map(s.sem, (
             "loaded", "raw_in", "rows_set", "mask_in", "kept", "row_ready", "q_scaled", "q_projected",
             "q_split", "k_projected", "k_copied", "k_placed", "v_projected", "v_copied", "v_masked", "scored",
             "part_found", "top_found", "top_turned", "top_placed", "weighed", "exp_done", "mixed_done", "share_done",
             "mixed_out", "mixed_turned", "heads_out"))
        (stats_done, aggregated, spread_done, deviation_done, rstd_done, normed, ctx_turned,
         ctx_placed, spread_set) = map(s.sem, ("stats_done", "aggregated", "spread_done", "deviation_done", "rstd_done",
                                   "normed", "ctx_turned", "ctx_placed", "spread_set"))
        n_loads = 3 + 2 * bool(bq) + bool(bv) + bool(scale) + 2 * shared
        k_pieces = NKC * (1 if shared else DC)
        key_groups = cols(KT, 4)
        n_turns = DC * len(key_groups)
        q_cuts = 2 if shared else 2 * UNITS
        n_placed = 16 * (4 + (UNITS if mask else 0))
        with nc.Block() as block:

            @block.sync
            def _(sp):
                if context_gamma:
                    sp.dma_start(affine[:, 0, :], d[context_gamma].rearrange("(c p) -> p c", p=P),
                                 allow_slow_non_contiguous=True).then_inc(loaded, 16)
                    sp.dma_start(affine[:, 1, :], d[context_beta].rearrange("(c p) -> p c", p=P),
                                 allow_slow_non_contiguous=True).then_inc(loaded, 16)
                sp.dma_start(w_q[:, :, :], d[wq].rearrange("(c p) f -> p c f", p=P)).then_inc(loaded, 16)
                sp.dma_start(w_k[:, :, :], d[wk].rearrange("(c p) f -> p c f", p=P)).then_inc(loaded, 16)
                sp.dma_start(w_v[:, :, :], d[wv].rearrange("(c p) f -> p c f", p=P)).then_inc(loaded, 16)
                if bq:
                    for n, name in enumerate((bq, bk)):
                        sp.dma_start(bias_cols[:, n, :], d[name].rearrange("(c p) -> p c", p=P),
                                     allow_slow_non_contiguous=True).then_inc(loaded, 16)
                if bv:
                    sp.dma_start(v_bias[:, :], d[bv].partition_broadcast(P)).then_inc(loaded, 16)
                if scale:
                    sp.dma_start(scale_col[:, :], d[scale].partition_broadcast(P)).then_inc(loaded, 16)
                with sp.Fori(0, B) as b:
                    if shared:
                        sp.wait_ge(ctx_turned, n_turns * b)
                    else:
                        sp.wait_ge(v_projected, KT * b)
                    if shared:
                        rows = d["ctx"][bass.ds(b, 1), :, :].rearrange("b n f -> (b n) f")
                        sp.dma_start(ctx_raw[:, 0:KT - 1, :],
                                     rows[0:(KT - 1) * P, :].rearrange("(t p) f -> p t f", p=P)).then_inc(raw_in, 16)
                        sp.dma_start(ctx_raw[0:TAIL, KT - 1, :], rows[(KT - 1) * P:KEYS, :]).then_inc(raw_in, 16)
                    else:
                        sp.dma_start(ctx_t[:, :, :], d["ctx_t"][bass.ds(b, 1), :, :].rearrange(
                            "b (c p) n -> p (b c) n", p=P)).then_inc(raw_in, 16)
                    if mask:
                        sp.wait_ge(kept, 2 * b)
                        sp.dma_start(mask_int[:, :], d[mask][bass.ds(b, 1), :].rearrange(
                            "b n -> (b n)").partition_broadcast(P)).then_inc(mask_in, 16)
                        sp.dma_start(keep_int[:, :], d[mask_cols][bass.ds(b, 1), :, :].rearrange(
                            "b p t -> p (b t)")).then_inc(mask_in, 16)
                    if not shared:
                        sp.wait_ge(mixed_done, UNITS * b)
                        sp.wait_ge(k_copied, k_pieces * (b + 1))
                        for a in range(4):
                            sp.dma_start(k_rows[0:32, :, :].rearrange("p (c a) n -> p c a n", a=4)[:, :, a, :],
                                         k_t[32 * a:32 * a + 32, :, :]).then_inc(k_placed, 16)
                        if mask:
                            sp.wait_ge(row_ready, b + 1)
                            sp.wait_ge(rows_set, 4)
                            for u in range(UNITS):
                                sp.dma_start(k_rows[kd:kd + 1, u, :], mask_row[:, :]).then_inc(k_placed, 16)
                sp.wait_ge(raw_in, 16 * (2 if shared else 1) * B)
                if not shared:
                    sp.wait_ge(k_placed, n_placed * B)

            if mask_values:
                @block.gpsimd
                def _(pool):
                    with pool.Fori(0, B) as b:
                        pool.wait_ge(kept, 2 * (b + 1))
                        pool.wait_ge(v_copied, KT * (b + 1))
                        whole, last = v[:, 0:KT - 1, :, :], v[0:TAIL, KT - 1, :, :]
                        pool.tensor_tensor(whole[:, :, :, 0:dv], whole[:, :, :, 0:dv],
                                           keep_cols[:, 0:KT - 1].unsqueeze(2).unsqueeze(3).broadcast_to(
                                               [P, KT - 1, nk, dv]), ALU.mult).then_inc(v_masked, 1)
                        pool.tensor_tensor(last[:, :, 0:dv], last[:, :, 0:dv],
                                           keep_cols[0:TAIL, KT - 1:KT].unsqueeze(2).broadcast_to([TAIL, nk, dv]),
                                           ALU.mult).then_inc(v_masked, 1)

            @block.tensor
            def _(pe):
                pe.wait_ge(loaded, 16 * n_loads)
                pe.wait_ge(rows_set, 3)

                def scores(b, u):
                    for n, (a, w) in enumerate(key_cols):
                        if n >= 2:
                            pe.wait_ge(part_found, NKC * (UNITS * b + u) + n - 1)
                        elif u >= 1:
                            pe.wait_ge(part_found, NKC * (UNITS * b + u) + n - 1)
                        rows = kd + extra - 1
                        pe.matmul(score_ps[n % 2][:, 0:w], q_rows[0:rows, u, :, :],
                                  k_rows[0:rows, u % nk, a:a + w], start=True, stop=True).then_inc(scored, 1)

                def place_top(b, u):
                    pe.wait_ge(top_found, UNITS * b + u + 1)
                    pe.matmul(proj_ps[0][kd:kd + extra, 0:P], top_cols[:, 2 - extra:2], core.ident[:, :],
                              start=True, stop=True, tile_position=(0, kd)).then_inc(top_turned, 1)

                with pe.Fori(0, B) as b:
                    if shared:
                        pe.wait_ge(normed, KT * (b + 1))
                        n = 0
                        for c in range(DC):
                            for t0, k in key_groups:
                                if n >= 2:
                                    pe.wait_ge(ctx_placed, n_turns * b + n - 1)
                                for t in range(t0, t0 + k):
                                    m = keys_in(t)
                                    mm = pe.transpose(proj_ps[n % 2][:, (t - t0) * P:(t - t0) * P + m],
                                                      ctx_raw[0:m, t, c * P:(c + 1) * P], core.ident[0:m, 0:m])
                                mm.then_inc(ctx_turned, 1)
                                n += 1
                        pe.wait_ge(ctx_placed, n_turns * (b + 1))
                    for c2 in range(n_q // P):
                        for c in range(DC):
                            mm = pe.matmul(weight_ps[0][:, c2 * S:(c2 + 1) * S], w_q[:, c, c2 * P:(c2 + 1) * P],
                                           core.xnt[:, c, bass.ds(b * S, S)], start=(c == 0), stop=(c == DC - 1))
                    mm.then_inc(q_projected, 1)
                    if not shared:
                        pe.wait_ge(raw_in, 16 * (b + 1))
                    n = 0
                    for c2 in range(1 if shared else DC):
                        m = kd if shared else P
                        for a, w in key_cols:
                            if n >= 2:
                                pe.wait_ge(k_copied, k_pieces * b + n - 1)
                            for c in range(DC):
                                mm = pe.matmul(proj_ps[n % 2][0:m, 0:w], w_k[:, c, c2 * P:c2 * P + m],
                                               ctx_t[:, c, a:a + w], start=(c == 0), stop=(c == DC - 1))
                            mm.then_inc(k_projected, 1)
                            n += 1
                    nv = dv if shared else D
                    for t in range(KT):
                        if t >= 2:
                            pe.wait_ge(v_copied, KT * b + t - 1)
                        m = keys_in(t)
                        for c in range(DC):
                            mm = pe.matmul(score_ps[t % 2][0:m, 0:nv], ctx_t[:, c, t * P:t * P + m], w_v[:, c, :],
                                           start=(c == 0), stop=(c == DC - 1))
                        mm.then_inc(v_projected, 1)
                    pe.wait_ge(v_copied, KT * (b + 1))
                    if mask_values:
                        pe.wait_ge(v_masked, 2 * (b + 1))
                    pe.wait_ge(k_copied, k_pieces * (b + 1))
                    if not shared:
                        pe.wait_ge(k_placed, n_placed * (b + 1))
                    pe.wait_ge(q_split, q_cuts * (b + 1))
                    scores(b, 0)
                    place_top(b, 0)
                    for u in range(UNITS):
                        pe.wait_ge(top_placed, UNITS * b + u + 1)
                        for g, (t0, k) in enumerate(key_groups):
                            n = len(key_groups) * u + g
                            if n >= 3:
                                pe.wait_ge(exp_done, len(key_groups) * UNITS * b + n - 2)
                            for t in range(t0, t0 + k):
                                m = keys_in(t)
                                mm = pe.matmul(weight_ps[n % 3][0:m, (t - t0) * P:(t - t0 + 1) * P],
                                               k_rows[:, u % nk, t * P:t * P + m], q_rows[:, u, :, :],
                                               start=True, stop=True)
                            mm.then_inc(weighed, 1)
                        if u + 1 < UNITS:
                            scores(b, u + 1)
                        if u:
                            pe.wait_ge(mixed_out, 2 * (UNITS * b + u))
                        for t in range(KT):
                            g = [i for i, (t0, k) in enumerate(key_groups) if t0 <= t < t0 + k][0]
                            pe.wait_ge(exp_done, len(key_groups) * (UNITS * b + u) + g + 1)
                            m = keys_in(t)
                            mm = pe.matmul(mixed_ps[:, 0:dv + 1], probs[0:m, t, :], v[0:m, t, u % nk, :],
                                           start=(t == 0), stop=(t == KT - 1))
                            if t == KT // 2 and u + 1 < UNITS:
                                place_top(b, u + 1)
                        mm.then_inc(mixed_done, 1)
                    pe.wait_ge(mixed_out, 2 * UNITS * (b + 1))
                    for c in range(out_chunks):
                        w = UNITS // out_chunks
                        mm = pe.transpose(proj_ps[1][:, c * P:(c + 1) * P], mixed[:, c * w:(c + 1) * w, :],
                                          core.ident[:, :])
                    mm.then_inc(mixed_turned, 1)
                    pe.wait_ge(heads_out, b + 1)

            @block.scalar
            def _(act):
                act.wait_ge(loaded, 16 * n_loads)
                with act.Fori(0, B) as b:
                    if shared:
                        act.wait_ge(spread_done, b + 1)
                        act.activation(deviation[:, :], spread[:, :], ACT.Sqrt).then_inc(deviation_done, 1)
                        n = 0
                        for c in range(DC):
                            for t0, k in key_groups:
                                act.wait_ge(ctx_turned, n_turns * b + n + 1)
                                w = min(k * P, KEYS - t0 * P)
                                act.activation(ctx_t[:, c, t0 * P:t0 * P + w], proj_ps[n % 2][:, 0:w], ACT.Identity,
                                               scale=affine[:, 0, c:c + 1], bias=affine[:, 1, c:c + 1]).then_inc(ctx_placed, 1)
                                n += 1
                    if not mask:
                        n = 0
                        for c2 in range(1 if shared else DC):
                            for a, w in key_cols:
                                act.wait_ge(k_projected, k_pieces * b + n + 1)
                                if shared:
                                    act.activation(k_rows[0:kd, 0, a:a + w], proj_ps[n % 2][0:kd, 0:w],
                                                   ACT.Copy).then_inc(k_copied, 1)
                                else:
                                    act.activation(k_t[:, c2, a:a + w], proj_ps[n % 2][:, 0:w], ACT.Identity,
                                                   bias=bias_cols[:, 1, c2:c2 + 1]).then_inc(k_copied, 1)
                                n += 1
                    if shared:
                        for t in range(KT):
                            m = keys_in(t)
                            act.wait_ge(v_projected, KT * b + t + 1)
                            act.activation(v[0:m, t, 0, 0:dv], score_ps[t % 2][0:m, 0:dv], ACT.Copy).then_inc(v_copied, 1)
                    for u in range(UNITS):
                        for g, (t0, k) in enumerate(key_groups):
                            n = len(key_groups) * u + g
                            act.wait_ge(weighed, len(key_groups) * UNITS * b + n + 1)
                            m = P if k > 1 else TAIL
                            act.activation(probs[0:m, t0:t0 + k, :], weight_ps[n % 3][0:m, 0:k * P],
                                           ACT.Exp).then_inc(exp_done, 1)

            @block.vector
            def _(dve):
                dve.memset(k_rows[kd:kd + extra, :, :], 1.0).then_inc(rows_set, 1)
                dve.memset(v[:, :, :, dv:dv + 1], 1.0).then_inc(rows_set, 1)
                dve.memset(q_rows[kd:kd + extra, :, :, :], 1.0).then_inc(rows_set, 1)
                dve.memset(top_cols[:, :], 1.0).then_inc(rows_set, 1)
                dve.wait_ge(loaded, 16 * n_loads)
                dve.wait_ge(rows_set, 4)
                if scale:
                    dve.tensor_scalar(q_scale[:, :], core.head_of_pair[:, :], scale_col[:, 0:1], None,
                                      ALU.mult).then_inc(q_scaled, 1)
                else:
                    dve.tensor_scalar(q_scale[:, :], core.head_of_pair[:, :], DH ** -0.5, None,
                                      ALU.mult).then_inc(q_scaled, 1)
                dve.wait_ge(q_scaled, 1)
                with dve.Fori(0, B) as b:
                    if shared:
                        dve.wait_ge(raw_in, 32 * (b + 1))
                        for t in range(KT):
                            m = keys_in(t)
                            dve.bn_stats(stats[0:m, t, :], ctx_raw[0:m, t, :]).then_inc(stats_done, 1)
                        dve.wait_ge(stats_done, KT * (b + 1))
                        dve.memset(mean_var[:, :, :], 0.0).then_inc(spread_set, 1)
                        dve.wait_ge(spread_set, b + 1)
                        dve.memset(spread[:, :], 0.0)
                        for t in range(KT):
                            m = keys_in(t)
                            dve.bn_aggr(mean_var[0:m, t, :], stats[0:m, t, :]).then_inc(aggregated, 1)
                        dve.wait_ge(aggregated, KT * (b + 1))
                        dve.tensor_scalar(spread[:, :], mean_var[:, :, 1], EPS, None, ALU.add).then_inc(spread_done, 1)
                        dve.wait_ge(deviation_done, b + 1)
                        dve.reciprocal(rstd[:, :], deviation[:, :]).then_inc(rstd_done, 1)
                        dve.wait_ge(rstd_done, b + 1)
                        for t in range(KT):
                            m = keys_in(t)
                            dve.tensor_scalar(ctx_raw[0:m, t, :], ctx_raw[0:m, t, :], mean_var[0:m, t, 0:1],
                                              rstd[0:m, t:t + 1], ALU.subtract, ALU.mult).then_inc(normed, 1)
                    if mask:
                        dve.wait_ge(mask_in, 32 * (b + 1))
                        dve.wait_ge(k_placed, n_placed * b)
                        if mask_values:
                            dve.wait_ge(v_masked, 2 * b)
                        dve.tensor_scalar(keep[:, :], mask_int[:, :], 0, None, ALU.not_equal).then_inc(kept, 1)
                        dve.tensor_scalar(keep_cols[:, :], keep_int[:, :], 0, None, ALU.not_equal).then_inc(kept, 1)
                        dve.wait_ge(kept, 2 * (b + 1))
                        dve.tensor_scalar(mask_row[:, :], keep[0:1, :], -MASKED, MASKED, ALU.mult,
                                          ALU.add).then_inc(row_ready, 1)
                    dve.wait_ge(q_projected, b + 1)
                    if shared:
                        q = weight_ps[0][:, :].rearrange("p (u s) -> p u s", u=UNITS)
                        for h2 in range(2):
                            dve.tensor_scalar(q_rows[0:kd, :, h2, :], q[kd * h2:kd * h2 + kd], kd ** -0.5, None,
                                              ALU.mult).then_inc(q_split, 1)
                    else:
                        for c in range(DC):
                            for a in range(4):
                                rows = slice(32 * a, 32 * a + 32)
                                for h2 in range(2):
                                    dve.tensor_scalar(q_rows[0:kd, 4 * c + a, h2, :],
                                                      weight_ps[0][rows, c * S:(c + 1) * S],
                                                      bias_cols[rows, 0, c:c + 1], q_scale[rows, h2:h2 + 1],
                                                      ALU.add, ALU.mult).then_inc(q_split, 1)
                    if mask:
                        n = 0
                        for c2 in range(DC):
                            for a, w in key_cols:
                                dve.wait_ge(k_projected, k_pieces * b + n + 1)
                                dve.scalar_tensor_tensor(out=k_t[:, c2, a:a + w], in0=proj_ps[n % 2][:, 0:w],
                                                         scalar=bias_cols[:, 1, c2:c2 + 1], in1=keep[:, a:a + w],
                                                         op0=ALU.add, op1=ALU.mult).then_inc(k_copied, 1)
                                n += 1
                    if not shared:
                        for t in range(KT):
                            m = keys_in(t)
                            dve.wait_ge(v_projected, KT * b + t + 1)
                            dve.tensor_tensor(v[0:m, t, :, 0:dv],
                                              score_ps[t % 2][0:m, 0:D].rearrange("p (u f) -> p u f", u=UNITS),
                                              v_bias[0:m, :].rearrange("p (u f) -> p u f", u=UNITS),
                                              ALU.add).then_inc(v_copied, 1)

                    def find_top(u):
                        for n, (a, w) in enumerate(key_cols):
                            dve.wait_ge(scored, NKC * (UNITS * b + u) + n + 1)
                            dve.tensor_reduce(top_parts[:, u % 2, n:n + 1], score_ps[n % 2][:, 0:w], AX.X,
                                              ALU.max).then_inc(part_found, 1)
                        dve.wait_ge(part_found, NKC * (UNITS * b + u + 1))
                        dve.tensor_reduce(top_cols[:, 1:2], top_parts[:, u % 2, :], AX.X, ALU.max,
                                          negate=True).then_inc(top_found, 1)

                    def put_top(u):
                        dve.wait_ge(top_turned, UNITS * b + u + 1)
                        dve.tensor_copy(q_rows[kd:kd + extra, u, :, :], proj_ps[0][kd:kd + extra, 0:P]).then_inc(top_placed, 1)

                    find_top(0)
                    put_top(0)
                    for u in range(UNITS):
                        if u + 1 < UNITS:
                            find_top(u + 1)
                            put_top(u + 1)
                        dve.wait_ge(mixed_done, UNITS * b + u + 1)
                        dve.reciprocal(share[:, u:u + 1], mixed_ps[:, dv:dv + 1]).then_inc(share_done, 1)
                        dve.wait_ge(share_done, UNITS * b + u + 1)
                        for h2 in range(2):
                            rows = slice(S * h2, S * h2 + S)
                            f = 0 if shared else DH * h2
                            dve.tensor_scalar(mixed[rows, u, :], mixed_ps[rows, f:f + (dv if shared else DH)],
                                              share[rows, u:u + 1], None, ALU.mult).then_inc(mixed_out, 1)
                    dve.wait_ge(mixed_turned, b + 1)
                    dve.tensor_copy(heads[:, 0:2 * out_chunks, bass.ds(b * S, S)],
                                    proj_ps[1][:, 0:out_chunks * P].rearrange("p (c s) -> p c s", s=S)).then_inc(heads_out, 1)
                dve.wait_ge(heads_out, B)


def choose_experts(core, router, bias=None, experts=8, first=2, by_score=False, at=0):
    nc, d = core.nc, core.dram
    E = experts
    with Stage(core, "gate") as s:
        w = s.sb("w", [P, DC, E])
        bias_rows = s.sb("bias_rows", [P, E])
        lower = s.sb("lower", [P, E, E])
        score = s.sb("score", [P, NT, E])
        top = s.sb("top", [P, NT])
        prob = s.sb("prob", [P, NT, E])
        total = s.sb("total", [P, NT])
        share = s.sb("share", [P, NT])
        above = s.sb("above", [P, NT, E, E])
        equal = s.sb("equal", [P, NT, E, E])
        rank = s.sb("rank", [P, NT, E])
        logit = s.banks("logit", 1)[0]
        loaded, routed, exp_done, step = map(s.sem, ("loaded", "routed", "exp_done", "step"))
        n_loads = 2 + bool(bias)

        def over_tile(a):
            return a.unsqueeze(1).broadcast_to([P, NT] + list(a.shape[1:]))

        with nc.Block() as block:

            @block.sync
            def _(sp):
                sp.dma_start(w[:, :, :], d[router].rearrange("(c p) e -> p c e", p=P)).then_inc(loaded, 16)
                sp.dma_start(lower[:, :, :], d["c_lower"]).then_inc(loaded, 16)
                if bias:
                    sp.dma_start(bias_rows[:, :], d[bias].partition_broadcast(P)).then_inc(loaded, 16)
                sp.wait_ge(loaded, 16 * n_loads)

            @block.tensor
            def _(pe):
                pe.wait_ge(loaded, 16 * n_loads)
                for t in range(NT):
                    for c in range(DC):
                        mm = pe.matmul(logit[:, t * E:(t + 1) * E], core.xnt[:, c, t * P:(t + 1) * P], w[:, c, :],
                                       start=(c == 0), stop=(c == DC - 1))
                mm.then_inc(routed, 1)

            @block.scalar
            def _(act):
                act.wait_ge(step, 3)
                act.activation(prob[:, :, :], prob[:, :, :], ACT.Exp).then_inc(exp_done, 1)

            @block.vector
            def _(dve):
                n = [0]

                def chain(i):
                    n[0] += 1
                    i.then_inc(step, 1)
                    dve.wait_ge(step, n[0])

                dve.wait_ge(loaded, 16 * n_loads)
                dve.wait_ge(routed, 1)
                got = logit[:, 0:NT * E].rearrange("p (t e) -> p t e", t=NT)
                if bias:
                    chain(dve.tensor_tensor(score[:, :, :], got, over_tile(bias_rows[:, :]), ALU.add))
                else:
                    chain(dve.tensor_copy(score[:, :, :], got))
                chain(dve.tensor_reduce(top[:, :], score[:, :, :], AX.X, ALU.max))
                chain(dve.tensor_tensor(prob[:, :, :], score[:, :, :], top[:, :].unsqueeze(2).broadcast_to([P, NT, E]),
                                        ALU.subtract))
                dve.wait_ge(exp_done, 1)
                chain(dve.tensor_reduce(total[:, :], prob[:, :, :], AX.X, ALU.add))
                chain(dve.reciprocal(share[:, :], total[:, :]))
                chain(dve.tensor_tensor(prob[:, :, :], prob[:, :, :], share[:, :].unsqueeze(2).broadcast_to([P, NT, E]),
                                        ALU.mult))
                key = score if by_score else prob
                mine = key[:, :, :].unsqueeze(3).broadcast_to([P, NT, E, E])
                other = key[:, :, :].unsqueeze(2).broadcast_to([P, NT, E, E])
                chain(dve.tensor_tensor(equal[:, :, :, :], other, mine, ALU.is_equal))
                chain(dve.tensor_tensor(equal[:, :, :, :], equal[:, :, :, :], over_tile(lower[:, :, :]), ALU.mult))
                chain(dve.tensor_tensor(above[:, :, :, :], other, mine, ALU.is_gt))
                chain(dve.tensor_tensor(above[:, :, :, :], above[:, :, :, :], equal[:, :, :, :], ALU.add))
                chain(dve.tensor_reduce(rank[:, :, :], above[:, :, :, :], AX.X, ALU.add))
                chain(dve.tensor_scalar(rank[:, :, :], rank[:, :, :], float(first) - 0.5, None, ALU.is_lt))
                chain(dve.tensor_tensor(core.gates[:, :, at:at + E], rank[:, :, :], prob[:, :, :], ALU.mult))


def feed_forward(core, up, down, hidden, experts, func, paired=False, up_bias=None, down_bias=None, gated=True,
                 first_gate_one=False, add_norm=False):
    nc, d = core.nc, core.dram
    pieces = cols(hidden, P)
    NF = len(pieces)
    TH = T // BANK
    wide = hidden * (2 if paired else 1)
    full = hidden // P
    rest = hidden - full * P
    with Stage(core, "ffn") as s:
        w_up = s.sb("w_up", [P, DC, wide])
        w_down = s.sb("w_down", [P, NF, D])
        hid = s.sb("hid", [P, NF, T])
        gate_act = s.sb("gate_act", [P, 2, BANK]) if paired else None
        bias_now = s.sb("bias_now", [P, NF])
        down_bias_rows = s.sb("down_bias_rows", [8, D]) if down_bias else None
        gates_t = s.sb("gates_t", [8, T]) if down_bias else None
        up_ps = s.banks("up_ps", 4)
        out_ps = s.banks("out_ps", 4)
        (up_in, down_in, loaded, started, up_used, down_used, up_done, act_done, hid_done, out_done, added,
         gates_turned, gates_copied, bias_in) = map(s.sem, (
             "up_in", "down_in", "loaded", "started", "up_used", "down_used", "up_done", "act_done", "hid_done",
             "out_done", "added", "gates_turned", "gates_copied", "bias_in"))
        n_down = (1 if full else 0) + (1 if rest else 0)
        n_up = NF * TH
        n_started = first_gate_one + add_norm
        n_bias = NT if down_bias else 0
        with nc.Block() as block:

            @block.sync
            def _(sp):
                if down_bias:
                    sp.dma_start(down_bias_rows[:, :], d[down_bias]).then_inc(loaded, 16)
                with sp.Fori(0, experts) as e:
                    sp.wait_ge(up_used, e)
                    sp.dma_start(w_up[:, :, :], d[up][bass.ds(e, 1), :, :].rearrange(
                        "e (c p) f -> p (e c) f", p=P)).then_inc(up_in, 16)
                    if up_bias:
                        sp.wait_ge(hid_done, n_up * e)
                        sp.dma_start(bias_now[:, :], d[up_bias][bass.ds(e, 1), :, :].rearrange(
                            "e p f -> p (e f)")).then_inc(bias_in, 16)
                    sp.wait_ge(down_used, e)
                    rows = d[down][bass.ds(e, 1), :, :].rearrange("e f m -> (e f) m")
                    if full:
                        sp.dma_start(w_down[:, 0:full, :],
                                     rows[0:full * P, :].rearrange("(f p) m -> p f m", p=P)).then_inc(down_in, 16)
                    if rest:
                        sp.dma_start(w_down[0:rest, full, :], rows[full * P:hidden, :]).then_inc(down_in, 16)
                if up_bias:
                    sp.wait_ge(bias_in, 16 * experts)
                    sp.wait_ge(loaded, 16)
                sp.wait_ge(up_in, 16 * experts)
                sp.wait_ge(down_in, 16 * n_down * experts)

            @block.tensor
            def _(pe):
                if down_bias:
                    for h in range(TH):
                        for k in range(4):
                            t = 4 * h + k
                            mm = pe.transpose(up_ps[h][0:8, k * P:(k + 1) * P], core.gates[:, t, 0:8], core.ident[:, :])
                        mm.then_inc(gates_turned, 1)
                    pe.wait_ge(gates_copied, TH)
                    pe.wait_ge(loaded, 16)
                    for t in range(NT):
                        if t >= 4:
                            pe.wait_ge(added, t - 3)
                        pe.matmul(out_ps[t % 4][:, 0:D], gates_t[:, t * P:(t + 1) * P], down_bias_rows[:, :],
                                  start=True, stop=True).then_inc(out_done, 1)
                with pe.Fori(0, experts) as e:
                    pe.wait_ge(up_in, 16 * (e + 1))
                    n = 0
                    for f, (a, w) in enumerate(pieces):
                        for h in range(TH):
                            if n >= (2 if paired else 4):
                                pe.wait_ge(hid_done, n_up * e + n - (1 if paired else 3))
                            for part in range(2 if paired else 1):
                                bank = up_ps[(2 * n + part) % 4] if paired else up_ps[n % 4]
                                for c in range(DC):
                                    mm = pe.matmul(bank[0:w, :], w_up[:, c, part * hidden + a:part * hidden + a + w],
                                                   core.xnt[:, c, h * BANK:(h + 1) * BANK],
                                                   start=(c == 0), stop=(c == DC - 1))
                            mm.then_inc(up_done, 1)
                            n += 1
                    pe.wait_ge(down_in, 16 * n_down * (e + 1))
                    pe.wait_ge(hid_done, n_up * (e + 1))
                    for t in range(NT):
                        if t >= 4:
                            pe.wait_ge(added, n_bias + NT * e + t - 3)
                        elif down_bias:
                            pe.wait_ge(added, NT * e + t + 5)
                        else:
                            pe.wait_ge(added, NT * e)
                        for f, (a, w) in enumerate(pieces):
                            mm = pe.matmul(out_ps[t % 4][:, 0:D], hid[0:w, f, t * P:(t + 1) * P], w_down[0:w, f, :],
                                           start=(f == 0), stop=(f == NF - 1))
                        mm.then_inc(out_done, 1)

            @block.scalar
            def _(act):
                if down_bias:
                    for h in range(TH):
                        act.wait_ge(gates_turned, h + 1)
                        act.activation(gates_t[:, h * BANK:(h + 1) * BANK], up_ps[h][0:8, :], ACT.Copy).then_inc(gates_copied, 1)
                with act.Fori(0, experts) as e:
                    n = 0
                    if up_bias:
                        act.wait_ge(bias_in, 16 * (e + 1))
                    for f, (a, w) in enumerate(pieces):
                        for h in range(TH):
                            act.wait_ge(up_done, n_up * e + n + 1)
                            if paired:
                                if n >= 2:
                                    act.wait_ge(hid_done, n_up * e + n - 1)
                                act.activation(gate_act[0:w, n % 2, :], up_ps[(2 * n + 1) % 4][0:w, :], func).then_inc(act_done, 1)
                            elif up_bias:
                                act.activation(hid[0:w, f, h * BANK:(h + 1) * BANK], up_ps[n % 4][0:w, :], func,
                                               bias=bias_now[0:w, f:f + 1]).then_inc(hid_done, 1)
                            else:
                                act.activation(hid[0:w, f, h * BANK:(h + 1) * BANK], up_ps[n % 4][0:w, :],
                                               func).then_inc(hid_done, 1)
                            n += 1

            @block.vector
            def _(dve):
                if first_gate_one:
                    dve.memset(core.gates[:, :, 0:1], 1.0).then_inc(started, 1)
                if add_norm:
                    dve.tensor_tensor(core.x[:, :, :], core.x[:, :, :], core.xn[:, :, :], ALU.add).then_inc(started, 1)
                if n_started:
                    dve.wait_ge(started, n_started)
                if down_bias:
                    for t in range(NT):
                        dve.wait_ge(out_done, t + 1)
                        dve.tensor_tensor(core.x[:, t, :], core.x[:, t, :], out_ps[t % 4][:, 0:D], ALU.add).then_inc(added, 1)
                with dve.Fori(0, experts) as e:
                    if paired:
                        n = 0
                        for f, (a, w) in enumerate(pieces):
                            for h in range(TH):
                                dve.wait_ge(act_done, n_up * e + n + 1)
                                dve.tensor_tensor(hid[0:w, f, h * BANK:(h + 1) * BANK], up_ps[(2 * n) % 4][0:w, :],
                                                  gate_act[0:w, n % 2, :], ALU.mult).then_inc(hid_done, 1)
                                n += 1
                    for t in range(NT):
                        dve.wait_ge(out_done, n_bias + NT * e + t + 1)
                        dve.wait_ge(added, n_bias + NT * e + t - (NT - 1) if down_bias else NT * e)
                        if gated:
                            gate = core.gates[:, t, bass.ds(e, 1)]
                            dve.scalar_tensor_tensor(out=core.x[:, t, :], in0=out_ps[t % 4][:, 0:D], scalar=gate,
                                                     in1=core.x[:, t, :], op0=ALU.mult, op1=ALU.add).then_inc(added, 1)
                        else:
                            dve.tensor_tensor(core.x[:, t, :], core.x[:, t, :], out_ps[t % 4][:, 0:D],
                                              ALU.add).then_inc(added, 1)
                dve.wait_ge(added, n_bias + NT * experts)

            @block.gpsimd
            def _(pool):
                with pool.Fori(0, experts) as e:
                    pool.wait_ge(up_done, n_up * (e + 1))
                    pool.nop().then_inc(up_used, 1)
                    pool.wait_ge(out_done, n_bias + NT * (e + 1))
                    pool.nop().then_inc(down_used, 1)


def quantised_linear(core, weight, bias, grid_max=448.0, least=1e-12):
    nc, d = core.nc, core.dram
    with Stage(core, "fp8") as s:
        w = s.sb("w", [P, DC, D])
        bias_rows = s.sb("bias_rows", [P, D])
        tensors = [core.xnt[:, :, :].rearrange("p c t -> p (c t)"), w[:, :, :].rearrange("p c f -> p (c f)")]
        sizes = [DC * T, DC * D]
        peak = s.sb("peak", [P, 2])
        peak_row = s.sb("peak_row", [1, 2])
        row = s.sb("row", [1, 2])
        scale = s.sb("scale", [P, 2])
        back = s.sb("back", [P, 2])
        back_both = s.sb("back_both", [P, 1])
        scaled = s.sb("scaled", [P, DC * T])
        magic = s.sb("magic", [P, DC * T])
        quant = [s.sb("quant_x", [P, DC, T]), s.sb("quant_w", [P, DC, D])]
        turn_ps, cast_ps = s.banks("turn_ps", 2)
        out_ps = s.banks("out_ps", 4)
        loaded, step, peaks_turned, rows_cast, projected, added = map(
            s.sem, ("loaded", "step", "peaks_turned", "rows_cast", "projected", "added"))
        with nc.Block() as block:

            @block.sync
            def _(sp):
                sp.dma_start(w[:, :, :], d[weight].rearrange("(c p) f -> p c f", p=P)).then_inc(loaded, 16)
                sp.dma_start(bias_rows[:, :], d[bias].partition_broadcast(P)).then_inc(loaded, 16)
                sp.wait_ge(loaded, 32)

            @block.tensor
            def _(pe):
                pe.wait_ge(step, 2)
                for n in range(2):
                    mm = pe.transpose(turn_ps[0:1, n * P:(n + 1) * P], peak[:, n:n + 1], core.ident[:, :])
                mm.then_inc(peaks_turned, 1)
                pe.wait_ge(step, 6)
                pe.matmul(cast_ps[:, 0:2], core.ones[0:1, :], row[:, :], start=True, stop=True).then_inc(rows_cast, 1)
                pe.wait_ge(step, 19)
                for t in range(NT):
                    if t >= 4:
                        pe.wait_ge(added, t - 3)
                    for c in range(DC):
                        mm = pe.matmul(out_ps[t % 4][:, 0:D], quant[0][:, c, t * P:(t + 1) * P], quant[1][:, c, :],
                                       start=(c == 0), stop=(c == DC - 1))
                    mm.then_inc(projected, 1)

            @block.vector
            def _(dve):
                n = [0]

                def chain(i):
                    n[0] += 1
                    i.then_inc(step, 1)
                    dve.wait_ge(step, n[0])

                dve.wait_ge(loaded, 32)
                for k in range(2):
                    chain(dve.tensor_reduce(peak[:, k:k + 1], tensors[k], AX.X, ALU.max, apply_absolute_value=True))
                dve.wait_ge(peaks_turned, 1)
                chain(dve.tensor_reduce(peak_row[:, :], turn_ps[0:1, 0:2 * P].rearrange("p (n k) -> p n k", n=2), AX.X,
                                        ALU.max))
                chain(dve.tensor_scalar(peak_row[:, :], peak_row[:, :], least, None, ALU.max))
                chain(dve.reciprocal(row[:, :], peak_row[:, :]))
                chain(dve.tensor_scalar(row[:, :], row[:, :], grid_max, None, ALU.mult))
                dve.wait_ge(rows_cast, 1)
                chain(dve.tensor_copy(scale[:, :], cast_ps[:, 0:2]))
                chain(dve.reciprocal(back[:, :], scale[:, :]))
                chain(dve.tensor_tensor(back_both[:, :], back[:, 0:1], back[:, 1:2], ALU.mult))
                for k in range(2):
                    v, m = scaled[:, 0:sizes[k]], magic[:, 0:sizes[k]]
                    q = quant[k][:, :, :].rearrange("p c t -> p (c t)")
                    chain(dve.tensor_scalar(v, tensors[k], scale[:, k:k + 1], None, ALU.mult))
                    chain(dve.tensor_scalar(m.bitcast(I32), v.bitcast(I32), 0x7F800000, None, ALU.bitwise_and))
                    chain(dve.tensor_scalar(m, m, 2.0 ** -6, 1.5 * 2.0 ** 20, ALU.max, ALU.mult))
                    chain(dve.tensor_tensor(v, v, m, ALU.add))
                    chain(dve.tensor_tensor(q, v, m, ALU.subtract))
                chain(dve.tensor_tensor(core.x[:, :, :], core.x[:, :, :],
                                        bias_rows[:, :].unsqueeze(1).broadcast_to([P, NT, D]), ALU.add))
                for t in range(NT):
                    dve.wait_ge(projected, t + 1)
                    dve.scalar_tensor_tensor(out=core.x[:, t, :], in0=out_ps[t % 4][:, 0:D], scalar=back_both[:, 0:1],
                                             in1=core.x[:, t, :], op0=ALU.mult, op1=ALU.add).then_inc(added, 1)
                dve.wait_ge(added, NT)


def gated_convolution(core, mixed):
    nc, d = core.nc, core.dram
    CH = 3 * DC
    PAD = 3
    G = CH * (T // BANK)
    with Stage(core, "conv") as s:
        w_in = s.sb("w_in", [P, DC, 3 * D])
        in_bias = s.sb("in_bias", [P, CH])
        short_w = s.sb("short_w", [P, CH, 3])
        short_b = s.sb("short_b", [P, CH])
        inner_w = s.sb("inner_w", [P, DC, 4])
        inner_b = s.sb("inner_b", [P, DC])
        z = s.sb("z", [P, CH, B, PAD + S])
        conv = s.sb("conv", [P, CH, B, S])
        kv = s.sb("kv", [P, DC, B, PAD + S])
        ps = s.banks("ps", 4)
        loaded, padded, projected, copied, short_done, kv_done, inner_done, mixed_done = map(
            s.sem, ("loaded", "padded", "projected", "copied", "short_done", "kv_done", "inner_done", "mixed_done"))
        with nc.Block() as block:

            @block.sync
            def _(sp):
                sp.dma_start(w_in[:, :, :], d["L2_attn_W_in"].rearrange("(c p) f -> p c f", p=P)).then_inc(loaded, 16)
                for dst, name in ((in_bias[:, :], "L2_attn_b_in"), (short_b[:, :], "L2_attn_short_b"),
                                  (inner_b[:, :], "L2_attn_inner_b")):
                    sp.dma_start(dst, d[name].rearrange("(c p) -> p c", p=P),
                                 allow_slow_non_contiguous=True).then_inc(loaded, 16)
                for dst, name in ((short_w[:, :, :], "L2_attn_short_w"), (inner_w[:, :, :], "L2_attn_inner_w")):
                    sp.dma_start(dst, d[name].rearrange("(c p) k -> p c k", p=P),
                                 allow_slow_non_contiguous=True).then_inc(loaded, 16)
                sp.wait_ge(loaded, 96)

            @block.gpsimd
            def _(pool):
                pool.memset(z[:, :, :, 0:PAD], 0.0).then_inc(padded, 1)
                pool.memset(kv[:, :, :, 0:PAD], 0.0).then_inc(padded, 1)
                pool.wait_ge(padded, 2)

            @block.tensor
            def _(pe):
                pe.wait_ge(loaded, 96)
                n = 0
                for ch in range(CH):
                    for h in range(T // BANK):
                        if n >= 4:
                            pe.wait_ge(copied, n - 3)
                        for c in range(DC):
                            mm = pe.matmul(ps[n % 4][:, :], w_in[:, c, ch * P:(ch + 1) * P],
                                           core.xnt[:, c, h * BANK:(h + 1) * BANK], start=(c == 0), stop=(c == DC - 1))
                        mm.then_inc(projected, 1)
                        n += 1

            @block.scalar
            def _(act):
                act.wait_ge(loaded, 96)
                n = 0
                for ch in range(CH):
                    for h in range(T // BANK):
                        act.wait_ge(projected, n + 1)
                        nb = BANK // S
                        act.activation(z[:, ch, h * nb:(h + 1) * nb, PAD:],
                                       ps[n % 4][:, :].rearrange("p (b s) -> p b s", s=S), ACT.Identity,
                                       bias=in_bias[:, ch:ch + 1]).then_inc(copied, 1)
                        n += 1

            @block.vector
            def _(dve):
                dve.wait_ge(loaded, 96)
                dve.wait_ge(padded, 2)

                def taps(dst, src, w, bias, done, before):
                    K = w.shape[1]
                    for k in range(K):
                        part = src[:, :, PAD - K + 1 + k:PAD - K + 1 + k + S]
                        if k == 0:
                            dve.tensor_scalar(dst, part, w[:, 0:1], bias, ALU.mult, ALU.add).then_inc(done, 1)
                        else:
                            dve.wait_ge(done, before + k)
                            dve.scalar_tensor_tensor(out=dst, in0=part, scalar=w[:, k:k + 1], in1=dst, op0=ALU.mult,
                                                     op1=ALU.add).then_inc(done, 1)

                for ch in range(CH):
                    dve.wait_ge(copied, 2 * ch + 2)
                    taps(conv[:, ch], z[:, ch], short_w[:, ch, :], short_b[:, ch:ch + 1], short_done, 3 * ch)
                dve.wait_ge(short_done, 3 * CH)
                for c in range(DC):
                    dve.tensor_tensor(kv[:, c, :, PAD:], conv[:, DC + c], conv[:, 2 * DC + c], ALU.mult).then_inc(kv_done, 1)
                dve.wait_ge(kv_done, DC)
                for c in range(DC):
                    taps(conv[:, DC + c], kv[:, c], inner_w[:, c, :], inner_b[:, c:c + 1], inner_done, 4 * c)
                dve.wait_ge(inner_done, 4 * DC)
                for c in range(DC):
                    dve.tensor_tensor(mixed[:, c, :], conv[:, c].rearrange("p b s -> p (b s)"),
                                      conv[:, DC + c].rearrange("p b s -> p (b s)"), ALU.mult).then_inc(mixed_done, 1)
                dve.wait_ge(mixed_done, DC)


def build(nc, dram, stages=range(12)):
    with ExitStack() as ctx:
        core = Core(nc, dram, ctx)
        load_residual(core)

        def with_heads(chunks, attend, weight, bias=None):
            with nc.sbuf_tensor(f"heads{core.stage}", [P, chunks, T], F32) as heads:
                attend(heads)
                project_and_add(core, heads, chunks, weight, bias)

        def layer0_cross():
            normalise(core, core.x)
            normalise(core, core.xn, gamma="L0_xattn_ln_g", beta="L0_xattn_ln_b")
            with_heads(8, lambda h: cross_attention(
                core, h, "L0_xattn_Wq", "L0_xattn_Wk", "L0_xattn_Wv", context_gamma="L0_xattn_cln_g",
                context_beta="L0_xattn_cln_b"), "L0_xattn_Wo")
            feed_forward(core, "L0_xattn_Wff1", "L0_xattn_Wff2", 4 * D, 1, ACT.Silu, paired=True, gated=False)

        def cross(p, mask=None, mask_cols=None, mask_values=False, scale=None):
            normalise(core, core.x)
            with_heads(2, lambda h: cross_attention(
                core, h, p + "Wq", p + "Wk", p + "Wv", p + "bq", p + "bk", p + "bv", mask=mask, mask_cols=mask_cols,
                mask_values=mask_values, scale=scale), p + "Wo", p + "bo")

        def layer0_self():
            normalise(core, core.x)
            with_heads(2, lambda h: self_attention(core, h, "L0_attn_wq", "L0_attn_wk", "L0_attn_wv"), "L0_attn_w_out")

        def layer0_ffn():
            normalise(core, core.x)
            quantised_linear(core, "L0_ffn_weight", "L0_ffn_bias")

        def layer1_self():
            normalise(core, core.x)
            with_heads(2, lambda h: self_attention(core, h, "L1_attn_wq", None, "L1_attn_wv", bv="L1_attn_wv_b"),
                       "L1_attn_out_w", "L1_attn_out_b")

        def layer1_ffn():
            normalise(core, core.x)
            choose_experts(core, "L1_ffn_router_w", first=2, at=1)
            feed_forward(core, "L1_ffn_up", "L1_ffn_down", 1024, 9, ACT.Gelu, first_gate_one=True, add_norm=True)

        def layer2_conv():
            normalise(core, core.x)
            with_heads(2, lambda h: gated_convolution(core, h), "L2_attn_W_out", "L2_attn_b_out")

        def layer2_ffn():
            normalise(core, core.x)
            normalise(core, core.xn, rms=True, gamma="L2_ffn_norm_scale", eps=1e-6)
            choose_experts(core, "L2_ffn_w_router", first=2, by_score=True)
            feed_forward(core, "L2_ffn_w_up", "L2_ffn_w_down", 704, 8, ACT.Silu, paired=True, add_norm=True)

        def layer3_self():
            normalise(core, core.x)
            with_heads(2, lambda h: self_attention(core, h, "L3_attn_wq", "L3_attn_wk", "L3_attn_wv", rope=True,
                                                   causal=True), "L3_attn_W_out")

        def layer3_ffn():
            normalise(core, core.x)
            choose_experts(core, "L3_ffn_Wg", bias="L3_ffn_bg", first=1)
            feed_forward(core, "L3_ffn_W1", "L3_ffn_W2", 1024, 8, ACT.Silu, up_bias="L3_ffn_b1", down_bias="L3_ffn_b2")

        run = [
            layer0_cross, layer0_self, layer0_ffn,
            lambda: cross("L1_xattn_", mask="mask1", mask_cols="mask1_cols", mask_values=True), layer1_self, layer1_ffn,
            lambda: cross("L2_xattn_", scale="L2_xattn_scale"), layer2_conv, layer2_ffn,
            lambda: cross("L3_xattn_", mask="mask3", mask_cols="mask3_cols"), layer3_self, layer3_ffn,
        ]
        for n in stages:
            run[n]()
        store_residual(core)


def lay_out(a):
    o = {}
    o["x"] = a["x"].reshape(T, D)
    o["ctx"] = a["ctx_1024"]
    o["ctx_t"] = a["ctx_1024"].transpose(0, 2, 1)
    for n, name in (("1", "mask_Bx1xS2_ik0"), ("3", "mask_Bx1x1xS2_ik0")):
        m = a[name].reshape(B, KEYS)
        o["mask" + n] = m
        o[f"mask{n}_cols"] = np.pad(m, ((0, 0), (0, KT * P - KEYS))).reshape(B, KT, P).transpose(0, 2, 1)

    def pair_rows(w):
        return w.reshape(UNITS, 2, DH, D).transpose(1, 0, 2, 3).reshape(D, D)

    for k in ("ln_g", "ln_b", "cln_g", "cln_b", "Wq"):
        o["L0_xattn_" + k] = a["L0_xattn_" + k]
    o["L0_xattn_Wk"], o["L0_xattn_Wv"] = a["L0_xattn_Wkv"][:, :64], a["L0_xattn_Wkv"][:, 64:]
    o["L0_xattn_Wo"] = a["L0_xattn_Wo"].reshape(4, 2, 2, 64, D).transpose(0, 2, 1, 3, 4).reshape(1024, D)
    o["L0_xattn_Wff1"], o["L0_xattn_Wff2"] = a["L0_xattn_Wff1"][None], a["L0_xattn_Wff2"][None]
    w = a["L0_attn_w_qkv"]
    o["L0_attn_wq"], o["L0_attn_wk"], o["L0_attn_wv"] = w[:, :D], w[:, D:2 * D], w[:, 2 * D:]
    o["L0_attn_w_out"] = pair_rows(a["L0_attn_w_out"])
    o["L0_ffn_weight"], o["L0_ffn_bias"] = a["L0_ffn_weight"].T, a["L0_ffn_bias"]
    for p, out in (("L1_xattn_", "o"), ("L2_xattn_", "p"), ("L3_xattn_", "o")):
        for k in ("Wq", "Wk", "Wv"):
            o[p + k] = a[p + k].T
        for k in ("bq", "bk", "bv"):
            o[p + k] = a[p + k]
        o[p + "Wo"], o[p + "bo"] = pair_rows(a[p + "W" + out].T), a[p + "b" + out]
    o["L2_xattn_scale"] = a["L2_xattn_scale"]
    o["L1_attn_wq"] = np.zeros((D, D), a["L1_attn_w_att_val"].dtype)
    for h in range(H):
        o["L1_attn_wq"][h * DH:(h + 1) * DH, h * DH:(h + 1) * DH] = a["L1_attn_w_att_val"][h]
    o["L1_attn_wv"], o["L1_attn_wv_b"] = a["L1_attn_wv_w"].T, a["L1_attn_wv_b"]
    o["L1_attn_out_w"], o["L1_attn_out_b"] = pair_rows(a["L1_attn_out_w"].T), a["L1_attn_out_b"]
    o["L1_ffn_up"] = np.concatenate([a["L1_ffn_shared_up"], a["L1_ffn_routed_up"]])
    o["L1_ffn_down"] = np.concatenate([a["L1_ffn_shared_down"], a["L1_ffn_routed_down"]])
    o["L1_ffn_router_w"] = a["L1_ffn_router_w"]
    for k in ("W_in", "b_in", "short_w", "short_b", "inner_w", "inner_b", "W_out", "b_out"):
        o["L2_attn_" + k] = a["L2_attn_" + k]
    o["L2_ffn_norm_scale"] = a["L2_ffn_norm_scale"]
    o["L2_ffn_w_router"] = a["L2_ffn_w_router"].T
    o["L2_ffn_w_up"], o["L2_ffn_w_down"] = a["L2_ffn_w_up"].transpose(0, 2, 1), a["L2_ffn_w_down"].transpose(0, 2, 1)
    w = a["L3_attn_W_qkv"].T
    swap = np.arange(D) ^ 1
    o["L3_attn_wq"] = np.concatenate([w[:, :D], w[:, :D][:, swap]], axis=1)
    o["L3_attn_wk"] = np.concatenate([w[:, D:2 * D], w[:, D:2 * D][:, swap]], axis=1)
    o["L3_attn_wv"], o["L3_attn_W_out"] = w[:, 2 * D:], pair_rows(a["L3_attn_W_out"].T)
    for k in ("Wg", "bg", "W1", "W2", "b2"):
        o["L3_ffn_" + k] = a["L3_ffn_" + k]
    o["L3_ffn_b1"] = a["L3_ffn_b1"].reshape(8, 8, P).transpose(0, 2, 1)
    o["c_ident"] = np.eye(P, dtype=np.float32)
    o["c_head_of_pair"] = (np.arange(P)[:, None] // DH % 2 == np.arange(2)[None, :]).astype(np.float32)
    o["c_lower"] = np.broadcast_to(np.tril(np.ones((8, 8), np.float32), -1), (P, 8, 8))
    o["c_later"] = np.where(np.arange(S)[None, :] > np.arange(P)[:, None] % S, np.float32(-1e30), np.float32(0))
    freqs = 1.0 / 10000.0 ** (np.arange(0, DH, 2) / DH)
    angle = np.arange(S)[None, :] * freqs[np.arange(P) % DH // 2][:, None]
    sign = np.where(np.arange(P) % 2 == 0, -1.0, 1.0)[:, None]
    o["c_wave"] = np.stack([np.cos(angle), np.sin(angle) * sign], axis=1).astype(np.float32)
    return {k: np.ascontiguousarray(v) for k, v in o.items()}


def kernel(**inputs):
    import concourse.bacc as bacc
    from concourse.bass_utils import run_bass_kernel_spmd

    arrays = lay_out({k: np.asarray(v) for k, v in inputs.items()})
    nc = bacc.Bacc("TRN2", target_bir_lowering=False, num_devices=1)
    dram = {k: nc.dram_tensor(f"in_{k}", v.shape, mybir.dt.from_np(v.dtype), kind="ExternalInput").ap()
            for k, v in arrays.items()}
    dram["out"] = nc.dram_tensor("out_x", (T, D), F32, kind="ExternalOutput").ap()
    build(nc, dram)
    r = run_bass_kernel_spmd(nc, [{f"in_{k}": v for k, v in arrays.items()}], core_ids=[0])
    return r.results[0]["out_x"].reshape(B, S, D)
```

```python
from contextlib import ExitStack

import numpy as np

import concourse.bass as bass
from concourse import mybir

F32 = mybir.dt.float32
I32 = mybir.dt.int32
F16 = mybir.dt.float16
ALU = mybir.AluOpType
ACT = mybir.ActivationFunctionType
AX = mybir.AxisListType

P = 128
B, S, D, H = 16, 64, 256, 16
T = B * S
NT = T // P
DC = D // P
DH = D // H
KEYS = 1601
KT = -(-KEYS // P)
TAIL = KEYS - (KT - 1) * P
BANK = 512
UNITS = H // 2
EPS = 1e-5
SHIFT = float(2**15)
W_SCALE = 64.0


def cols(n, step):
    return [(a, min(step, n - a)) for a in range(0, n, step)]


def keys_in(t):
    return TAIL if t == KT - 1 else P


class Core:

    def __init__(self, nc, dram, ctx):
        self.nc, self.dram = nc, dram
        self.stage = 0

        def sb(name, shape, dt=F32):
            return ctx.enter_context(nc.sbuf_tensor(name, shape, dt))

        self.x = sb("x_res", [P, NT, D])
        self.xn = sb("x_norm", [P, NT, D])
        self.xnt = sb("x_norm_t", [P, DC, T])
        self.gates = sb("gates", [P, NT, 16])
        self.ident = sb("ident", [P, P])
        self.ones = sb("ones", [P, P])
        self.head_of_pair = sb("head_of_pair", [P, 2])


class Stage:

    def __init__(self, core, name):
        core.stage += 1
        self.nc, self.ctx, self.name = core.nc, ExitStack(), f"{name}{core.stage}"
        self.sems = []

    def sb(self, name, shape, dt=F32):
        return self.ctx.enter_context(self.nc.sbuf_tensor(f"{self.name}_{name}", shape, dt))

    def banks(self, name, n, dt=F32):
        return [self.ctx.enter_context(self.nc.psum_tensor(f"{self.name}_{name}{i}", [P, BANK], dt)) for i in range(n)]

    def sem(self, name):
        self.sems.append(self.nc.alloc_semaphore(name=f"{self.name}_{name}"))
        return self.sems[-1]

    def __enter__(self):
        self.ctx.__enter__()
        return self

    def __exit__(self, *e):
        if e[0] is None:
            self.nc.clear_and_free_semaphores(self.sems)
            self.nc.all_engine_barrier()
        return self.ctx.__exit__(*e)


def load_residual(core):
    nc, d = core.nc, core.dram
    with Stage(core, "load") as s:
        loaded = s.sem("loaded")
        ones_set = s.sem("ones_set")
        with nc.Block() as block:

            @block.sync
            def _(sp):
                sp.dma_start(core.x[:, :, :], d["x"].rearrange("(t p) d -> p t d", p=P)).then_inc(loaded, 16)
                sp.dma_start(core.ident[:, :], d["c_ident"]).then_inc(loaded, 16)
                sp.dma_start(core.head_of_pair[:, :], d["c_head_of_pair"]).then_inc(loaded, 16)
                sp.wait_ge(loaded, 48)

            @block.vector
            def _(dve):
                dve.memset(core.ones[:, :], 1.0).then_inc(ones_set, 1)
                dve.wait_ge(ones_set, 1)


def store_residual(core):
    nc, d = core.nc, core.dram
    with Stage(core, "store") as s:
        stored = s.sem("stored")
        with nc.Block() as block:

            @block.sync
            def _(sp):
                sp.dma_start(d["out"].rearrange("(t p) d -> p t d", p=P), core.x[:, :, :]).then_inc(stored, 16)
                sp.wait_ge(stored, 16)


def normalise(core, src, rms=False, gamma=None, beta=None, eps=EPS):
    nc, d = core.nc, core.dram
    dst = core.xn
    with Stage(core, "norm") as s:
        stats = s.sb("stats", [P, NT, 6])
        mean_var = s.sb("mean_var", [P, NT, 2])
        square = s.sb("square", [P, NT])
        spread = s.sb("spread", [P, NT])
        deviation = s.sb("deviation", [P, NT])
        rstd = s.sb("rstd", [P, NT])
        scaled = s.sb("scaled", [P, NT, D]) if rms else dst
        affine = s.sb("affine", [P, 2, DC])
        turned = s.banks("turned", 4)
        loaded, stats_done, aggregated, square_done, spread_done = map(
            s.sem, ("loaded", "stats_done", "aggregated", "square_done", "spread_done"))
        deviation_done, rstd_done, scaled_done, turned_done, copied = map(
            s.sem, ("deviation_done", "rstd_done", "scaled_done", "turned_done", "copied"))
        with nc.Block() as block:

            @block.sync
            def _(sp):
                if gamma:
                    sp.dma_start(affine[:, 0, :], d[gamma].rearrange("(c p) -> p c", p=P),
                                 allow_slow_non_contiguous=True).then_inc(loaded, 16)
                    sp.wait_ge(loaded, 16)
                if beta:
                    sp.dma_start(affine[:, 1, :], d[beta].rearrange("(c p) -> p c", p=P),
                                 allow_slow_non_contiguous=True).then_inc(loaded, 16)
                    sp.wait_ge(loaded, 32)

            @block.vector
            def _(dve):
                for t in range(NT):
                    dve.bn_stats(stats[:, t, :], src[:, t, :]).then_inc(stats_done, 1)
                for t in range(NT):
                    dve.wait_ge(stats_done, t + 1)
                    dve.bn_aggr(mean_var[:, t, :], stats[:, t, :]).then_inc(aggregated, 1)
                dve.wait_ge(aggregated, NT)
                if rms:
                    dve.tensor_tensor(square[:, :], mean_var[:, :, 0], mean_var[:, :, 0], ALU.mult).then_inc(square_done, 1)
                    dve.wait_ge(square_done, 1)
                    dve.scalar_tensor_tensor(out=spread[:, :], in0=mean_var[:, :, 1], scalar=eps, in1=square[:, :],
                                             op0=ALU.add, op1=ALU.add).then_inc(spread_done, 1)
                else:
                    dve.tensor_scalar(spread[:, :], mean_var[:, :, 1], eps, None, ALU.add).then_inc(spread_done, 1)
                dve.wait_ge(deviation_done, 1)
                dve.reciprocal(rstd[:, :], deviation[:, :]).then_inc(rstd_done, 1)
                dve.wait_ge(rstd_done, 1)
                for t in range(NT):
                    if rms:
                        dve.tensor_scalar(scaled[:, t, :], src[:, t, :], rstd[:, t:t + 1], None,
                                          ALU.mult).then_inc(scaled_done, 1)
                    else:
                        dve.tensor_scalar(scaled[:, t, :], src[:, t, :], mean_var[:, t, 0:1], rstd[:, t:t + 1],
                                          ALU.subtract, ALU.mult).then_inc(scaled_done, 1)

            @block.tensor
            def _(pe):
                for g in range(NT // 4):
                    for c in range(DC):
                        pe.wait_ge(scaled_done, 4 * g + 4)
                        for k in range(4):
                            t = 4 * g + k
                            mm = pe.transpose(turned[g * DC + c][:, k * P:(k + 1) * P],
                                              scaled[:, t, c * P:(c + 1) * P], core.ident[:, :])
                        mm.then_inc(turned_done, 1)

            @block.scalar
            def _(act):
                act.wait_ge(spread_done, 1)
                act.activation(deviation[:, :], spread[:, :], ACT.Sqrt).then_inc(deviation_done, 1)
                if gamma:
                    act.wait_ge(loaded, 32 if beta else 16)
                for g in range(NT // 4):
                    for c in range(DC):
                        act.wait_ge(turned_done, g * DC + c + 1)
                        out = core.xnt[:, c, g * 4 * P:(g + 1) * 4 * P]
                        if gamma and beta:
                            act.activation(out, turned[g * DC + c][:, :], ACT.Identity, scale=affine[:, 0, c:c + 1],
                                           bias=affine[:, 1, c:c + 1]).then_inc(copied, 1)
                        elif gamma:
                            act.activation(out, turned[g * DC + c][:, :], ACT.Identity,
                                           scale=affine[:, 0, c:c + 1]).then_inc(copied, 1)
                        else:
                            act.activation(out, turned[g * DC + c][:, :], ACT.Copy).then_inc(copied, 1)
                act.wait_ge(copied, DC * NT // 4)


def project_and_add(core, heads, chunks, weight, bias=None):
    nc, d = core.nc, core.dram
    with Stage(core, "proj") as s:
        w = s.sb("w", [P, chunks, D])
        bias_rows = s.sb("bias_rows", [P, D])
        acc = s.banks("acc", 4)
        loaded, projected, biased, added = map(s.sem, ("loaded", "projected", "biased", "added"))
        n_loads = 2 if bias else 1
        with nc.Block() as block:

            @block.sync
            def _(sp):
                sp.dma_start(w[:, :, :], d[weight].rearrange("(c p) f -> p c f", p=P)).then_inc(loaded, 16)
                if bias:
                    sp.dma_start(bias_rows[:, :], d[bias].partition_broadcast(P)).then_inc(loaded, 16)
                sp.wait_ge(loaded, 16 * n_loads)

            @block.tensor
            def _(pe):
                pe.wait_ge(loaded, 16 * n_loads)
                for t in range(NT):
                    if t >= 4:
                        pe.wait_ge(added, t - 3)
                    for c in range(chunks):
                        mm = pe.matmul(acc[t % 4][:, 0:D], heads[:, c, S + t * P:S + (t + 1) * P], w[:, c, :],
                                       start=(c == 0), stop=(c == chunks - 1))
                    mm.then_inc(projected, 1)

            @block.vector
            def _(dve):
                if bias:
                    dve.wait_ge(loaded, 16 * n_loads)
                    dve.tensor_tensor(core.x[:, :, :], core.x[:, :, :],
                                      bias_rows[:, :].unsqueeze(1).broadcast_to([P, NT, D]), ALU.add).then_inc(biased, 1)
                    dve.wait_ge(biased, 1)
                for t in range(NT):
                    dve.wait_ge(projected, t + 1)
                    dve.tensor_tensor(core.x[:, t, :], core.x[:, t, :], acc[t % 4][:, 0:D], ALU.add).then_inc(added, 1)
                dve.wait_ge(added, NT)


def self_attention(core, heads, wq, wk, wv, bv=None, rope=False, causal=False):
    nc, d = core.nc, core.dram
    halves = 2 if rope else 1
    with Stage(core, "self") as s:
        w_q = s.sb("w_q", [P, DC, halves * D])
        w_k = s.sb("w_k", [P, DC, halves * D]) if wk else None
        w_v = s.sb("w_v", [P, DC, D])
        v_bias = s.sb("v_bias", [P, D])
        wave = s.sb("wave", [P, 2, S])
        later = s.sb("later", [P, S])
        quarter = s.sb("quarter", [P, 2])
        tile_t = s.sb("tile_t", [P, DC, P])
        qk = s.sb("qk", [P, 2, DC, P])
        qk_cos = s.sb("qk_cos", [P, 2 * DC, 2, S])
        qk_sin = s.sb("qk_sin", [P, 2 * DC, 2, S])
        q_pair = s.sb("q_pair", [32, UNITS, 2, 2, S])
        k_pair = s.sb("k_pair", [32, UNITS, P])
        v = s.sb("v", [S, 2, D])
        shifted = s.sb("shifted", [P, 2, UNITS, S])
        probs = s.sb("probs", [P, 2, UNITS + 1, S])
        top = s.sb("top", [P, 2, UNITS])
        total = s.sb("total", [P, 2, UNITS])
        share = s.sb("share", [P, 2, UNITS])
        probs_t = s.sb("probs_t", [S, 2, UNITS, P])
        mixed = s.sb("mixed", [P, 2, UNITS, DH])
        qk_ps, swap_ps, v_ps, mixed_ps = s.banks("qk_ps", 4)
        score_ps = s.banks("score_ps", 2)
        turn_ps = s.banks("turn_ps", 2)
        (loaded, quarter_set, tile_copied, q_projected, v_projected, qk_copied, waved, split, v_copied, scored,
         masked, top_found, shift_done, exp_done, sum_done, share_done, turned, turn_copied, weighed, mixed_done,
         mixed_turned, heads_out) = map(s.sem, (
             "loaded", "quarter_set", "tile_copied", "q_projected", "v_projected", "qk_copied", "waved", "split",
             "v_copied", "scored", "masked", "top_found", "shift_done", "exp_done", "sum_done", "share_done",
             "turned", "turn_copied", "weighed", "mixed_done", "mixed_turned", "heads_out"))
        n_loads = 2 + bool(wk) + bool(bv) + bool(rope) + bool(causal)
        with nc.Block() as block:

            @block.sync
            def _(sp):
                sp.dma_start(w_q[:, :, :], d[wq].rearrange("(c p) f -> p c f", p=P)).then_inc(loaded, 16)
                sp.dma_start(w_v[:, :, :], d[wv].rearrange("(c p) f -> p c f", p=P)).then_inc(loaded, 16)
                if wk:
                    sp.dma_start(w_k[:, :, :], d[wk].rearrange("(c p) f -> p c f", p=P)).then_inc(loaded, 16)
                if bv:
                    sp.dma_start(v_bias[:, :], d[bv].partition_broadcast(P)).then_inc(loaded, 16)
                if rope:
                    sp.dma_start(wave[:, :, :], d["c_wave"]).then_inc(loaded, 16)
                if causal:
                    sp.dma_start(later[:, :], d["c_later"]).then_inc(loaded, 16)
                sp.wait_ge(loaded, 16 * n_loads)

            @block.tensor
            def _(pe):
                pe.wait_ge(loaded, 16 * n_loads)
                with pe.Fori(0, NT) as i:
                    pe.wait_ge(quarter_set, 2)
                    pe.wait_ge(tile_copied, i + 1)
                    for c2 in range(DC):
                        for c in range(DC):
                            mm = pe.matmul(qk_ps[:, c2 * P:(c2 + 1) * P], w_q[:, c, c2 * P:(c2 + 1) * P],
                                           tile_t[:, c, :], start=(c == 0), stop=(c == DC - 1))
                        if wk:
                            for c in range(DC):
                                mm = pe.matmul(qk_ps[:, (DC + c2) * P:(DC + c2 + 1) * P],
                                               w_k[:, c, c2 * P:(c2 + 1) * P],
                                               tile_t[:, c, :], start=(c == 0), stop=(c == DC - 1))
                        if rope:
                            for n, w in enumerate((w_q, w_k)):
                                for c in range(DC):
                                    mm = pe.matmul(swap_ps[:, (n * DC + c2) * P:(n * DC + c2 + 1) * P],
                                                   w[:, c, D + c2 * P:D + (c2 + 1) * P],
                                                   tile_t[:, c, :], start=(c == 0), stop=(c == DC - 1))
                    mm.then_inc(q_projected, 1)
                    for j in range(2):
                        for c in range(DC):
                            mm = pe.matmul(v_ps[0:S, j * D:(j + 1) * D], tile_t[:, c, j * S:(j + 1) * S],
                                           w_v[:, c, :], start=(c == 0), stop=(c == DC - 1))
                    mm.then_inc(v_projected, 1)
                    pe.wait_ge(split, i + 1)
                    for j in range(2):
                        for u in range(UNITS):
                            mm = pe.matmul(score_ps[j][:, u * S:(u + 1) * S], q_pair[:, u, j, :, :],
                                           k_pair[:, u, j * S:(j + 1) * S], start=True, stop=True)
                        mm.then_inc(scored, 1)
                    for j in range(2):
                        pe.wait_ge(exp_done, 2 * i + j + 1)
                        if j:
                            pe.wait_ge(turn_copied, 2 * i + 1)
                        for u in range(UNITS):
                            mm = pe.transpose(turn_ps[u // 4][:, (u % 4) * P:(u % 4 + 1) * P],
                                              probs[:, j, u:u + 2, :], core.ident[:, :])
                        mm.then_inc(turned, 1)
                    for j in range(2):
                        pe.wait_ge(turn_copied, 2 * i + j + 1)
                        pe.wait_ge(v_copied, i + 1)
                        for u in range(UNITS):
                            mm = pe.matmul(mixed_ps[:, j * D + u * 32:j * D + (u + 1) * 32], probs_t[:, j, u, :],
                                           v[:, j, u * 32:(u + 1) * 32], start=True, stop=True)
                        mm.then_inc(weighed, 1)
                    for j in range(2):
                        pe.wait_ge(mixed_done, 4 * i + 2 * j + 2)
                        mm = pe.transpose(qk_ps[:, j * P:(j + 1) * P], mixed[:, j, :, :], core.ident[:, :])
                    mm.then_inc(mixed_turned, 1)

            @block.scalar
            def _(act):
                with act.Fori(0, NT) as i:
                    act.wait_ge(heads_out, i + 1)
                    act.activation(tile_t[:, :, :], core.xnt[:, :, bass.ds(i * P, P)], ACT.Copy).then_inc(tile_copied, 1)
                    act.wait_ge(q_projected, i + 1)
                    act.activation(qk[:, 0, :, :], qk_ps[:, 0:DC * P], ACT.Copy).then_inc(qk_copied, 1)
                    act.wait_ge(tile_copied, i + 1)
                    act.activation(qk[:, 1, :, :], qk_ps[:, DC * P:2 * DC * P] if wk else tile_t[:, :, :],
                                   ACT.Copy).then_inc(qk_copied, 1)
                    act.wait_ge(v_projected, i + 1)
                    if not bv:
                        act.activation(v[:, :, :], v_ps[0:S, :], ACT.Copy).then_inc(v_copied, 1)
                    for j in range(2):
                        act.wait_ge(shift_done, 2 * i + j + 1)
                        act.activation(probs[:, j, 0:UNITS, :], shifted[:, j, :, :], ACT.Exp).then_inc(exp_done, 1)
                    for j in range(2):
                        act.wait_ge(turned, 2 * i + j + 1)
                        act.activation(probs_t[:, j, 0:4, :], turn_ps[0][0:S, :], ACT.Copy)
                        act.activation(probs_t[:, j, 4:8, :], turn_ps[1][0:S, :], ACT.Copy).then_inc(turn_copied, 1)

            @block.vector
            def _(dve):
                dve.tensor_scalar(quarter[:, :], core.head_of_pair[:, :], DH ** -0.5, None, ALU.mult).then_inc(quarter_set, 1)
                dve.memset(probs[:, :, UNITS, :], 0.0).then_inc(quarter_set, 1)
                dve.wait_ge(quarter_set, 2)
                dve.wait_ge(loaded, 16 * n_loads)
                dve.sem_inc(heads_out, 1)
                with dve.Fori(0, NT) as i:
                    dve.wait_ge(qk_copied, 2 * i + 2)
                    source = qk[:, :, :, :].rearrange("p n c (j s) -> p (n c) j s", j=2)
                    if rope:
                        swap = swap_ps[:, :].rearrange("p (n j s) -> p n j s", n=2 * DC, j=2)
                        for n in range(2 * DC):
                            dve.tensor_tensor(qk_cos[:, n], source[:, n],
                                              wave[:, 0:1, :].broadcast_to([P, 2, S]), ALU.mult)
                            rot = dve.tensor_tensor(qk_sin[:, n], swap[:, n],
                                                    wave[:, 1:2, :].broadcast_to([P, 2, S]), ALU.mult)
                        rot.then_inc(waved, 1)
                        dve.wait_ge(waved, 2 * i + 1)
                        dve.tensor_tensor(qk_cos[:, :, :, :], qk_cos[:, :, :, :], qk_sin[:, :, :, :], ALU.add).then_inc(waved, 1)
                        dve.wait_ge(waved, 2 * i + 2)
                        source = qk_cos[:, :, :, :]
                    for a in range(4):
                        rows = slice(32 * a, 32 * a + 32)
                        for c in range(DC):
                            u = 4 * c + a
                            for h2 in range(2):
                                dve.tensor_scalar(q_pair[:, u, :, h2, :], source[rows, c, :, :],
                                                  quarter[rows, h2:h2 + 1], None, ALU.mult)
                            cut = dve.tensor_copy(k_pair[:, u, :].rearrange("p (j s) -> p j s", j=2),
                                                  source[rows, DC + c, :, :])
                    cut.then_inc(split, 1)
                    if bv:
                        dve.wait_ge(v_projected, i + 1)
                        dve.tensor_tensor(v[:, :, :], v_ps[0:S, :].rearrange("p (j f) -> p j f", j=2),
                                          v_bias[0:S, :].unsqueeze(1).broadcast_to([S, 2, D]), ALU.add).then_inc(v_copied, 1)
                    for j in range(2):
                        dve.wait_ge(scored, 2 * i + j + 1)
                        score = score_ps[j][:, :].rearrange("p (u s) -> p u s", u=UNITS)
                        if causal:
                            dve.tensor_tensor(shifted[:, j], score,
                                              later[:, :].unsqueeze(1).broadcast_to([P, UNITS, S]), ALU.add).then_inc(masked, 1)
                            dve.wait_ge(masked, 2 * i + j + 1)
                            score = shifted[:, j]
                        dve.tensor_reduce(top[:, j, :], score, AX.X, ALU.max).then_inc(top_found, 1)
                        dve.wait_ge(top_found, 2 * i + j + 1)
                        dve.tensor_tensor(shifted[:, j], score, top[:, j, :].unsqueeze(2).broadcast_to([P, UNITS, S]),
                                          ALU.subtract).then_inc(shift_done, 1)
                    for j in range(2):
                        dve.wait_ge(exp_done, 2 * i + j + 1)
                        dve.tensor_reduce(total[:, j, :], probs[:, j, 0:UNITS, :], AX.X, ALU.add).then_inc(sum_done, 1)
                        dve.wait_ge(sum_done, 2 * i + j + 1)
                        dve.reciprocal(share[:, j, :], total[:, j, :]).then_inc(share_done, 1)
                    for j in range(2):
                        dve.wait_ge(weighed, 2 * i + 2)
                        dve.wait_ge(share_done, 2 * i + j + 1)
                        out = mixed_ps[:, j * D:(j + 1) * D].rearrange("p (u h f) -> p u h f", u=UNITS, h=2)
                        for h2 in range(2):
                            rows = slice(S * h2, S * h2 + S)
                            dve.tensor_tensor(mixed[rows, j, :, :], out[rows, :, h2, :],
                                              share[rows, j, :].unsqueeze(2).broadcast_to([S, UNITS, DH]),
                                              ALU.mult).then_inc(mixed_done, 1)
                    dve.wait_ge(mixed_turned, i + 1)
                    dve.tensor_copy(heads[:, 0:2, bass.ds(i * P + S, P)].rearrange("p h (j s) -> p h j s", j=2),
                                    qk_ps[:, 0:2 * P].rearrange("p (j h s) -> p h j s", j=2, h=2)).then_inc(heads_out, 1)
                dve.wait_ge(heads_out, NT + 1)


def cross_attention(core, heads, wq, wk, wv, bq=None, bk=None, bv=None, mask=None, mask_cols=None, mask_values=False,
                    scale=None, context_gamma=None, context_beta=None):
    nc, d = core.nc, core.dram
    shared = context_gamma is not None
    kd = 64 if shared else 32
    extra = 2 if mask else 1
    low_at, cross_at, top_at = (64, 0, 64) if shared else (0, 32, 96)
    dv = 64 if shared else 32
    dm = 64 if shared else DH
    nk = 1 if shared else UNITS
    n_q = H * 64 if shared else D
    n_kc = 1 if shared else DC
    nv = dv if shared else D
    out_chunks = UNITS * dm // P
    key_cols = cols(KEYS, BANK)
    key_groups = cols(KT, 4)
    v_groups = cols(KT, BANK // nv)
    NKC, NKG, NV = len(key_cols), len(key_groups), len(v_groups)
    NK = n_kc * NKC
    NC = DC * NKG if shared else 0
    RING, V_RING = 2, 2
    NCP = DC * NKG
    with Stage(core, "cross") as s:
        w_q = s.sb("w_q", [P, DC, n_q])
        w_kv = s.sb("w_kv", [P, DC, n_kc * (kd if shared else P) + nv])
        nkv = n_kc * (kd if shared else P)
        w_high = s.sb("w_high", [P, DC, nkv + nv], F16)
        w_low = s.sb("w_low", [P, DC, nkv + nv], F16)
        bias_cols = s.sb("bias_cols", [P, 2, DC])
        v_bias = s.sb("v_bias", [P, D])
        scale_col = s.sb("scale_col", [P, 1])
        q_scale = s.sb("q_scale", [P, 2])
        ident_down = s.sb("ident_down", [P, P])
        ctx = s.sb("ctx", [P, DC, KEYS])
        ctx_high = [s.sb(f"ctx_high{i}", [P, DC, KEYS], F16) for i in range(2)]
        ctx_low = [s.sb(f"ctx_low{i}", [P, DC, KEYS], F16) for i in range(2)]
        k_piece = core.xn[:, 0:NT // 2, :].rearrange("p (n a) f -> p n (a f)", a=2)
        v_piece = core.xn[:, NT // 2:, :].rearrange("p (n a) f -> p n (a f)", a=2)
        if shared:
            q_rows = s.sb("q_rows", [kd, UNITS, 2, S])
            k_rows = [s.sb(f"k_rows{i}", [2 * kd, 1, KEYS], F16) for i in range(2)]
            k_cross = [s.sb(f"k_cross{i}", [kd + 1, 1, KEYS], F16) for i in range(2)]
            q_parts = [s.sb(f"q_parts{i}", [2 * kd, UNITS, 2, S], F16) for i in range(2)]
            q_cross = [s.sb(f"q_cross{i}", [kd + 1, UNITS, 2, S], F16) for i in range(2)]
        else:
            k_rows = [s.sb(f"k_rows{i}", [3 * kd + extra, UNITS, KEYS], F16) for i in range(2)]
            q_parts = [s.sb(f"q_parts{i}", [3 * kd + extra, UNITS, 2, S], F16) for i in range(2)]
            k_cross, q_cross = k_rows, q_parts
            q_both = s.sb("q_both", [P, DC, 2, S])
            q_high = s.sb("q_high", [P, DC, 2, S], F16)
            q_low = s.sb("q_low", [P, DC, 2, S], F16)
            k_high = s.sb("k_high", [P, DC, KEYS], F16)
            k_low = s.sb("k_low", [P, DC, KEYS], F16)
        v_parts = [s.sb(f"v_parts{i}", [P, KT, nk, 2, dv + 1], F16) for i in range(2)]
        probs = s.sb("probs", [P, KT, P])
        probs_high = s.sb("probs_high", [P, KT, P], F16)
        probs_low = s.sb("probs_low", [P, KT, P], F16)
        top_parts = s.sb("top_parts", [P, 2, 4])
        top_cols = s.sb("top_cols", [P, 2, 2])
        share = s.sb("share", [P, UNITS])
        mixed = s.sb("mixed", [P, 2, UNITS, dm])
        if mask:
            mask_int = s.sb("mask_int", [P, KEYS], I32)
            keep = s.sb("keep", [P, KEYS], F16)
            mask_row = s.sb("mask_row", [1, KEYS], F16)
            keep_int = s.sb("keep_int", [P, KT], I32)
            keep_cols = s.sb("keep_cols", [P, 2, KT])
        if shared:
            ctx_raw = s.sb("ctx_raw", [P, KT, D])
            stats = s.sb("stats", [P, KT, 6])
            mean_var = s.sb("mean_var", [P, KT, 2])
            spread = s.sb("spread", [P, KT])
            deviation = s.sb("deviation", [P, KT])
            rstd = s.sb("rstd", [P, KT])
            affine = s.sb("affine", [P, 2, DC])
        score_ps = s.banks("score_ps", RING)
        weight_ps = s.banks("weight_ps", RING)
        fill_ps = s.banks("fill_ps", RING)
        mixed_ps = s.banks("mixed_ps", 1)[0]
        side_ps = s.banks("side_ps", 1)[0]
        (loaded, ctx_in, rows_set, w_scaled, w_split, mask_in, kept, row_ready, q_scaled, q_projected, q_cut,
         q_split, q_placed, k_projected, k_copied, k_split, k_placed, k_placed_2, v_projected, v_copied,
         v_masked, v_high_done, v_split, scored, part_found, top_found, top_turned, top_placed, weighed,
         exp_done, low_pool, low_dve, mixed_done, share_done, mixed_out, mixed_turned, heads_out, ctx_high_done,
         ctx_split, raw_in, stats_done, aggregated, spread_set, spread_done, deviation_done, rstd_done, normed,
         ctx_turned, ctx_placed) = map(s.sem, (
             "loaded", "ctx_in", "rows_set", "w_scaled", "w_split", "mask_in", "kept", "row_ready",
             "q_scaled", "q_projected", "q_cut", "q_split", "q_placed", "k_projected", "k_copied",
             "k_split", "k_placed", "k_placed_2", "v_projected", "v_copied", "v_masked", "v_high_done",
             "v_split", "scored", "part_found", "top_found", "top_turned", "top_placed", "weighed",
             "exp_done", "low_pool", "low_dve", "mixed_done", "share_done", "mixed_out", "mixed_turned",
             "heads_out", "ctx_high_done", "ctx_split", "raw_in", "stats_done", "aggregated", "spread_set",
             "spread_done", "deviation_done", "rstd_done", "normed", "ctx_turned", "ctx_placed"))
        n_loads = 4 + 2 * bool(bq) + bool(bv) + bool(scale) + 2 * shared
        q_cuts = 2 if shared else 2 * DC
        q_parts_made = 3 if shared else 2
        k_parts_made = 3 if shared else (3 if mask else 2)
        n_placed = 16 * (12 + bool(mask))
        n_placed_2 = 16 * 12
        n_q_placed = 16 * 12
        n_sets = 9 if shared else 8
        low_groups = {"pool": () if mask else ((0, 2) if shared else (2,))}
        low_groups["dve"] = tuple(g for g in range(NKG) if g not in low_groups["pool"])
        first_late = 0 if shared else 1
        context_units = [[], [], [0], [1], [2], [3], [4, 5], [6, 7]]

        project_fills = [("q", 0)] + [("k", n) for n in range(NK)] + [("v", n) for n in range(NV)]
        context_fills = [("ctx", n) for n in range(NC)]
        fills = project_fills + [None] * (2 * UNITS - len(project_fills) - NC) + context_fills

        def fill_done(eng, fill, nb):
            kind, n = fill
            if kind == "k":
                eng.wait_ge(k_copied, NK * nb + n + 1)
            elif kind == "v":
                eng.wait_ge(v_copied, NV * nb + n + 1)
            elif kind == "q":
                eng.wait_ge(q_cut, q_cuts * (nb + 1))
            else:
                eng.wait_ge(ctx_placed, NC * nb + n + 1)

        def low_part(eng, done, b, u, g):
            t0, k = key_groups[g]
            m = P if k > 1 else TAIL
            eng.wait_ge(exp_done, RING + NKG * (UNITS * b + u) + g + 1)
            return eng.tensor_tensor(probs_low[0:m, t0:t0 + k, :], probs[0:m, t0:t0 + k, :],
                                     probs_high[0:m, t0:t0 + k, :], ALU.subtract).then_inc(done, 1)

        def value_rows(n):
            t0, k = v_groups[n]
            full = [t for t in range(t0, t0 + k) if keys_in(t) == P]
            parts = [(P, t0, t0 + len(full))] if full else []
            return parts + ([(TAIL, KT - 1, KT)] if len(full) < k else [])

        def late_values(u, b, q, project):
            lots = []
            for slot in (2 * u - 1, 2 * u):
                f = fills[slot]
                own = slot < 0
                lots.append([(f[1], b, q) if own else (f[1], b + 1, 1 - q)] if f and f[0] == "v" and (own or project)
                            else [])
            return lots

        def pipeline(eng, body):
            with eng.Fori(0, B // 2 - 1) as i:
                body(i, 2 * i, 0, True, True)
                body(i, 2 * i + 1, 1, True, True)
            body(None, B - 2, 0, True, False)
            body(None, B - 1, 1, False, False)

        with nc.Block() as block:

            @block.sync
            def _(sp):
                if context_gamma:
                    sp.dma_start(affine[:, 0, :], d[context_gamma].rearrange("(c p) -> p c", p=P),
                                 allow_slow_non_contiguous=True).then_inc(loaded, 16)
                    sp.dma_start(affine[:, 1, :], d[context_beta].rearrange("(c p) -> p c", p=P),
                                 allow_slow_non_contiguous=True).then_inc(loaded, 16)
                sp.dma_start(w_q[:, :, :], d[wq].rearrange("(c p) f -> p c f", p=P)).then_inc(loaded, 16)
                sp.dma_start(w_kv[:, :, 0:nkv], d[wk].rearrange("(c p) f -> p c f", p=P)).then_inc(loaded, 16)
                sp.dma_start(w_kv[:, :, nkv:], d[wv].rearrange("(c p) f -> p c f", p=P)).then_inc(loaded, 16)
                sp.dma_start(ident_down[:, :], d["c_ident_down"]).then_inc(loaded, 16)
                if bq:
                    for n, name in enumerate((bq, bk)):
                        sp.dma_start(bias_cols[:, n, :], d[name].rearrange("(c p) -> p c", p=P),
                                     allow_slow_non_contiguous=True).then_inc(loaded, 16)
                if bv:
                    sp.dma_start(v_bias[:, :], d[bv].partition_broadcast(P)).then_inc(loaded, 16)
                if scale:
                    sp.dma_start(scale_col[:, :], d[scale].partition_broadcast(P)).then_inc(loaded, 16)

                def of_batch(a, nb):
                    if isinstance(nb, int):
                        return a[nb:nb + 1]
                    i, pairs, q = nb
                    rest = " ".join("xyz"[:len(a.shape) - 1])
                    pair = a.rearrange(f"(i two) {rest} -> two i {rest}", two=2)
                    return pair[q, pairs:][bass.ds(i, 1)]

                def load_context(nb):
                    if shared:
                        rows = of_batch(d["ctx"], nb).rearrange("b n f -> (b n) f")
                        sp.dma_start(ctx_raw[:, 0:KT - 1, :],
                                     rows[0:(KT - 1) * P, :].rearrange("(t p) f -> p t f", p=P)).then_inc(raw_in, 16)
                        sp.dma_start(ctx_raw[0:TAIL, KT - 1, :], rows[(KT - 1) * P:KEYS, :]).then_inc(raw_in, 16)
                    else:
                        sp.dma_start(ctx[:, :, :], of_batch(d["ctx_t"], nb).rearrange(
                            "b (c p) n -> p (b c) n", p=P)).then_inc(ctx_in, 16)

                def load_mask(nb):
                    sp.dma_start(mask_int[:, :], of_batch(d[mask], nb).rearrange(
                        "b n -> (b n)").partition_broadcast(P)).then_inc(mask_in, 16)
                    sp.dma_start(keep_int[:, :], of_batch(d[mask_cols], nb).rearrange(
                        "b p t -> p (b t)")).then_inc(mask_in, 16)

                def place_queries(nb, q):
                    sp.wait_ge(q_split, q_parts_made * (nb + 1))
                    for a in range(4):
                        for at, part in ((0, q_high), (32, q_low), (64, q_high)):
                            sp.dma_start(
                                q_parts[q][at:at + 32, :, :, :].rearrange("p (c a) h s -> p c a h s", a=4)[:, :, a],
                                part[32 * a:32 * a + 32, :, :, :]).then_inc(q_placed, 16)

                def place_keys(nb, q):
                    for c, placed in enumerate((k_placed, k_placed_2)):
                        sp.wait_ge(k_split, k_parts_made * (NK * nb + NKC * (c + 1)))
                        for a in range(4):
                            for at, part in ((0, k_low), (32, k_high), (64, k_high)):
                                sp.dma_start(k_rows[q][at:at + 32, 4 * c + a, :],
                                             part[32 * a:32 * a + 32, c, :]).then_inc(placed, 16)
                        if mask and c == 0:
                            sp.wait_ge(row_ready, nb + 1)
                            sp.dma_start(k_rows[q][top_at:top_at + 1, :, :], mask_row[:, :].unsqueeze(1).broadcast_to(
                                [1, UNITS, KEYS])).then_inc(placed, 16)

                load_context(0)
                if mask:
                    load_mask(0)
                if shared:
                    sp.wait_ge(ctx_turned, NC)
                else:
                    sp.wait_ge(ctx_split, NCP)
                load_context(1)
                if not shared:
                    sp.wait_ge(rows_set, n_sets)
                    place_queries(0, 0)
                    place_keys(0, 0)
                if mask:
                    load_mask(1)

                def body(i, b, q, project, prepare):
                    if prepare:
                        if shared:
                            sp.wait_ge(ctx_turned, NC * (b + 2))
                        else:
                            sp.wait_ge(ctx_split, NCP * (b + 2))
                        load_context((i, 1, q))
                        if mask:
                            sp.wait_ge(kept, 2 * (b + 2))
                            load_mask((i, 1, q))
                    if project and not shared:
                        place_queries(b + 1, 1 - q)
                        place_keys(b + 1, 1 - q)

                pipeline(sp, body)
                if shared:
                    sp.wait_ge(raw_in, 32 * B)
                else:
                    sp.wait_ge(ctx_in, 16 * B)
                    sp.wait_ge(q_placed, n_q_placed * B)
                    sp.wait_ge(k_placed, n_placed * B)
                    sp.wait_ge(k_placed_2, n_placed_2 * B)
                if mask:
                    sp.wait_ge(mask_in, 32 * B)

            @block.gpsimd
            def _(pool):
                def context_low(n, nb, q):
                    g, c = divmod(n, DC)
                    a, w = key_cols[g]
                    pool.wait_ge(ctx_high_done, NCP * nb + n + 1)
                    pool.tensor_tensor(ctx_low[q][:, c, a:a + w], ctx[:, c, a:a + w], ctx_high[q][:, c, a:a + w],
                                       ALU.subtract).then_inc(ctx_split, 1)

                def split_keys(n, nb, q):
                    c, i = divmod(n, NKC)
                    a, w = key_cols[i]
                    at = k_parts_made * (NK * nb + n)
                    pool.wait_ge(k_copied, NK * nb + n + 1)
                    piece = k_piece[:, n % 2, 0:w]
                    if mask:
                        pool.tensor_tensor(piece, piece, keep[:, a:a + w], ALU.mult).then_inc(k_split, 1)
                        pool.wait_ge(k_split, at + 1)
                    pool.tensor_tensor(k_high[:, c, a:a + w], piece, core.ones[:, 0:1].broadcast_to([P, w]),
                                       ALU.mult).then_inc(k_split, 1)
                    pool.wait_ge(k_split, at + k_parts_made - 1)
                    pool.tensor_tensor(k_low[:, c, a:a + w], piece, k_high[:, c, a:a + w],
                                       ALU.subtract).then_inc(k_split, 1)

                def values_low(n, nb, q):
                    t0, k = v_groups[n]
                    pool.wait_ge(v_high_done, NV * nb + n + 1)
                    if mask_values:
                        m = keys_in(t0)
                        piece = v_piece[0:m, n % V_RING, 0:k * nv].rearrange("p (t f) -> p t f", f=nv)
                        pool.tensor_tensor(piece, piece, keep_cols[0:m, q, t0:t0 + k].unsqueeze(2).broadcast_to(
                            [m, k, nv]), ALU.mult).then_inc(v_masked, 1)
                        pool.wait_ge(v_masked, NV * nb + n + 1)
                    for m, t1, t2 in value_rows(n):
                        piece = v_piece[0:m, n % V_RING, (t1 - t0) * nv:(t2 - t0) * nv].rearrange(
                            "p (t u f) -> p t u f", u=nk, f=dv)
                        done = pool.tensor_tensor(v_parts[q][0:m, t1:t2, :, 1, 0:dv], piece,
                                                  v_parts[q][0:m, t1:t2, :, 0, 0:dv], ALU.subtract)
                    done.then_inc(v_split, 1)

                for n in range(NCP):
                    context_low(n, 0, 0)
                if mask:
                    pool.wait_ge(kept, 2)
                if not shared:
                    for n in range(NK):
                        split_keys(n, 0, 0)
                for n in range(NV - first_late):
                    values_low(n, 0, 0)
                for n in range(NCP):
                    context_low(n, 1, 1)

                def body(i, b, q, project, prepare):
                    def do_fill(slot):
                        f = fills[slot]
                        if f and f[0] == "k" and project and not shared:
                            split_keys(f[1], b + 1, 1 - q)
                        if f and f[0] == "ctx" and prepare:
                            context_low(f[1], b + 2, q)

                    if project and not shared:
                        pool.wait_ge(k_placed, n_placed * (b + 1))
                        pool.wait_ge(k_placed_2, n_placed_2 * (b + 1))
                        if mask:
                            pool.wait_ge(kept, 2 * (b + 2))
                    for u in range(UNITS):
                        late = late_values(u, b, q, project)
                        if shared:
                            do_fill(2 * u)
                        elif u:
                            do_fill(2 * u - 1)
                        for g in low_groups["pool"]:
                            low_part(pool, low_pool, b, u, g)
                        for piece in late[0]:
                            values_low(*piece)
                        do_fill(2 * u + 1 if shared else 2 * u)
                        if prepare and not shared:
                            for n in context_units[u]:
                                context_low(n, b + 2, q)
                        for piece in late[1]:
                            values_low(*piece)

                pipeline(pool, body)

            @block.tensor
            def _(pe):
                pe.wait_ge(loaded, 16 * n_loads)
                pe.wait_ge(rows_set, n_sets)
                pe.wait_ge(w_split, 2)

                def scores(b, u, q, n):
                    a, w = key_cols[n]
                    piece = NKC * (UNITS * b + u) + n
                    pe.wait_ge(part_found, piece + 1)
                    rows = slice(0, kd) if shared else slice(64, 96 + extra - 1)
                    pe.matmul(score_ps[n % 2][:, 0:w], q_parts[q][rows, u, :, :], k_rows[q][rows, u % nk, a:a + w],
                              start=True, stop=True).then_inc(scored, 1)

                def place_top(b, u):
                    pe.wait_ge(top_found, UNITS * b + u + 1)
                    pe.matmul(side_ps[top_at:top_at + extra, 0:P], top_cols[:, u % 2, 2 - extra:2], ident_down[:, :],
                              start=True, stop=True, tile_position=(0, top_at)).then_inc(top_turned, 1)

                def weights(b, u, q, g):
                    t0, k = key_groups[g]
                    piece = NKG * (UNITS * b + u) + g
                    pe.wait_ge(exp_done, piece + 1)
                    for t in range(t0, t0 + k):
                        m = keys_in(t)
                        out = weight_ps[g % 2][0:m, (t - t0) * P:(t - t0 + 1) * P]
                        keys = slice(t * P, t * P + m)
                        mm = pe.matmul(out, k_rows[q][:, u % nk, keys], q_parts[q][:, u, :, :], start=True,
                                       stop=not shared)
                        if shared:
                            mm = pe.matmul(out, k_cross[q][:, 0, keys], q_cross[q][:, u, :, :], start=False, stop=True)
                    mm.then_inc(weighed, 1)

                def weigh(b, u, q):
                    for g, (t0, k) in enumerate(key_groups):
                        pe.wait_ge(exp_done, RING + NKG * (UNITS * b + u) + g + 1)
                        for t in range(t0, t0 + k):
                            m = keys_in(t)
                            pe.matmul(mixed_ps[:, 0:2 * (dv + 1)], probs_high[0:m, t, :],
                                      v_parts[q][0:m, t, u % nk, :, :], start=(t == 0), stop=False)
                        for who, done in (("pool", low_pool), ("dve", low_dve)):
                            if g in low_groups[who]:
                                n = len(low_groups[who])
                                pe.wait_ge(done, n * (UNITS * b + u) + low_groups[who].index(g) + 1)
                        for t in range(t0, t0 + k):
                            m = keys_in(t)
                            mm = pe.matmul(mixed_ps[:, 0:dv + 1], probs_low[0:m, t, :],
                                           v_parts[q][0:m, t, u % nk, 0, :], start=False, stop=(t == KT - 1))
                    mm.then_inc(mixed_done, 1)

                def queries(nb, bank):
                    for c2 in range(n_q // P):
                        for c in range(DC):
                            mm = pe.matmul(bank[:, c2 * S:(c2 + 1) * S], w_q[:, c, c2 * P:(c2 + 1) * P],
                                           core.xnt[:, c, bass.ds(nb * S, S)], start=(c == 0), stop=(c == DC - 1))
                    mm.then_inc(q_projected, 1)

                def turn_result():
                    w = UNITS // out_chunks
                    for c in range(out_chunks):
                        for part in range(2):
                            mm = pe.matmul(side_ps[:, c * P:(c + 1) * P], mixed[:, part, c * w:(c + 1) * w, :],
                                           core.ident[:, :], start=(part == 0), stop=(part == 1))
                    mm.then_inc(mixed_turned, 1)

                def fill(kind, n, nb, q, bank):
                    if kind == "q":
                        queries(nb, bank)
                    elif kind == "k":
                        c2, i = divmod(n, NKC)
                        a, w = key_cols[i]
                        m = kd if shared else P
                        pairs = [(w_high, ctx_high), (w_high, ctx_low), (w_low, ctx_high)]
                        for c in range(DC):
                            for j, (wp, cp) in enumerate(pairs):
                                mm = pe.matmul(bank[0:m, 0:w], wp[:, c, c2 * P:c2 * P + m], cp[q][:, c, a:a + w],
                                               start=(c == 0 and j == 0), stop=(c == DC - 1 and j == 2))
                        mm.then_inc(k_projected, 1)
                    elif kind == "v":
                        t0, k = v_groups[n]
                        pairs = [(ctx_high, w_high), (ctx_high, w_low), (ctx_low, w_high)]
                        for t in range(t0, t0 + k):
                            m = keys_in(t)
                            for c in range(DC):
                                for j, (cp, wp) in enumerate(pairs):
                                    mm = pe.matmul(bank[0:m, (t - t0) * nv:(t - t0 + 1) * nv],
                                                   cp[q][:, c, t * P:t * P + m], wp[:, c, nkv:],
                                                   start=(c == 0 and j == 0), stop=(c == DC - 1 and j == 2))
                        mm.then_inc(v_projected, 1)
                    else:
                        g, c = divmod(n, DC)
                        t0, k = key_groups[g]
                        for t in range(t0, t0 + k):
                            m = keys_in(t)
                            mm = pe.transpose(bank[:, (t - t0) * P:(t - t0) * P + m], ctx_raw[0:m, t, c * P:(c + 1) * P],
                                              core.ident[0:m, 0:m])
                        mm.then_inc(ctx_turned, 1)

                def straight(todo, nb, q):
                    for n, (kind, i) in enumerate(todo):
                        if n >= RING:
                            fill_done(pe, todo[n - RING], nb)
                        fill(kind, i, nb, q, fill_ps[n % 2])
                    for f in todo[-RING:]:
                        fill_done(pe, f, nb)

                if shared:
                    pe.wait_ge(normed, KT)
                    straight(context_fills, 0, 0)
                pe.wait_ge(ctx_split, NCP)
                straight(project_fills, 0, 0)
                if not shared:
                    pe.wait_ge(q_placed, n_q_placed)
                    pe.wait_ge(k_placed, n_placed)
                    pe.wait_ge(k_placed_2, n_placed_2)
                else:
                    pe.wait_ge(q_split, q_parts_made)
                    pe.wait_ge(k_split, k_parts_made * NK)
                for u in range(2):
                    for n in range(NKC):
                        scores(0, u, 0, n)
                place_top(0, 0)
                if shared:
                    pe.wait_ge(normed, 2 * KT)
                    straight(context_fills, 1, 1)

                def body(i, b, q, project, prepare):
                    if project:
                        pe.wait_ge(ctx_split, NCP * (b + 2))

                    def do_fill(slot):
                        f = fills[slot]
                        if f is None or not (project if f[0] != "ctx" else prepare):
                            return
                        if f == ("ctx", 0):
                            pe.wait_ge(normed, KT * (b + 3))
                        before = slot - RING
                        while before >= 0 and fills[before] is None:
                            before -= RING
                        if before >= 0:
                            fill_done(pe, fills[before], b + 2 if fills[before][0] == "ctx" else b + 1)
                        else:
                            before = slot + 2 * UNITS - RING
                            while fills[before] is None:
                                before -= RING
                            fill_done(pe, fills[before], b + 1 if fills[before][0] == "ctx" else b)
                        if f[0] == "ctx":
                            fill("ctx", f[1], b + 2, q, fill_ps[slot % 2])
                        else:
                            fill(f[0], f[1], b + 1, 1 - q, fill_ps[slot % 2])

                    for u in range(UNITS):
                        ahead = project or u + 1 < UNITS
                        ahead_2 = project or u + 2 < UNITS
                        following_2 = (b, u + 2, q) if u + 2 < UNITS else (b + 1, u + 2 - UNITS, 1 - q)
                        if u == UNITS - 2 and project:
                            if shared:
                                pe.wait_ge(q_split, q_parts_made * (b + 2))
                                pe.wait_ge(k_split, k_parts_made * NK * (b + 2))
                            else:
                                pe.wait_ge(q_placed, n_q_placed * (b + 2))
                                pe.wait_ge(k_placed, n_placed * (b + 2))
                        if u == 2 and not shared:
                            pe.wait_ge(k_placed_2, n_placed_2 * (b + 1))
                        pe.wait_ge(top_placed, UNITS * b + u + 1)
                        weights(b, u, q, 0)
                        weights(b, u, q, 1)
                        if ahead_2:
                            scores(*following_2, 0)
                        do_fill(2 * u)
                        if u == 0:
                            pe.wait_ge(mixed_out, 2 * UNITS * b + 1)
                            turn_result()
                        weights(b, u, q, 2)
                        if ahead_2:
                            scores(*following_2, 1)
                        weights(b, u, q, 3)
                        if ahead:
                            if u == 0:
                                pe.wait_ge(heads_out, b + 1)
                            place_top(*((b, u + 1) if u + 1 < UNITS else (b + 1, 0)))
                        if ahead_2:
                            scores(*following_2, 2)
                        do_fill(2 * u + 1)
                        if ahead_2:
                            scores(*following_2, 3)
                        if u == 0:
                            pe.wait_ge(v_split, NV * (b + 1))
                        pe.wait_ge(mixed_out, 2 * (UNITS * b + u) + 1)
                        weigh(b, u, q)

                pipeline(pe, body)
                pe.wait_ge(mixed_out, 2 * UNITS * B + 1)
                turn_result()

            @block.scalar
            def _(act):
                act.sem_inc(exp_done, RING)
                act.wait_ge(loaded, 16 * n_loads)

                def deviations(nb):
                    act.wait_ge(spread_done, nb + 1)
                    act.activation(deviation[:, :], spread[:, :], ACT.Sqrt).then_inc(deviation_done, 1)

                def copy_fill(kind, n, nb, q, bank):
                    if kind == "k":
                        c2, i = divmod(n, NKC)
                        a, w = key_cols[i]
                        m = kd if shared else P
                        act.wait_ge(k_projected, NK * nb + n + 1)
                        if not (isinstance(nb, int) and nb == 0 and n < 2):
                            act.wait_ge(k_split, k_parts_made * (NK * nb + n - 1))
                        if bk:
                            act.activation(k_piece[0:m, n % 2, 0:w], bank[0:m, 0:w], ACT.Identity, scale=1 / W_SCALE,
                                           bias=bias_cols[:, 1, c2:c2 + 1]).then_inc(k_copied, 1)
                        else:
                            act.activation(k_piece[0:m, n % 2, 0:w], bank[0:m, 0:w], ACT.Copy,
                                           scale=1 / W_SCALE).then_inc(k_copied, 1)
                    elif kind == "v" and shared:
                        t0, k = v_groups[n]
                        act.wait_ge(v_projected, NV * nb + n + 1)
                        if not (isinstance(nb, int) and NV * nb + n < V_RING):
                            act.wait_ge(v_split, NV * nb + n - V_RING + 1)
                        for m, t1, t2 in value_rows(n):
                            at = slice((t1 - t0) * nv, (t2 - t0) * nv)
                            done = act.activation(v_piece[0:m, n % V_RING, at], bank[0:m, at], ACT.Copy)
                        done.then_inc(v_copied, 1)
                    elif kind == "ctx":
                        g, c = divmod(n, DC)
                        t0, k = key_groups[g]
                        w = min(k * P, KEYS - t0 * P)
                        act.wait_ge(ctx_turned, NC * nb + n + 1)
                        act.activation(ctx[:, c, t0 * P:t0 * P + w], bank[:, 0:w], ACT.Identity,
                                       scale=affine[:, 0, c:c + 1], bias=affine[:, 1, c:c + 1]).then_inc(ctx_placed, 1)
                        context_high(n, nb, q)

                def context_high(n, nb, q):
                    g, c = divmod(n, DC)
                    a, w = key_cols[g]
                    if shared:
                        act.wait_ge(ctx_placed, NCP * nb + n + 1)
                    else:
                        act.wait_ge(ctx_in, 16 * (nb + 1))
                    act.activation(ctx_high[q][:, c, a:a + w], ctx[:, c, a:a + w], ACT.Copy).then_inc(ctx_high_done, 1)

                def values_high(n, nb, q):
                    t0, k = v_groups[n]
                    act.wait_ge(v_copied, NV * nb + n + 1)
                    for m, t1, t2 in value_rows(n):
                        for t in (range(t1, t2) if mask_values else [None]):
                            lo, hi = (t, t + 1) if mask_values else (t1, t2)
                            piece = v_piece[0:m, n % V_RING, (lo - t0) * nv:(hi - t0) * nv].rearrange(
                                "p (t u f) -> p t u f", u=nk, f=dv)
                            scale_by = keep_cols[0:m, q, lo:hi] if mask_values else 1.0
                            done = act.activation(v_parts[q][0:m, lo:hi, :, 0, 0:dv], piece, ACT.Copy, scale=scale_by)
                    done.then_inc(v_high_done, 1)

                def high_queries(nb, q):
                    act.wait_ge(q_cut, q_cuts * (nb + 1))
                    for at in (0, kd):
                        act.activation(q_parts[q][at:at + kd], q_rows[:, :, :, :], ACT.Copy).then_inc(q_split, 1)

                if shared:
                    deviations(0)
                    for n, (kind, i) in enumerate(context_fills):
                        copy_fill(kind, i, 0, 0, fill_ps[n % 2])
                else:
                    for n in range(NCP):
                        context_high(n, 0, 0)
                act.wait_ge(rows_set, n_sets)
                if shared:
                    high_queries(0, 0)
                for n, (kind, i) in enumerate(project_fills):
                    copy_fill(kind, i, 0, 0, fill_ps[n % 2])
                    if kind == "v" and i < NV - first_late:
                        values_high(i, 0, 0)
                if not shared:
                    for n in range(NCP):
                        context_high(n, 1, 1)
                if shared:
                    deviations(1)
                    act.wait_ge(ctx_split, NCP)
                    for n, (kind, i) in enumerate(context_fills):
                        copy_fill(kind, i, 1, 1, fill_ps[n % 2])

                def body(i, b, q, project, prepare):
                    def do_fill(slot):
                        f = fills[slot]
                        if f is None or not (project if f[0] != "ctx" else prepare):
                            return
                        if f == ("ctx", 0):
                            act.wait_ge(ctx_split, NCP * (b + 2))
                        if f[0] == "ctx":
                            copy_fill("ctx", f[1], b + 2, q, fill_ps[slot % 2])
                        else:
                            copy_fill(f[0], f[1], b + 1, 1 - q, fill_ps[slot % 2])

                    def exps(u, g):
                        t0, k = key_groups[g]
                        m = P if k > 1 else TAIL
                        act.wait_ge(weighed, NKG * (UNITS * b + u) + g + 1)
                        act.activation(probs_high[0:m, t0:t0 + k, :], weight_ps[g % 2][0:m, 0:k * P], ACT.Exp)
                        act.activation(probs[0:m, t0:t0 + k, :], weight_ps[g % 2][0:m, 0:k * P],
                                       ACT.Exp).then_inc(exp_done, 1)

                    for u in range(UNITS):
                        exps(u, 0)
                        exps(u, 1)
                        do_fill(2 * u)
                        late = late_values(u, b, q, project)
                        for piece in late[0]:
                            values_high(*piece)
                        exps(u, 2)
                        exps(u, 3)
                        do_fill(2 * u + 1)
                        for piece in late[1]:
                            values_high(*piece)
                        if u == 1 and project and shared:
                            act.wait_ge(mixed_done, UNITS * b + 1)
                            high_queries(b + 1, 1 - q)
                        if prepare and not shared:
                            if u == 2:
                                act.wait_ge(v_projected, NV * (b + 1))
                            for n in context_units[u]:
                                context_high(n, b + 2, q)
                        if shared and prepare and u == 2:
                            deviations(b + 2)

                pipeline(act, body)

            @block.vector
            def _(dve):
                for i in range(2):
                    dve.memset((k_cross if shared else k_rows)[i][top_at:top_at + extra, :, :], SHIFT).then_inc(rows_set, 1)
                    dve.memset(v_parts[i][:, :, :, 0, dv:dv + 1], 1.0).then_inc(rows_set, 1)
                    dve.memset(v_parts[i][:, :, :, 1, dv:dv + 1], 0.0).then_inc(rows_set, 1)
                    if not shared:
                        dve.memset(q_parts[i][top_at:top_at + extra, :, :, :], SHIFT)
                if shared:
                    dve.memset(mean_var[:, :, :], 1.0).then_inc(rows_set, 1)
                dve.memset(mixed[:, :, :, :], 0.0).then_inc(rows_set, 1)
                dve.memset(top_cols[:, :, :], SHIFT * SHIFT).then_inc(rows_set, 1)
                dve.wait_ge(loaded, 16 * n_loads)
                dve.tensor_scalar(w_kv[:, :, :], w_kv[:, :, :], W_SCALE, None, ALU.mult).then_inc(w_scaled, 1)
                dve.wait_ge(w_scaled, 1)
                dve.tensor_copy(w_high[:, :, :], w_kv[:, :, :]).then_inc(w_split, 1)
                dve.wait_ge(w_split, 1)
                dve.tensor_tensor(w_low[:, :, :], w_kv[:, :, :], w_high[:, :, :], ALU.subtract).then_inc(w_split, 1)
                if scale:
                    dve.tensor_scalar(q_scale[:, :], core.head_of_pair[:, :], scale_col[:, 0:1], None,
                                      ALU.mult).then_inc(q_scaled, 1)
                else:
                    dve.tensor_scalar(q_scale[:, :], core.head_of_pair[:, :], DH ** -0.5, None,
                                      ALU.mult).then_inc(q_scaled, 1)
                dve.wait_ge(q_scaled, 1)
                dve.wait_ge(rows_set, n_sets)
                dve.sem_inc(part_found, RING)
                dve.sem_inc(mixed_out, 1)

                def context_stats(nb, tiles):
                    dve.wait_ge(raw_in, 32 * (nb + 1))
                    for t in tiles:
                        m = keys_in(t)
                        dve.bn_stats(stats[0:m, t, :], ctx_raw[0:m, t, :]).then_inc(stats_done, 1)

                def context_spread(nb):
                    dve.wait_ge(stats_done, KT * (nb + 1))
                    dve.memset(spread[:, :], 0.0).then_inc(spread_set, 1)
                    for t in range(KT):
                        m = keys_in(t)
                        dve.bn_aggr(mean_var[0:m, t, :], stats[0:m, t, :]).then_inc(aggregated, 1)
                    dve.wait_ge(spread_set, nb + 1)
                    dve.wait_ge(aggregated, KT * (nb + 1))
                    dve.tensor_scalar(spread[:, :], mean_var[:, :, 1], EPS, None, ALU.add).then_inc(spread_done, 1)

                def context_norm(nb):
                    dve.wait_ge(deviation_done, nb + 1)
                    dve.reciprocal(rstd[:, :], deviation[:, :]).then_inc(rstd_done, 1)
                    dve.wait_ge(rstd_done, nb + 1)
                    for t in range(KT):
                        m = keys_in(t)
                        dve.tensor_scalar(ctx_raw[0:m, t, :], ctx_raw[0:m, t, :], mean_var[0:m, t, 0:1],
                                          rstd[0:m, t:t + 1], ALU.subtract, ALU.mult).then_inc(normed, 1)

                def convert_mask(nb, q):
                    dve.wait_ge(mask_in, 32 * (nb + 1))
                    dve.tensor_scalar(keep[:, :], mask_int[:, :], 0, None, ALU.not_equal).then_inc(kept, 1)
                    dve.tensor_scalar(keep_cols[:, q, :], keep_int[:, :], 0, None, ALU.not_equal).then_inc(kept, 1)
                    dve.wait_ge(kept, 2 * (nb + 1))
                    dve.tensor_scalar(mask_row[:, :], keep[0:1, :], SHIFT, -SHIFT, ALU.mult, ALU.add).then_inc(row_ready, 1)

                def cut_queries(nb, bank):
                    dve.wait_ge(q_projected, nb + 1)
                    if shared:
                        both = bank[:, :].rearrange("p (u s) -> p u s", u=UNITS)
                        for h2 in range(2):
                            dve.tensor_scalar(q_rows[:, :, h2, :], both[kd * h2:kd * h2 + kd], kd ** -0.5, None,
                                              ALU.mult).then_inc(q_cut, 1)
                    else:
                        for c in range(DC):
                            for h2 in range(2):
                                dve.tensor_scalar(q_both[:, c, h2, :], bank[:, c * S:(c + 1) * S],
                                                  bias_cols[:, 0, c:c + 1], q_scale[:, h2:h2 + 1],
                                                  ALU.add, ALU.mult).then_inc(q_cut, 1)

                def split_queries(nb, q):
                    n = q_parts_made * nb
                    if shared:
                        dve.wait_ge(q_split, n + 2)
                        dve.tensor_tensor(q_cross[q][0:kd], q_rows[:, :, :, :], q_parts[q][0:kd],
                                          ALU.subtract).then_inc(q_split, 1)
                    else:
                        dve.wait_ge(q_cut, q_cuts * (nb + 1))
                        dve.tensor_copy(q_high[:, :, :, :], q_both[:, :, :, :]).then_inc(q_split, 1)
                        dve.wait_ge(q_split, n + 1)
                        dve.tensor_tensor(q_low[:, :, :, :], q_both[:, :, :, :], q_high[:, :, :, :],
                                          ALU.subtract).then_inc(q_split, 1)

                def split_shared_keys(n, nb, q):
                    a, w = key_cols[n]
                    at = k_parts_made * (NK * nb + n)
                    piece = k_piece[0:kd, n % 2, 0:w]
                    dve.wait_ge(k_copied, NK * nb + n + 1)
                    dve.tensor_copy(k_rows[q][0:kd, 0, a:a + w], piece).then_inc(k_split, 1)
                    dve.tensor_copy(k_cross[q][0:kd, 0, a:a + w], piece).then_inc(k_split, 1)
                    dve.wait_ge(k_split, at + 2)
                    dve.tensor_tensor(k_rows[q][kd:2 * kd, 0, a:a + w], piece, k_cross[q][0:kd, 0, a:a + w],
                                      ALU.subtract).then_inc(k_split, 1)

                def copy_values(n, nb, bank):
                    t0, k = v_groups[n]
                    m = keys_in(t0)
                    dve.wait_ge(v_projected, NV * nb + n + 1)
                    if not (isinstance(nb, int) and NV * nb + n < V_RING):
                        dve.wait_ge(v_split, NV * nb + n - V_RING + 1)
                    bias = v_bias[0:m, :].unsqueeze(1).broadcast_to([m, k, nv])
                    dve.scalar_tensor_tensor(
                        out=v_piece[0:m, n % V_RING, 0:k * nv].rearrange("p (t f) -> p t f", f=nv), in0=bias,
                        scalar=W_SCALE, in1=bank[0:m, 0:k * nv].rearrange("p (t f) -> p t f", f=nv),
                        op0=ALU.mult, op1=ALU.add).then_inc(v_copied, 1)

                def find_top(b, u, n):
                    a, w = key_cols[n]
                    dve.wait_ge(scored, NKC * (UNITS * b + u) + n + 1)
                    dve.tensor_reduce(top_parts[:, u % 2, n:n + 1], score_ps[n % 2][:, 0:w], AX.X,
                                      ALU.max).then_inc(part_found, 1)

                def join_top(b, u):
                    dve.wait_ge(part_found, RING + NKC * (UNITS * b + u + 1))
                    dve.tensor_reduce(top_cols[:, u % 2, 1:2], top_parts[:, u % 2, :], AX.X, ALU.max,
                                      negate=True).then_inc(top_found, 1)

                def put_top(b, u, q):
                    dve.wait_ge(top_turned, UNITS * b + u + 1)
                    dve.tensor_copy(q_cross[q][top_at:top_at + extra, u, :, :],
                                    side_ps[top_at:top_at + extra, 0:P]).then_inc(top_placed, 1)

                if shared:
                    context_stats(0, range(KT))
                    context_spread(0)
                    context_norm(0)
                if mask:
                    convert_mask(0, 0)
                cut_queries(0, fill_ps[0])
                split_queries(0, 0)
                if shared:
                    for n in range(NK):
                        split_shared_keys(n, 0, 0)
                if not shared:
                    for n in range(NV):
                        copy_values(n, 0, fill_ps[(1 + NK + n) % 2])
                for u in range(2):
                    for n in range(NKC):
                        find_top(0, u, n)
                    join_top(0, u)
                put_top(0, 0, 0)
                if shared:
                    context_stats(1, range(KT))
                    context_spread(1)
                    context_norm(1)
                if mask:
                    dve.wait_ge(k_placed, n_placed)
                    dve.wait_ge(k_split, k_parts_made * NK)
                    convert_mask(1, 1)

                def dve_low(b, u, g):
                    if g in low_groups["dve"]:
                        low_part(dve, low_dve, b, u, g)

                def put_result(b):
                    dve.tensor_copy(heads[:, 0:2 * out_chunks, bass.ds(b * S, S)],
                                    side_ps[:, 0:out_chunks * P].rearrange("p (c s) -> p c s", s=S)).then_inc(heads_out, 1)

                def body(i, b, q, project, prepare):
                    def do_fill(slot):
                        f = fills[slot]
                        if f and f[0] == "v" and project and not shared:
                            copy_values(f[1], b + 1, fill_ps[slot % 2])
                        if f and f[0] == "q" and project:
                            if shared:
                                dve.wait_ge(q_split, q_parts_made * (b + 1))
                            else:
                                dve.wait_ge(q_placed, n_q_placed * (b + 1))
                            cut_queries(b + 1, fill_ps[slot % 2])
                        if f and f[0] == "k" and project and shared:
                            split_shared_keys(f[1], b + 1, 1 - q)

                    for u in range(UNITS):
                        ahead = project or u + 1 < UNITS
                        ahead_2 = project or u + 2 < UNITS
                        following_2 = (b, u + 2) if u + 2 < UNITS else (b + 1, u + 2 - UNITS)
                        if ahead_2:
                            find_top(*following_2, 0)
                        do_fill(2 * u)
                        dve_low(b, u, 0)
                        if u == 0:
                            dve.wait_ge(mixed_turned, b + 1)
                            put_result(b)
                        if ahead_2:
                            find_top(*following_2, 1)
                        dve_low(b, u, 1)
                        if ahead:
                            put_top(*((b, u + 1, q) if u + 1 < UNITS else (b + 1, 0, 1 - q)))
                        if ahead_2:
                            find_top(*following_2, 2)
                        dve_low(b, u, 2)
                        dve_low(b, u, 3)
                        if ahead_2:
                            find_top(*following_2, 3)
                            join_top(*following_2)
                        do_fill(2 * u + 1)
                        if u == 2 and shared and project:
                            split_queries(b + 1, 1 - q)
                        if shared and prepare:
                            if u < 3:
                                context_stats(b + 2, [range(0, 5), range(5, 9), range(9, KT)][u])
                            if u == 2:
                                context_spread(b + 2)
                            if u == 3:
                                context_norm(b + 2)
                        if mask and prepare and u == 6:
                            dve.wait_ge(k_split, k_parts_made * NK * (b + 2))
                            dve.wait_ge(k_placed, n_placed * (b + 2))
                            if mask_values:
                                dve.wait_ge(v_split, NV * (b + 1))
                            convert_mask(b + 2, q)
                        dve.wait_ge(mixed_done, UNITS * b + u + 1)
                        dve.reciprocal(share[:, u:u + 1], mixed_ps[:, dv:dv + 1]).then_inc(share_done, 1)
                        dve.wait_ge(share_done, UNITS * b + u + 1)
                        for h2 in range(2):
                            rows = slice(S * h2, S * h2 + S)
                            f = 0 if shared else DH * h2
                            parts = mixed_ps[rows, 0:2 * (dv + 1)].rearrange("p (n f) -> p n f", n=2)
                            dve.tensor_scalar(mixed[rows, :, u, :], parts[:, :, f:f + dm], share[rows, u:u + 1],
                                              1 / W_SCALE, ALU.mult, ALU.mult).then_inc(mixed_out, 1)
                        if u == 0 and project and not shared:
                            split_queries(b + 1, 1 - q)

                pipeline(dve, body)
                dve.wait_ge(mixed_turned, B + 1)
                put_result(B)
                dve.wait_ge(heads_out, B + 1)


def choose_experts(core, router, bias=None, experts=8, first=2, by_score=False, at=0):
    nc, d = core.nc, core.dram
    E = experts
    with Stage(core, "gate") as s:
        w = s.sb("w", [P, DC, E])
        bias_rows = s.sb("bias_rows", [P, E])
        lower = s.sb("lower", [P, E, E])
        score = s.sb("score", [P, NT, E])
        top = s.sb("top", [P, NT])
        prob = s.sb("prob", [P, NT, E])
        total = s.sb("total", [P, NT])
        share = s.sb("share", [P, NT])
        above = s.sb("above", [P, NT, E, E])
        equal = s.sb("equal", [P, NT, E, E])
        rank = s.sb("rank", [P, NT, E])
        logit = s.banks("logit", 1)[0]
        loaded, routed, exp_done, step = map(s.sem, ("loaded", "routed", "exp_done", "step"))
        n_loads = 2 + bool(bias)

        def over_tile(a):
            return a.unsqueeze(1).broadcast_to([P, NT] + list(a.shape[1:]))

        with nc.Block() as block:

            @block.sync
            def _(sp):
                sp.dma_start(w[:, :, :], d[router].rearrange("(c p) e -> p c e", p=P)).then_inc(loaded, 16)
                sp.dma_start(lower[:, :, :], d["c_lower"]).then_inc(loaded, 16)
                if bias:
                    sp.dma_start(bias_rows[:, :], d[bias].partition_broadcast(P)).then_inc(loaded, 16)
                sp.wait_ge(loaded, 16 * n_loads)

            @block.tensor
            def _(pe):
                pe.wait_ge(loaded, 16 * n_loads)
                for t in range(NT):
                    for c in range(DC):
                        mm = pe.matmul(logit[:, t * E:(t + 1) * E], core.xnt[:, c, t * P:(t + 1) * P], w[:, c, :],
                                       start=(c == 0), stop=(c == DC - 1))
                mm.then_inc(routed, 1)

            @block.scalar
            def _(act):
                act.wait_ge(step, 3)
                act.activation(prob[:, :, :], prob[:, :, :], ACT.Exp).then_inc(exp_done, 1)

            @block.vector
            def _(dve):
                n = [0]

                def chain(i):
                    n[0] += 1
                    i.then_inc(step, 1)
                    dve.wait_ge(step, n[0])

                dve.wait_ge(loaded, 16 * n_loads)
                dve.wait_ge(routed, 1)
                got = logit[:, 0:NT * E].rearrange("p (t e) -> p t e", t=NT)
                if bias:
                    chain(dve.tensor_tensor(score[:, :, :], got, over_tile(bias_rows[:, :]), ALU.add))
                else:
                    chain(dve.tensor_copy(score[:, :, :], got))
                chain(dve.tensor_reduce(top[:, :], score[:, :, :], AX.X, ALU.max))
                chain(dve.tensor_tensor(prob[:, :, :], score[:, :, :], top[:, :].unsqueeze(2).broadcast_to([P, NT, E]),
                                        ALU.subtract))
                dve.wait_ge(exp_done, 1)
                chain(dve.tensor_reduce(total[:, :], prob[:, :, :], AX.X, ALU.add))
                chain(dve.reciprocal(share[:, :], total[:, :]))
                chain(dve.tensor_tensor(prob[:, :, :], prob[:, :, :], share[:, :].unsqueeze(2).broadcast_to([P, NT, E]),
                                        ALU.mult))
                key = score if by_score else prob
                mine = key[:, :, :].unsqueeze(3).broadcast_to([P, NT, E, E])
                other = key[:, :, :].unsqueeze(2).broadcast_to([P, NT, E, E])
                chain(dve.tensor_tensor(equal[:, :, :, :], other, mine, ALU.is_equal))
                chain(dve.tensor_tensor(equal[:, :, :, :], equal[:, :, :, :], over_tile(lower[:, :, :]), ALU.mult))
                chain(dve.tensor_tensor(above[:, :, :, :], other, mine, ALU.is_gt))
                chain(dve.tensor_tensor(above[:, :, :, :], above[:, :, :, :], equal[:, :, :, :], ALU.add))
                chain(dve.tensor_reduce(rank[:, :, :], above[:, :, :, :], AX.X, ALU.add))
                chain(dve.tensor_scalar(rank[:, :, :], rank[:, :, :], float(first) - 0.5, None, ALU.is_lt))
                chain(dve.tensor_tensor(core.gates[:, :, at:at + E], rank[:, :, :], prob[:, :, :], ALU.mult))


def feed_forward(core, up, down, hidden, experts, func, paired=False, up_bias=None, down_bias=None, gated=True,
                 first_gate_one=False, add_norm=False):
    nc, d = core.nc, core.dram
    pieces = cols(hidden, P)
    NF = len(pieces)
    TH = T // BANK
    wide = hidden * (2 if paired else 1)
    full = hidden // P
    rest = hidden - full * P
    with Stage(core, "ffn") as s:
        w_up = s.sb("w_up", [P, DC, wide])
        w_down = s.sb("w_down", [P, NF, D])
        hid = s.sb("hid", [P, NF, T])
        gate_act = s.sb("gate_act", [P, 2, BANK]) if paired else None
        bias_now = s.sb("bias_now", [P, NF])
        down_bias_rows = s.sb("down_bias_rows", [8, D]) if down_bias else None
        gates_t = s.sb("gates_t", [8, T]) if down_bias else None
        up_ps = s.banks("up_ps", 4)
        out_ps = s.banks("out_ps", 4)
        (up_in, down_in, loaded, started, up_used, down_used, up_done, act_done, hid_done, out_done, added,
         gates_turned, gates_copied, bias_in, bias_used) = map(s.sem, (
             "up_in", "down_in", "loaded", "started", "up_used", "down_used", "up_done", "act_done", "hid_done",
             "out_done", "added", "gates_turned", "gates_copied", "bias_in", "bias_used"))
        n_down = (1 if full else 0) + (1 if rest else 0)
        n_up = NF * TH
        n_started = first_gate_one + add_norm
        n_bias = NT if down_bias else 0
        n_added = NT if down_bias else 1
        with nc.Block() as block:

            @block.sync
            def _(sp):
                if down_bias:
                    sp.dma_start(down_bias_rows[:, :], d[down_bias]).then_inc(loaded, 16)
                with sp.Fori(0, experts) as e:
                    sp.wait_ge(up_used, e + 1)
                    sp.dma_start(w_up[:, :, :], d[up][bass.ds(e, 1), :, :].rearrange(
                        "e (c p) f -> p (e c) f", p=P)).then_inc(up_in, 16)
                    if up_bias:
                        sp.wait_ge(bias_used, e + 1)
                        sp.dma_start(bias_now[:, :], d[up_bias][bass.ds(e, 1), :, :].rearrange(
                            "e p f -> p (e f)")).then_inc(bias_in, 16)
                    sp.wait_ge(down_used, e + 1)
                    rows = d[down][bass.ds(e, 1), :, :].rearrange("e f m -> (e f) m")
                    if full:
                        sp.dma_start(w_down[:, 0:full, :],
                                     rows[0:full * P, :].rearrange("(f p) m -> p f m", p=P)).then_inc(down_in, 16)
                    if rest:
                        sp.dma_start(w_down[0:rest, full, :], rows[full * P:hidden, :]).then_inc(down_in, 16)
                if up_bias:
                    sp.wait_ge(bias_in, 16 * experts)
                    sp.wait_ge(loaded, 16)
                sp.wait_ge(up_in, 16 * experts)
                sp.wait_ge(down_in, 16 * n_down * experts)

            @block.tensor
            def _(pe):
                if down_bias:
                    for h in range(TH):
                        for k in range(4):
                            t = 4 * h + k
                            mm = pe.transpose(up_ps[h][0:8, k * P:(k + 1) * P], core.gates[:, t, 0:8], core.ident[:, :])
                        mm.then_inc(gates_turned, 1)
                    pe.wait_ge(gates_copied, TH)
                    pe.wait_ge(loaded, 16)
                    for t in range(NT):
                        if t >= 4:
                            pe.wait_ge(added, t - 3)
                        pe.matmul(out_ps[t % 4][:, 0:D], gates_t[:, t * P:(t + 1) * P], down_bias_rows[:, :],
                                  start=True, stop=True).then_inc(out_done, 1)
                with pe.Fori(0, experts) as e:
                    pe.wait_ge(up_in, 16 * (e + 1))
                    n = 0
                    for f, (a, w) in enumerate(pieces):
                        for h in range(TH):
                            if n >= (2 if paired else 4):
                                pe.wait_ge(hid_done, n_up * e + n - (1 if paired else 3))
                            for part in range(2 if paired else 1):
                                bank = up_ps[(2 * n + part) % 4] if paired else up_ps[n % 4]
                                for c in range(DC):
                                    mm = pe.matmul(bank[0:w, :], w_up[:, c, part * hidden + a:part * hidden + a + w],
                                                   core.xnt[:, c, h * BANK:(h + 1) * BANK],
                                                   start=(c == 0), stop=(c == DC - 1))
                            mm.then_inc(up_done, 1)
                            n += 1
                    pe.wait_ge(down_in, 16 * n_down * (e + 1))
                    pe.wait_ge(hid_done, n_up * (e + 1))
                    for t in range(NT):
                        if t >= 4:
                            pe.wait_ge(added, n_added + NT * e + t - 3)
                        elif down_bias:
                            pe.wait_ge(added, NT * e + t + 5)
                        else:
                            pe.wait_ge(added, n_added + NT * e)
                        for f, (a, w) in enumerate(pieces):
                            mm = pe.matmul(out_ps[t % 4][:, 0:D], hid[0:w, f, t * P:(t + 1) * P], w_down[0:w, f, :],
                                           start=(f == 0), stop=(f == NF - 1))
                        mm.then_inc(out_done, 1)

            @block.scalar
            def _(act):
                if down_bias:
                    for h in range(TH):
                        act.wait_ge(gates_turned, h + 1)
                        act.activation(gates_t[:, h * BANK:(h + 1) * BANK], up_ps[h][0:8, :], ACT.Copy).then_inc(gates_copied, 1)
                with act.Fori(0, experts) as e:
                    n = 0
                    if up_bias:
                        act.wait_ge(bias_in, 16 * (e + 1))
                    for f, (a, w) in enumerate(pieces):
                        for h in range(TH):
                            act.wait_ge(up_done, n_up * e + n + 1)
                            if paired:
                                if n >= 2:
                                    act.wait_ge(hid_done, n_up * e + n - 1)
                                act.activation(gate_act[0:w, n % 2, :], up_ps[(2 * n + 1) % 4][0:w, :], func).then_inc(act_done, 1)
                            elif up_bias:
                                act.activation(hid[0:w, f, h * BANK:(h + 1) * BANK], up_ps[n % 4][0:w, :], func,
                                               bias=bias_now[0:w, f:f + 1]).then_inc(hid_done, 1)
                            else:
                                act.activation(hid[0:w, f, h * BANK:(h + 1) * BANK], up_ps[n % 4][0:w, :],
                                               func).then_inc(hid_done, 1)
                            n += 1

            @block.vector
            def _(dve):
                if first_gate_one:
                    dve.memset(core.gates[:, :, 0:1], 1.0).then_inc(started, 1)
                if add_norm:
                    dve.tensor_tensor(core.x[:, :, :], core.x[:, :, :], core.xn[:, :, :], ALU.add).then_inc(started, 1)
                if n_started:
                    dve.wait_ge(started, n_started)
                if not down_bias:
                    dve.sem_inc(added, n_added)
                if down_bias:
                    for t in range(NT):
                        dve.wait_ge(out_done, t + 1)
                        dve.tensor_tensor(core.x[:, t, :], core.x[:, t, :], out_ps[t % 4][:, 0:D], ALU.add).then_inc(added, 1)
                with dve.Fori(0, experts) as e:
                    if paired:
                        n = 0
                        for f, (a, w) in enumerate(pieces):
                            for h in range(TH):
                                dve.wait_ge(act_done, n_up * e + n + 1)
                                dve.tensor_tensor(hid[0:w, f, h * BANK:(h + 1) * BANK], up_ps[(2 * n) % 4][0:w, :],
                                                  gate_act[0:w, n % 2, :], ALU.mult).then_inc(hid_done, 1)
                                n += 1
                    for t in range(NT):
                        dve.wait_ge(out_done, n_bias + NT * e + t + 1)
                        dve.wait_ge(added, NT * e + t + 1 if down_bias else n_added + NT * e)
                        if gated:
                            gate = core.gates[:, t, bass.ds(e, 1)]
                            dve.scalar_tensor_tensor(out=core.x[:, t, :], in0=out_ps[t % 4][:, 0:D], scalar=gate,
                                                     in1=core.x[:, t, :], op0=ALU.mult, op1=ALU.add).then_inc(added, 1)
                        else:
                            dve.tensor_tensor(core.x[:, t, :], core.x[:, t, :], out_ps[t % 4][:, 0:D],
                                              ALU.add).then_inc(added, 1)
                dve.wait_ge(added, n_added + NT * experts)

            @block.gpsimd
            def _(pool):
                pool.sem_inc(up_used, 1)
                pool.sem_inc(down_used, 1)
                pool.sem_inc(bias_used, 1)
                with pool.Fori(0, experts) as e:
                    pool.wait_ge(up_done, n_up * (e + 1))
                    pool.nop().then_inc(up_used, 1)
                    pool.wait_ge(hid_done, n_up * (e + 1))
                    pool.nop().then_inc(bias_used, 1)
                    pool.wait_ge(out_done, n_bias + NT * (e + 1))
                    pool.nop().then_inc(down_used, 1)


def quantised_linear(core, weight, bias, grid_max=448.0, least=1e-12):
    nc, d = core.nc, core.dram
    with Stage(core, "fp8") as s:
        w = s.sb("w", [P, DC, D])
        bias_rows = s.sb("bias_rows", [P, D])
        tensors = [core.xnt[:, :, :].rearrange("p c t -> p (c t)"), w[:, :, :].rearrange("p c f -> p (c f)")]
        sizes = [DC * T, DC * D]
        peak = s.sb("peak", [P, 2])
        peak_row = s.sb("peak_row", [1, 2])
        row = s.sb("row", [1, 2])
        scale = s.sb("scale", [P, 2])
        back = s.sb("back", [P, 2])
        back_both = s.sb("back_both", [P, 1])
        scaled = s.sb("scaled", [P, DC * T])
        magic = s.sb("magic", [P, DC * T])
        quant = [s.sb("quant_x", [P, DC, T]), s.sb("quant_w", [P, DC, D])]
        turn_ps, cast_ps = s.banks("turn_ps", 2)
        out_ps = s.banks("out_ps", 4)
        loaded, step, peaks_turned, rows_cast, projected, added = map(
            s.sem, ("loaded", "step", "peaks_turned", "rows_cast", "projected", "added"))
        with nc.Block() as block:

            @block.sync
            def _(sp):
                sp.dma_start(w[:, :, :], d[weight].rearrange("(c p) f -> p c f", p=P)).then_inc(loaded, 16)
                sp.dma_start(bias_rows[:, :], d[bias].partition_broadcast(P)).then_inc(loaded, 16)
                sp.wait_ge(loaded, 32)

            @block.tensor
            def _(pe):
                pe.wait_ge(step, 2)
                for n in range(2):
                    mm = pe.transpose(turn_ps[0:1, n * P:(n + 1) * P], peak[:, n:n + 1], core.ident[:, :])
                mm.then_inc(peaks_turned, 1)
                pe.wait_ge(step, 6)
                pe.matmul(cast_ps[:, 0:2], core.ones[0:1, :], row[:, :], start=True, stop=True).then_inc(rows_cast, 1)
                pe.wait_ge(step, 19)
                for t in range(NT):
                    if t >= 4:
                        pe.wait_ge(added, t - 3)
                    for c in range(DC):
                        mm = pe.matmul(out_ps[t % 4][:, 0:D], quant[0][:, c, t * P:(t + 1) * P], quant[1][:, c, :],
                                       start=(c == 0), stop=(c == DC - 1))
                    mm.then_inc(projected, 1)

            @block.vector
            def _(dve):
                n = [0]

                def chain(i):
                    n[0] += 1
                    i.then_inc(step, 1)
                    dve.wait_ge(step, n[0])

                dve.wait_ge(loaded, 32)
                for k in range(2):
                    chain(dve.tensor_reduce(peak[:, k:k + 1], tensors[k], AX.X, ALU.max, apply_absolute_value=True))
                dve.wait_ge(peaks_turned, 1)
                chain(dve.tensor_reduce(peak_row[:, :], turn_ps[0:1, 0:2 * P].rearrange("p (n k) -> p n k", n=2), AX.X,
                                        ALU.max))
                chain(dve.tensor_scalar(peak_row[:, :], peak_row[:, :], least, None, ALU.max))
                chain(dve.reciprocal(row[:, :], peak_row[:, :]))
                chain(dve.tensor_scalar(row[:, :], row[:, :], grid_max, None, ALU.mult))
                dve.wait_ge(rows_cast, 1)
                chain(dve.tensor_copy(scale[:, :], cast_ps[:, 0:2]))
                chain(dve.reciprocal(back[:, :], scale[:, :]))
                chain(dve.tensor_tensor(back_both[:, :], back[:, 0:1], back[:, 1:2], ALU.mult))
                for k in range(2):
                    v, m = scaled[:, 0:sizes[k]], magic[:, 0:sizes[k]]
                    q = quant[k][:, :, :].rearrange("p c t -> p (c t)")
                    chain(dve.tensor_scalar(v, tensors[k], scale[:, k:k + 1], None, ALU.mult))
                    chain(dve.tensor_scalar(m.bitcast(I32), v.bitcast(I32), 0x7F800000, None, ALU.bitwise_and))
                    chain(dve.tensor_scalar(m, m, 2.0 ** -6, 1.5 * 2.0 ** 20, ALU.max, ALU.mult))
                    chain(dve.tensor_tensor(v, v, m, ALU.add))
                    chain(dve.tensor_tensor(q, v, m, ALU.subtract))
                chain(dve.tensor_tensor(core.x[:, :, :], core.x[:, :, :],
                                        bias_rows[:, :].unsqueeze(1).broadcast_to([P, NT, D]), ALU.add))
                for t in range(NT):
                    dve.wait_ge(projected, t + 1)
                    dve.scalar_tensor_tensor(out=core.x[:, t, :], in0=out_ps[t % 4][:, 0:D], scalar=back_both[:, 0:1],
                                             in1=core.x[:, t, :], op0=ALU.mult, op1=ALU.add).then_inc(added, 1)
                dve.wait_ge(added, NT)


def gated_convolution(core, mixed):
    nc, d = core.nc, core.dram
    CH = 3 * DC
    PAD = 3
    G = CH * (T // BANK)
    with Stage(core, "conv") as s:
        w_in = s.sb("w_in", [P, DC, 3 * D])
        in_bias = s.sb("in_bias", [P, CH])
        short_w = s.sb("short_w", [P, CH, 3])
        short_b = s.sb("short_b", [P, CH])
        inner_w = s.sb("inner_w", [P, DC, 4])
        inner_b = s.sb("inner_b", [P, DC])
        z = s.sb("z", [P, CH, B, PAD + S])
        conv = s.sb("conv", [P, CH, B, S])
        kv = s.sb("kv", [P, DC, B, PAD + S])
        ps = s.banks("ps", 4)
        loaded, padded, projected, copied, short_done, kv_done, inner_done, mixed_done = map(
            s.sem, ("loaded", "padded", "projected", "copied", "short_done", "kv_done", "inner_done", "mixed_done"))
        with nc.Block() as block:

            @block.sync
            def _(sp):
                sp.dma_start(w_in[:, :, :], d["L2_attn_W_in"].rearrange("(c p) f -> p c f", p=P)).then_inc(loaded, 16)
                for dst, name in ((in_bias[:, :], "L2_attn_b_in"), (short_b[:, :], "L2_attn_short_b"),
                                  (inner_b[:, :], "L2_attn_inner_b")):
                    sp.dma_start(dst, d[name].rearrange("(c p) -> p c", p=P),
                                 allow_slow_non_contiguous=True).then_inc(loaded, 16)
                for dst, name in ((short_w[:, :, :], "L2_attn_short_w"), (inner_w[:, :, :], "L2_attn_inner_w")):
                    sp.dma_start(dst, d[name].rearrange("(c p) k -> p c k", p=P),
                                 allow_slow_non_contiguous=True).then_inc(loaded, 16)
                sp.wait_ge(loaded, 96)

            @block.gpsimd
            def _(pool):
                pool.memset(z[:, :, :, 0:PAD], 0.0).then_inc(padded, 1)
                pool.memset(kv[:, :, :, 0:PAD], 0.0).then_inc(padded, 1)
                pool.wait_ge(padded, 2)

            @block.tensor
            def _(pe):
                pe.wait_ge(loaded, 96)
                n = 0
                for ch in range(CH):
                    for h in range(T // BANK):
                        if n >= 4:
                            pe.wait_ge(copied, n - 3)
                        for c in range(DC):
                            mm = pe.matmul(ps[n % 4][:, :], w_in[:, c, ch * P:(ch + 1) * P],
                                           core.xnt[:, c, h * BANK:(h + 1) * BANK], start=(c == 0), stop=(c == DC - 1))
                        mm.then_inc(projected, 1)
                        n += 1

            @block.scalar
            def _(act):
                act.wait_ge(loaded, 96)
                n = 0
                for ch in range(CH):
                    for h in range(T // BANK):
                        act.wait_ge(projected, n + 1)
                        nb = BANK // S
                        act.activation(z[:, ch, h * nb:(h + 1) * nb, PAD:],
                                       ps[n % 4][:, :].rearrange("p (b s) -> p b s", s=S), ACT.Identity,
                                       bias=in_bias[:, ch:ch + 1]).then_inc(copied, 1)
                        n += 1

            @block.vector
            def _(dve):
                dve.wait_ge(loaded, 96)
                dve.wait_ge(padded, 2)

                def taps(dst, src, w, bias, done, before):
                    K = w.shape[1]
                    for k in range(K):
                        part = src[:, :, PAD - K + 1 + k:PAD - K + 1 + k + S]
                        if k == 0:
                            dve.tensor_scalar(dst, part, w[:, 0:1], bias, ALU.mult, ALU.add).then_inc(done, 1)
                        else:
                            dve.wait_ge(done, before + k)
                            dve.scalar_tensor_tensor(out=dst, in0=part, scalar=w[:, k:k + 1], in1=dst, op0=ALU.mult,
                                                     op1=ALU.add).then_inc(done, 1)

                for ch in range(CH):
                    dve.wait_ge(copied, 2 * ch + 2)
                    taps(conv[:, ch], z[:, ch], short_w[:, ch, :], short_b[:, ch:ch + 1], short_done, 3 * ch)
                dve.wait_ge(short_done, 3 * CH)
                for c in range(DC):
                    dve.tensor_tensor(kv[:, c, :, PAD:], conv[:, DC + c], conv[:, 2 * DC + c], ALU.mult).then_inc(kv_done, 1)
                dve.wait_ge(kv_done, DC)
                for c in range(DC):
                    taps(conv[:, DC + c], kv[:, c], inner_w[:, c, :], inner_b[:, c:c + 1], inner_done, 4 * c)
                dve.wait_ge(inner_done, 4 * DC)
                for c in range(DC):
                    dve.tensor_tensor(mixed[:, c, S:], conv[:, c].rearrange("p b s -> p (b s)"),
                                      conv[:, DC + c].rearrange("p b s -> p (b s)"), ALU.mult).then_inc(mixed_done, 1)
                dve.wait_ge(mixed_done, DC)


def build(nc, dram, stages=range(12)):
    with ExitStack() as ctx:
        core = Core(nc, dram, ctx)
        load_residual(core)

        def with_heads(chunks, attend, weight, bias=None):
            with nc.sbuf_tensor(f"heads{core.stage}", [P, chunks, S + T], F32) as heads:
                attend(heads)
                project_and_add(core, heads, chunks, weight, bias)

        def layer0_cross():
            normalise(core, core.x)
            normalise(core, core.xn, gamma="L0_xattn_ln_g", beta="L0_xattn_ln_b")
            with_heads(8, lambda h: cross_attention(
                core, h, "L0_xattn_Wq", "L0_xattn_Wk", "L0_xattn_Wv", context_gamma="L0_xattn_cln_g",
                context_beta="L0_xattn_cln_b"), "L0_xattn_Wo")
            feed_forward(core, "L0_xattn_Wff1", "L0_xattn_Wff2", 4 * D, 1, ACT.Silu, paired=True, gated=False)

        def cross(p, mask=None, mask_cols=None, mask_values=False, scale=None):
            normalise(core, core.x)
            with_heads(2, lambda h: cross_attention(
                core, h, p + "Wq", p + "Wk", p + "Wv", p + "bq", p + "bk", p + "bv", mask=mask, mask_cols=mask_cols,
                mask_values=mask_values, scale=scale), p + "Wo", p + "bo")

        def layer0_self():
            normalise(core, core.x)
            with_heads(2, lambda h: self_attention(core, h, "L0_attn_wq", "L0_attn_wk", "L0_attn_wv"), "L0_attn_w_out")

        def layer0_ffn():
            normalise(core, core.x)
            quantised_linear(core, "L0_ffn_weight", "L0_ffn_bias")

        def layer1_self():
            normalise(core, core.x)
            with_heads(2, lambda h: self_attention(core, h, "L1_attn_wq", None, "L1_attn_wv", bv="L1_attn_wv_b"),
                       "L1_attn_out_w", "L1_attn_out_b")

        def layer1_ffn():
            normalise(core, core.x)
            choose_experts(core, "L1_ffn_router_w", first=2, at=1)
            feed_forward(core, "L1_ffn_up", "L1_ffn_down", 1024, 9, ACT.Gelu, first_gate_one=True, add_norm=True)

        def layer2_conv():
            normalise(core, core.x)
            with_heads(2, lambda h: gated_convolution(core, h), "L2_attn_W_out", "L2_attn_b_out")

        def layer2_ffn():
            normalise(core, core.x)
            normalise(core, core.xn, rms=True, gamma="L2_ffn_norm_scale", eps=1e-6)
            choose_experts(core, "L2_ffn_w_router", first=2, by_score=True)
            feed_forward(core, "L2_ffn_w_up", "L2_ffn_w_down", 704, 8, ACT.Silu, paired=True, add_norm=True)

        def layer3_self():
            normalise(core, core.x)
            with_heads(2, lambda h: self_attention(core, h, "L3_attn_wq", "L3_attn_wk", "L3_attn_wv", rope=True,
                                                   causal=True), "L3_attn_W_out")

        def layer3_ffn():
            normalise(core, core.x)
            choose_experts(core, "L3_ffn_Wg", bias="L3_ffn_bg", first=1)
            feed_forward(core, "L3_ffn_W1", "L3_ffn_W2", 1024, 8, ACT.Silu, up_bias="L3_ffn_b1", down_bias="L3_ffn_b2")

        run = [
            layer0_cross, layer0_self, layer0_ffn,
            lambda: cross("L1_xattn_", mask="mask1", mask_cols="mask1_cols", mask_values=True), layer1_self, layer1_ffn,
            lambda: cross("L2_xattn_", scale="L2_xattn_scale"), layer2_conv, layer2_ffn,
            lambda: cross("L3_xattn_", mask="mask3", mask_cols="mask3_cols"), layer3_self, layer3_ffn,
        ]
        for n in stages:
            run[n]()
        store_residual(core)


def lay_out(a):
    o = {}
    o["x"] = a["x"].reshape(T, D)
    o["ctx"] = a["ctx_1024"]
    o["ctx_t"] = a["ctx_1024"].transpose(0, 2, 1)
    for n, name in (("1", "mask_Bx1xS2_ik0"), ("3", "mask_Bx1x1xS2_ik0")):
        m = a[name].reshape(B, KEYS)
        o["mask" + n] = m
        o[f"mask{n}_cols"] = np.pad(m, ((0, 0), (0, KT * P - KEYS))).reshape(B, KT, P).transpose(0, 2, 1)

    def pair_rows(w):
        return w.reshape(UNITS, 2, DH, D).transpose(1, 0, 2, 3).reshape(D, D)

    for k in ("ln_g", "ln_b", "cln_g", "cln_b", "Wq"):
        o["L0_xattn_" + k] = a["L0_xattn_" + k]
    o["L0_xattn_Wk"], o["L0_xattn_Wv"] = a["L0_xattn_Wkv"][:, :64], a["L0_xattn_Wkv"][:, 64:]
    o["L0_xattn_Wo"] = a["L0_xattn_Wo"].reshape(4, 2, 2, 64, D).transpose(0, 2, 1, 3, 4).reshape(1024, D)
    o["L0_xattn_Wff1"], o["L0_xattn_Wff2"] = a["L0_xattn_Wff1"][None], a["L0_xattn_Wff2"][None]
    w = a["L0_attn_w_qkv"]
    o["L0_attn_wq"], o["L0_attn_wk"], o["L0_attn_wv"] = w[:, :D], w[:, D:2 * D], w[:, 2 * D:]
    o["L0_attn_w_out"] = pair_rows(a["L0_attn_w_out"])
    o["L0_ffn_weight"], o["L0_ffn_bias"] = a["L0_ffn_weight"].T, a["L0_ffn_bias"]
    for p, out in (("L1_xattn_", "o"), ("L2_xattn_", "p"), ("L3_xattn_", "o")):
        for k in ("Wq", "Wk", "Wv"):
            o[p + k] = a[p + k].T
        for k in ("bq", "bk", "bv"):
            o[p + k] = a[p + k]
        o[p + "Wo"], o[p + "bo"] = pair_rows(a[p + "W" + out].T), a[p + "b" + out]
    o["L2_xattn_scale"] = a["L2_xattn_scale"]
    o["L1_attn_wq"] = np.zeros((D, D), a["L1_attn_w_att_val"].dtype)
    for h in range(H):
        o["L1_attn_wq"][h * DH:(h + 1) * DH, h * DH:(h + 1) * DH] = a["L1_attn_w_att_val"][h]
    o["L1_attn_wv"], o["L1_attn_wv_b"] = a["L1_attn_wv_w"].T, a["L1_attn_wv_b"]
    o["L1_attn_out_w"], o["L1_attn_out_b"] = pair_rows(a["L1_attn_out_w"].T), a["L1_attn_out_b"]
    o["L1_ffn_up"] = np.concatenate([a["L1_ffn_shared_up"], a["L1_ffn_routed_up"]])
    o["L1_ffn_down"] = np.concatenate([a["L1_ffn_shared_down"], a["L1_ffn_routed_down"]])
    o["L1_ffn_router_w"] = a["L1_ffn_router_w"]
    for k in ("W_in", "b_in", "short_w", "short_b", "inner_w", "inner_b", "W_out", "b_out"):
        o["L2_attn_" + k] = a["L2_attn_" + k]
    o["L2_ffn_norm_scale"] = a["L2_ffn_norm_scale"]
    o["L2_ffn_w_router"] = a["L2_ffn_w_router"].T
    o["L2_ffn_w_up"], o["L2_ffn_w_down"] = a["L2_ffn_w_up"].transpose(0, 2, 1), a["L2_ffn_w_down"].transpose(0, 2, 1)
    w = a["L3_attn_W_qkv"].T
    swap = np.arange(D) ^ 1
    o["L3_attn_wq"] = np.concatenate([w[:, :D], w[:, :D][:, swap]], axis=1)
    o["L3_attn_wk"] = np.concatenate([w[:, D:2 * D], w[:, D:2 * D][:, swap]], axis=1)
    o["L3_attn_wv"], o["L3_attn_W_out"] = w[:, 2 * D:], pair_rows(a["L3_attn_W_out"].T)
    for k in ("Wg", "bg", "W1", "W2", "b2"):
        o["L3_ffn_" + k] = a["L3_ffn_" + k]
    o["L3_ffn_b1"] = a["L3_ffn_b1"].reshape(8, 8, P).transpose(0, 2, 1)
    o["c_ident"] = np.eye(P, dtype=np.float32)
    o["c_ident_down"] = np.eye(P, dtype=np.float32) / np.float32(SHIFT)
    o["c_head_of_pair"] = (np.arange(P)[:, None] // DH % 2 == np.arange(2)[None, :]).astype(np.float32)
    o["c_lower"] = np.broadcast_to(np.tril(np.ones((8, 8), np.float32), -1), (P, 8, 8))
    o["c_later"] = np.where(np.arange(S)[None, :] > np.arange(P)[:, None] % S, np.float32(-1e30), np.float32(0))
    freqs = 1.0 / 10000.0 ** (np.arange(0, DH, 2) / DH)
    angle = np.arange(S)[None, :] * freqs[np.arange(P) % DH // 2][:, None]
    sign = np.where(np.arange(P) % 2 == 0, -1.0, 1.0)[:, None]
    o["c_wave"] = np.stack([np.cos(angle), np.sin(angle) * sign], axis=1).astype(np.float32)
    return {k: np.ascontiguousarray(v) for k, v in o.items()}


def kernel(**inputs):
    import concourse.bacc as bacc
    from concourse.bass_utils import run_bass_kernel_spmd

    arrays = lay_out({k: np.asarray(v) for k, v in inputs.items()})
    nc = bacc.Bacc("TRN2", target_bir_lowering=False, num_devices=1)
    dram = {k: nc.dram_tensor(f"in_{k}", v.shape, mybir.dt.from_np(v.dtype), kind="ExternalInput").ap()
            for k, v in arrays.items()}
    dram["out"] = nc.dram_tensor("out_x", (T, D), F32, kind="ExternalOutput").ap()
    build(nc, dram)
    r = run_bass_kernel_spmd(nc, [{f"in_{k}": v for k, v in arrays.items()}], core_ids=[0])
    return r.results[0]["out_x"].reshape(B, S, D)
```
